# Optimizing a Trainium2 kernel written in Bass

```python
import numpy as np
import jax
import jax.numpy as jnp

def _softmax(x, axis=-1):
    return jax.nn.softmax(x, axis=axis)

def _gelu(x):
    return jax.nn.gelu(x, approximate=True)

def _silu(x):
    return jax.nn.silu(x)

def _sigmoid(x):
    return jax.nn.sigmoid(x)

def _layernorm(x, axis=-1, eps=1e-05):
    m = jnp.mean(x, axis=axis, keepdims=True)
    v = jnp.var(x, axis=axis, keepdims=True)
    return (x - m) / jnp.sqrt(v + eps)

def _scatter_add(tgt, idx, src, axis=0):
    return tgt.at[idx].add(src)

def _segment_sum(src, seg, n):
    return jax.ops.segment_sum(src, seg, n)
kernel_name = 'mk_xattn_seq_d4_seqx_r8_547932'

def setup_inputs(seed: int=0):
    np.random.seed(seed)
    _w = jnp.asarray

    def _rec_inputs():
        import jax
        import jax.numpy as jnp
        _rk = jax.random.key(seed)
        x = -0.0002928 + 1 * jax.random.normal(jax.random.fold_in(_rk, 1), (8, 128, 256), jnp.float32)
        _lenS = 128 - jax.random.randint(jax.random.fold_in(_rk, 7), (8,), 0, max(1, 128 // 4) + 1, jnp.int32)
        _lenS2 = 128 - jax.random.randint(jax.random.fold_in(_rk, 8), (8,), 0, max(1, 128 // 4) + 1, jnp.int32)
        _ctx_2048P = jax.random.normal(jax.random.fold_in(_rk, 12), (8, 16, 256), jnp.float32)
        _ctx_2048c = jax.random.dirichlet(jax.random.fold_in(_rk, 512), 0.3 * jnp.ones((16,), jnp.float32), (8, 128))
        _ctx_2048t = jnp.einsum('bsk,bkd->bsd', _ctx_2048c, _ctx_2048P)
        _ctx_2048t = _ctx_2048t * jax.lax.rsqrt(jnp.mean(jnp.square(_ctx_2048t)) + 1e-12) * 0.953939
        ctx_2048 = -1.39393e-06 + 0.999914 * (_ctx_2048t + 0.3 * jax.random.normal(jax.random.fold_in(_rk, 612), (8, 128, 256), jnp.float32))
        _validS = jnp.arange(128)[None, :] < _lenS[:, None]
        _validS2 = jnp.arange(128)[None, :] < _lenS2[:, None]
        _causal = jnp.tril(jnp.ones((128, 128), dtype=bool))
        mask_Bx1x2048_bf1 = jnp.ones((8, 1, 256), dtype=bool)
        mask_BxS2_ik0 = jnp.where(jnp.broadcast_to(_validS2[:, :], (8, 128)), 0, 1).astype(jnp.int32)
        mask_BxS2_bf1 = jnp.ones((8, 128), dtype=bool)
        return (x, ctx_2048, mask_Bx1x2048_bf1, mask_BxS2_ik0, mask_BxS2_bf1)
    x, ctx_2048, mask_Bx1x2048_bf1, mask_BxS2_ik0, mask_BxS2_bf1 = _rec_inputs()

    def _L0_xattn_setup():
        import jax, jax.numpy as jnp
        import numpy as np
        import math
        N_HEADS = 16
        EPS = 1e-05

        def _masked_instance_norm(x, mask):
            m = mask.astype(x.dtype)
            x = x * m
            n_valid = jnp.sum(m, axis=-1, keepdims=True)
            mean = jnp.sum(x, axis=-1, keepdims=True) / n_valid
            var = jnp.sum(x * x, axis=-1, keepdims=True) / n_valid - mean * mean
            x = (x - mean) / jnp.sqrt(jax.nn.relu(var) + EPS)
            return x * m
        key = jax.random.key(seed)
        ks = jax.random.split(key, 8)
        bs, c, t1, t2 = (2, 128, 256, 256)
        s = 1.0 / math.sqrt(c)
        return {'x': jax.random.normal(ks[0], (bs, c, t1), jnp.float32), 'mask': jnp.ones((bs, 1, t1), jnp.bool_), 'kv': jax.random.normal(ks[1], (bs, c, t2), jnp.float32), 'kv_mask': jnp.ones((bs, 1, t2), jnp.bool_), 'Wq': jax.random.normal(ks[2], (c, c), jnp.float32) * s, 'bq': jnp.zeros((c,), jnp.float32), 'Wk': jax.random.normal(ks[3], (c, c), jnp.float32) * s, 'bk': jnp.zeros((c,), jnp.float32), 'Wv': jax.random.normal(ks[4], (c, c), jnp.float32) * s, 'bv': jnp.zeros((c,), jnp.float32)}
    _L0_xattn_all = _L0_xattn_setup()
    _L0_xattn_in = {k: v for k, v in _L0_xattn_all.items() if k in ('Wq', 'bq', 'Wk', 'bk', 'Wv', 'bv')}
    del _L0_xattn_all

    def _L1_xattn_setup():
        import jax, jax.numpy as jnp
        import numpy as np
        B, P, K, H, NH = (4, 256, 32, 256, 16)
        DH = H // NH
        EPS = 1e-06

        def rmsnorm(x, w):
            var = jnp.mean(jnp.square(x), axis=-1, keepdims=True)
            return x * jax.lax.rsqrt(var + EPS) * w
        key = jax.random.key(seed)
        ks = jax.random.split(key, 12)
        s = 0.02
        return {'x': jax.random.normal(ks[0], (B, P, H), jnp.float32), 'latents': jax.random.normal(ks[1], (B, K, H), jnp.float32), 'attention_mask': jax.random.randint(ks[2], (B, P), 0, 2, jnp.int32), 'q_w': s * jax.random.normal(ks[3], (H, H), jnp.float32), 'q_b': jnp.zeros((H,), jnp.float32), 'kv_w': s * jax.random.normal(ks[4], (H, 2 * H), jnp.float32), 'kv_b': jnp.zeros((2 * H,), jnp.float32), 'out_w': s * jax.random.normal(ks[5], (H, H), jnp.float32), 'out_b': jnp.zeros((H,), jnp.float32), 'postnorm_w': jnp.ones((H,), jnp.float32), 'mlp_w1': s * jax.random.normal(ks[6], (H, 4 * H), jnp.float32), 'mlp_b1': jnp.zeros((4 * H,), jnp.float32), 'mlp_w2': s * jax.random.normal(ks[7], (4 * H, H), jnp.float32), 'mlp_b2': jnp.zeros((H,), jnp.float32)}
    _L1_xattn_all = _L1_xattn_setup()
    _L1_xattn_in = {k: v for k, v in _L1_xattn_all.items() if k in ('q_w', 'q_b', 'kv_w', 'kv_b', 'out_w', 'out_b', 'postnorm_w', 'mlp_w1', 'mlp_b1', 'mlp_w2', 'mlp_b2')}
    del _L1_xattn_all

    def _L2_xattn_setup():
        import jax, jax.numpy as jnp
        import numpy as np
        B, Q, S1, S2 = (4, 32, 256, 256)
        D, H, K, F = (256, 16, 128, 1024)
        LN_EPS = 1e-05

        def _layer_norm(x, scale, offset):
            mu = jnp.mean(x, axis=-1, keepdims=True)
            var = jnp.var(x, axis=-1, keepdims=True)
            return (x - mu) * jax.lax.rsqrt(var + LN_EPS) * scale + offset

        def _cross_attention(q_in, kv_in, wq, bq, wk, bk, wv, bv, wo, bo, bias_k, bias_v):
            b, q_len, _ = q_in.shape
            t = kv_in.shape[1]
            qh = (q_in @ wq + bq).reshape(b, q_len, H, K)
            kh = (kv_in @ wk + bk).reshape(b, t, H, K)
            vh = (kv_in @ wv + bv).reshape(b, t, H, K)
            kh = jnp.concatenate([kh, jnp.broadcast_to(bias_k, (b, 1, H, K))], axis=1)
            vh = jnp.concatenate([vh, jnp.broadcast_to(bias_v, (b, 1, H, K))], axis=1)
            scale = jnp.sqrt(jnp.asarray(K, q_in.dtype))
            logits = jnp.einsum('bqhk,bthk->bhqt', qh, kh) / scale
            weights = jax.nn.softmax(logits, axis=-1)
            ctx = jnp.einsum('bhqt,bthk->bqhk', weights, vh).reshape(b, q_len, H * K)
            return ctx @ wo + bo

        def _forward(x, xf_1, xf_2, ln1_scale, ln1_offset, wq1, bq1, wk1, bk1, wv1, bv1, wo1, bo1, bias_k1, bias_v1, ln2_scale, ln2_offset, wq2, bq2, wk2, bk2, wv2, bv2, wo2, bo2, bias_k2, bias_v2, ln_mlp_scale, ln_mlp_offset, w_fc1, b_fc1, w_fc2, b_fc2):
            res = x
            h = _layer_norm(x, ln1_scale, ln1_offset)
            x = res + _cross_attention(h, xf_1, wq1, bq1, wk1, bk1, wv1, bv1, wo1, bo1, bias_k1, bias_v1)
            res = x
            h = _layer_norm(x, ln2_scale, ln2_offset)
            x = res + _cross_attention(h, xf_2, wq2, bq2, wk2, bk2, wv2, bv2, wo2, bo2, bias_k2, bias_v2)
            h = _layer_norm(x, ln_mlp_scale, ln_mlp_offset)
            h = jax.nn.gelu(h @ w_fc1 + b_fc1, approximate=False) @ w_fc2 + b_fc2
            return x + h
        key = jax.random.key(seed)
        ks = iter(jax.random.split(key, 64))

        def rn(shape, s=0.02):
            return jax.random.normal(next(ks), shape, jnp.float32) * s
        inp = {'x': rn((B, Q, D), 1.0), 'xf_1': rn((B, S1, D), 1.0), 'xf_2': rn((B, S2, D), 1.0)}
        for i in (1, 2):
            inp[f'ln{i}_scale'] = jnp.ones((D,), jnp.float32)
            inp[f'ln{i}_offset'] = jnp.zeros((D,), jnp.float32)
            inp[f'wq{i}'] = rn((D, H * K))
            inp[f'bq{i}'] = jnp.zeros((H * K,), jnp.float32)
            inp[f'wk{i}'] = rn((D, H * K))
            inp[f'bk{i}'] = jnp.zeros((H * K,), jnp.float32)
            inp[f'wv{i}'] = rn((D, H * K))
            inp[f'bv{i}'] = jnp.zeros((H * K,), jnp.float32)
            inp[f'wo{i}'] = rn((H * K, D))
            inp[f'bo{i}'] = jnp.zeros((D,), jnp.float32)
            inp[f'bias_k{i}'] = rn((1, 1, H, K))
            inp[f'bias_v{i}'] = rn((1, 1, H, K))
        inp['ln_mlp_scale'] = jnp.ones((D,), jnp.float32)
        inp['ln_mlp_offset'] = jnp.zeros((D,), jnp.float32)
        inp['w_fc1'] = rn((D, F))
        inp['b_fc1'] = jnp.zeros((F,), jnp.float32)
        inp['w_fc2'] = rn((F, D))
        inp['b_fc2'] = jnp.zeros((D,), jnp.float32)
        return inp
    _L2_xattn_all = _L2_xattn_setup()
    _L2_xattn_in = {k: v for k, v in _L2_xattn_all.items() if k in ('ln1_scale', 'ln1_offset', 'wq1', 'bq1', 'wk1', 'bk1', 'wv1', 'bv1', 'wo1', 'bo1', 'bias_k1', 'bias_v1', 'ln2_scale', 'ln2_offset', 'wq2', 'bq2', 'wk2', 'bk2', 'wv2', 'bv2', 'wo2', 'bo2', 'bias_k2', 'bias_v2', 'ln_mlp_scale', 'ln_mlp_offset', 'w_fc1', 'b_fc1', 'w_fc2', 'b_fc2')}
    del _L2_xattn_all

    def _L3_xattn_setup():
        import jax, jax.numpy as jnp
        import numpy as np
        D = 256
        H = 16
        HD = D // H
        INNER = 4 * D
        EPS = 1e-05

        def layer_norm(x, w, b):
            mu = jnp.mean(x, axis=-1, keepdims=True)
            var = jnp.mean(jnp.square(x - mu), axis=-1, keepdims=True)
            return (x - mu) * jax.lax.rsqrt(var + EPS) * w + b
        key = jax.random.key(seed)
        ks = jax.random.split(key, 12)
        B, LQ, LK = (4, 128, 256)
        std = 0.02
        inp = {'hidden_states': jax.random.normal(ks[0], (B, LQ, D), jnp.float32), 'encoder_hidden_states': jax.random.normal(ks[1], (B, LK, D), jnp.float32), 'encoder_attention_mask': jnp.ones((B, LK), dtype=bool), 'ln1_w': jnp.ones((D,), jnp.float32), 'ln1_b': jnp.zeros((D,), jnp.float32), 'q_w': jax.random.normal(ks[2], (D, D), jnp.float32) * std, 'q_b': jnp.zeros((D,), jnp.float32), 'k_w': jax.random.normal(ks[3], (D, D), jnp.float32) * std, 'k_b': jnp.zeros((D,), jnp.float32), 'v_w': jax.random.normal(ks[4], (D, D), jnp.float32) * std, 'v_b': jnp.zeros((D,), jnp.float32), 'cproj_w': jax.random.normal(ks[5], (D, D), jnp.float32) * std, 'cproj_b': jnp.zeros((D,), jnp.float32), 'ln2_w': jnp.ones((D,), jnp.float32), 'ln2_b': jnp.zeros((D,), jnp.float32), 'fc_w': jax.random.normal(ks[6], (D, INNER), jnp.float32) * std, 'fc_b': jnp.zeros((INNER,), jnp.float32), 'proj_w': jax.random.normal(ks[7], (INNER, D), jnp.float32) * std, 'proj_b': jnp.zeros((D,), jnp.float32)}
        return inp
    _L3_xattn_all = _L3_xattn_setup()
    _L3_xattn_in = {k: v for k, v in _L3_xattn_all.items() if k in ('ln1_w', 'ln1_b', 'q_w', 'q_b', 'k_w', 'k_b', 'v_w', 'v_b', 'cproj_w', 'cproj_b', 'ln2_w', 'ln2_b', 'fc_w', 'fc_b', 'proj_w', 'proj_b')}
    del _L3_xattn_all
    return {'x': x, 'ctx_2048': ctx_2048, 'mask_Bx1x2048_bf1': mask_Bx1x2048_bf1, 'mask_BxS2_ik0': mask_BxS2_ik0, 'mask_BxS2_bf1': mask_BxS2_bf1, 'L0_xattn_Wq': _L0_xattn_in['Wq'], 'L0_xattn_bq': _L0_xattn_in['bq'], 'L0_xattn_Wk': _L0_xattn_in['Wk'], 'L0_xattn_bk': _L0_xattn_in['bk'], 'L0_xattn_Wv': _L0_xattn_in['Wv'], 'L0_xattn_bv': _L0_xattn_in['bv'], 'L1_xattn_q_w': _L1_xattn_in['q_w'], 'L1_xattn_q_b': _L1_xattn_in['q_b'], 'L1_xattn_kv_w': _L1_xattn_in['kv_w'], 'L1_xattn_kv_b': _L1_xattn_in['kv_b'], 'L1_xattn_out_w': _L1_xattn_in['out_w'], 'L1_xattn_out_b': _L1_xattn_in['out_b'], 'L1_xattn_postnorm_w': _L1_xattn_in['postnorm_w'], 'L1_xattn_mlp_w1': _L1_xattn_in['mlp_w1'], 'L1_xattn_mlp_b1': _L1_xattn_in['mlp_b1'], 'L1_xattn_mlp_w2': _L1_xattn_in['mlp_w2'], 'L1_xattn_mlp_b2': _L1_xattn_in['mlp_b2'], 'L2_xattn_ln1_scale': _L2_xattn_in['ln1_scale'], 'L2_xattn_ln1_offset': _L2_xattn_in['ln1_offset'], 'L2_xattn_wq1': _L2_xattn_in['wq1'], 'L2_xattn_bq1': _L2_xattn_in['bq1'], 'L2_xattn_wk1': _L2_xattn_in['wk1'], 'L2_xattn_bk1': _L2_xattn_in['bk1'], 'L2_xattn_wv1': _L2_xattn_in['wv1'], 'L2_xattn_bv1': _L2_xattn_in['bv1'], 'L2_xattn_wo1': _L2_xattn_in['wo1'], 'L2_xattn_bo1': _L2_xattn_in['bo1'], 'L2_xattn_bias_k1': _L2_xattn_in['bias_k1'], 'L2_xattn_bias_v1': _L2_xattn_in['bias_v1'], 'L2_xattn_ln2_scale': _L2_xattn_in['ln2_scale'], 'L2_xattn_ln2_offset': _L2_xattn_in['ln2_offset'], 'L2_xattn_wq2': _L2_xattn_in['wq2'], 'L2_xattn_bq2': _L2_xattn_in['bq2'], 'L2_xattn_wk2': _L2_xattn_in['wk2'], 'L2_xattn_bk2': _L2_xattn_in['bk2'], 'L2_xattn_wv2': _L2_xattn_in['wv2'], 'L2_xattn_bv2': _L2_xattn_in['bv2'], 'L2_xattn_wo2': _L2_xattn_in['wo2'], 'L2_xattn_bo2': _L2_xattn_in['bo2'], 'L2_xattn_bias_k2': _L2_xattn_in['bias_k2'], 'L2_xattn_bias_v2': _L2_xattn_in['bias_v2'], 'L2_xattn_ln_mlp_scale': _L2_xattn_in['ln_mlp_scale'], 'L2_xattn_ln_mlp_offset': _L2_xattn_in['ln_mlp_offset'], 'L2_xattn_w_fc1': _L2_xattn_in['w_fc1'], 'L2_xattn_b_fc1': _L2_xattn_in['b_fc1'], 'L2_xattn_w_fc2': _L2_xattn_in['w_fc2'], 'L2_xattn_b_fc2': _L2_xattn_in['b_fc2'], 'L3_xattn_ln1_w': _L3_xattn_in['ln1_w'], 'L3_xattn_ln1_b': _L3_xattn_in['ln1_b'], 'L3_xattn_q_w': _L3_xattn_in['q_w'], 'L3_xattn_q_b': _L3_xattn_in['q_b'], 'L3_xattn_k_w': _L3_xattn_in['k_w'], 'L3_xattn_k_b': _L3_xattn_in['k_b'], 'L3_xattn_v_w': _L3_xattn_in['v_w'], 'L3_xattn_v_b': _L3_xattn_in['v_b'], 'L3_xattn_cproj_w': _L3_xattn_in['cproj_w'], 'L3_xattn_cproj_b': _L3_xattn_in['cproj_b'], 'L3_xattn_ln2_w': _L3_xattn_in['ln2_w'], 'L3_xattn_ln2_b': _L3_xattn_in['ln2_b'], 'L3_xattn_fc_w': _L3_xattn_in['fc_w'], 'L3_xattn_fc_b': _L3_xattn_in['fc_b'], 'L3_xattn_proj_w': _L3_xattn_in['proj_w'], 'L3_xattn_proj_b': _L3_xattn_in['proj_b']}

def reference(x, ctx_2048, mask_Bx1x2048_bf1, mask_BxS2_ik0, mask_BxS2_bf1, L0_xattn_Wq, L0_xattn_bq, L0_xattn_Wk, L0_xattn_bk, L0_xattn_Wv, L0_xattn_bv, L1_xattn_q_w, L1_xattn_q_b, L1_xattn_kv_w, L1_xattn_kv_b, L1_xattn_out_w, L1_xattn_out_b, L1_xattn_postnorm_w, L1_xattn_mlp_w1, L1_xattn_mlp_b1, L1_xattn_mlp_w2, L1_xattn_mlp_b2, L2_xattn_ln1_scale, L2_xattn_ln1_offset, L2_xattn_wq1, L2_xattn_bq1, L2_xattn_wk1, L2_xattn_bk1, L2_xattn_wv1, L2_xattn_bv1, L2_xattn_wo1, L2_xattn_bo1, L2_xattn_bias_k1, L2_xattn_bias_v1, L2_xattn_ln2_scale, L2_xattn_ln2_offset, L2_xattn_wq2, L2_xattn_bq2, L2_xattn_wk2, L2_xattn_bk2, L2_xattn_wv2, L2_xattn_bv2, L2_xattn_wo2, L2_xattn_bo2, L2_xattn_bias_k2, L2_xattn_bias_v2, L2_xattn_ln_mlp_scale, L2_xattn_ln_mlp_offset, L2_xattn_w_fc1, L2_xattn_b_fc1, L2_xattn_w_fc2, L2_xattn_b_fc2, L3_xattn_ln1_w, L3_xattn_ln1_b, L3_xattn_q_w, L3_xattn_q_b, L3_xattn_k_w, L3_xattn_k_b, L3_xattn_v_w, L3_xattn_v_b, L3_xattn_cproj_w, L3_xattn_cproj_b, L3_xattn_ln2_w, L3_xattn_ln2_b, L3_xattn_fc_w, L3_xattn_fc_b, L3_xattn_proj_w, L3_xattn_proj_b):
    import jax
    import jax.numpy as jnp

    def _L0_xattn_ref(x, mask, kv, kv_mask, Wq, bq, Wk, bk, Wv, bv):
        import jax, jax.numpy as jnp
        import numpy as np
        import math
        N_HEADS = 16
        EPS = 1e-05

        def _masked_instance_norm(x, mask):
            m = mask.astype(x.dtype)
            x = x * m
            n_valid = jnp.sum(m, axis=-1, keepdims=True)
            mean = jnp.sum(x, axis=-1, keepdims=True) / n_valid
            var = jnp.sum(x * x, axis=-1, keepdims=True) / n_valid - mean * mean
            x = (x - mean) / jnp.sqrt(jax.nn.relu(var) + EPS)
            return x * m
        bs, c, t1 = x.shape
        h = N_HEADS
        d = c // h
        scale = 1.0 / math.sqrt(d)
        q = jnp.einsum('oc,bct->bot', Wq, x) + bq[None, :, None]
        k = jnp.einsum('oc,bct->bot', Wk, kv) + bk[None, :, None]
        v = jnp.einsum('oc,bct->bot', Wv, kv) + bv[None, :, None]
        q = q.reshape(bs, h, d, t1).transpose(0, 1, 3, 2)
        k = k.reshape(bs, h, d, -1)
        v = v.reshape(bs, h, d, -1).transpose(0, 1, 3, 2)
        attn = jnp.einsum('bhqd,bhdk->bhqk', q * scale, k)
        attn = jnp.where(kv_mask[:, :, None, :], attn, -jnp.inf)
        attn = jax.nn.softmax(attn, axis=-1)
        mean = jnp.einsum('bhqk,bhkd->bhqd', attn, v)
        ex2 = jnp.einsum('bhqk,bhkd->bhqd', attn, v * v)
        std = jnp.sqrt(jax.nn.relu(ex2 - mean * mean))
        mean = mean.transpose(0, 1, 3, 2).reshape(bs, c, t1)
        std = std.transpose(0, 1, 3, 2).reshape(bs, c, t1)
        xn = _masked_instance_norm(x, mask)
        out = (xn * std + mean) * mask.astype(x.dtype)
        return out

    def _L1_xattn_ref(x, latents, attention_mask, q_w, q_b, kv_w, kv_b, out_w, out_b, postnorm_w, mlp_w1, mlp_b1, mlp_w2, mlp_b2):
        import jax, jax.numpy as jnp
        import numpy as np
        B, P, K, H, NH = (4, 256, 32, 256, 16)
        DH = H // NH
        EPS = 1e-06

        def rmsnorm(x, w):
            var = jnp.mean(jnp.square(x), axis=-1, keepdims=True)
            return x * jax.lax.rsqrt(var + EPS) * w
        b, p, _ = x.shape
        k_len = latents.shape[1]
        residual = latents
        h = jnp.concatenate([x, latents], axis=1)
        q = (latents @ q_w + q_b).reshape(b, k_len, NH, DH)
        kv = (h @ kv_w + kv_b).reshape(b, p + k_len, NH, DH, 2)
        kmat, v = (kv[..., 0], kv[..., 1])
        attn = jnp.einsum('bkhd,bnhd->bhkn', q, kmat) / DH
        full_mask = jnp.concatenate([attention_mask.astype(bool), jnp.ones((b, k_len), bool)], axis=-1)
        attn = jnp.where(full_mask[:, None, None, :], attn, -jnp.inf)
        attn = jax.nn.softmax(attn.astype(jnp.float32), axis=-1).astype(q.dtype)
        attn_out = jnp.einsum('bhkn,bnhd->bkhd', attn, v).reshape(b, k_len, H)
        attn_out = attn_out @ out_w + out_b + residual
        out = rmsnorm(attn_out, postnorm_w)
        out = jax.nn.gelu(out @ mlp_w1 + mlp_b1) @ mlp_w2 + mlp_b2
        return out + residual

    def _L2_xattn_ref(x, xf_1, xf_2, ln1_scale, ln1_offset, wq1, bq1, wk1, bk1, wv1, bv1, wo1, bo1, bias_k1, bias_v1, ln2_scale, ln2_offset, wq2, bq2, wk2, bk2, wv2, bv2, wo2, bo2, bias_k2, bias_v2, ln_mlp_scale, ln_mlp_offset, w_fc1, b_fc1, w_fc2, b_fc2):
        import jax, jax.numpy as jnp
        import numpy as np
        B, Q, S1, S2 = (4, 32, 256, 256)
        D, H, K, F = (256, 16, 128, 1024)
        LN_EPS = 1e-05

        def _layer_norm(x, scale, offset):
            mu = jnp.mean(x, axis=-1, keepdims=True)
            var = jnp.var(x, axis=-1, keepdims=True)
            return (x - mu) * jax.lax.rsqrt(var + LN_EPS) * scale + offset

        def _cross_attention(q_in, kv_in, wq, bq, wk, bk, wv, bv, wo, bo, bias_k, bias_v):
            b, q_len, _ = q_in.shape
            t = kv_in.shape[1]
            qh = (q_in @ wq + bq).reshape(b, q_len, H, K)
            kh = (kv_in @ wk + bk).reshape(b, t, H, K)
            vh = (kv_in @ wv + bv).reshape(b, t, H, K)
            kh = jnp.concatenate([kh, jnp.broadcast_to(bias_k, (b, 1, H, K))], axis=1)
            vh = jnp.concatenate([vh, jnp.broadcast_to(bias_v, (b, 1, H, K))], axis=1)
            scale = jnp.sqrt(jnp.asarray(K, q_in.dtype))
            logits = jnp.einsum('bqhk,bthk->bhqt', qh, kh) / scale
            weights = jax.nn.softmax(logits, axis=-1)
            ctx = jnp.einsum('bhqt,bthk->bqhk', weights, vh).reshape(b, q_len, H * K)
            return ctx @ wo + bo

        def _forward(x, xf_1, xf_2, ln1_scale, ln1_offset, wq1, bq1, wk1, bk1, wv1, bv1, wo1, bo1, bias_k1, bias_v1, ln2_scale, ln2_offset, wq2, bq2, wk2, bk2, wv2, bv2, wo2, bo2, bias_k2, bias_v2, ln_mlp_scale, ln_mlp_offset, w_fc1, b_fc1, w_fc2, b_fc2):
            res = x
            h = _layer_norm(x, ln1_scale, ln1_offset)
            x = res + _cross_attention(h, xf_1, wq1, bq1, wk1, bk1, wv1, bv1, wo1, bo1, bias_k1, bias_v1)
            res = x
            h = _layer_norm(x, ln2_scale, ln2_offset)
            x = res + _cross_attention(h, xf_2, wq2, bq2, wk2, bk2, wv2, bv2, wo2, bo2, bias_k2, bias_v2)
            h = _layer_norm(x, ln_mlp_scale, ln_mlp_offset)
            h = jax.nn.gelu(h @ w_fc1 + b_fc1, approximate=False) @ w_fc2 + b_fc2
            return x + h
        return _forward(x, xf_1, xf_2, ln1_scale, ln1_offset, wq1, bq1, wk1, bk1, wv1, bv1, wo1, bo1, bias_k1, bias_v1, ln2_scale, ln2_offset, wq2, bq2, wk2, bk2, wv2, bv2, wo2, bo2, bias_k2, bias_v2, ln_mlp_scale, ln_mlp_offset, w_fc1, b_fc1, w_fc2, b_fc2)

    def _L3_xattn_ref(hidden_states, encoder_hidden_states, encoder_attention_mask, ln1_w, ln1_b, q_w, q_b, k_w, k_b, v_w, v_b, cproj_w, cproj_b, ln2_w, ln2_b, fc_w, fc_b, proj_w, proj_b):
        import jax, jax.numpy as jnp
        import numpy as np
        D = 256
        H = 16
        HD = D // H
        INNER = 4 * D
        EPS = 1e-05

        def layer_norm(x, w, b):
            mu = jnp.mean(x, axis=-1, keepdims=True)
            var = jnp.mean(jnp.square(x - mu), axis=-1, keepdims=True)
            return (x - mu) * jax.lax.rsqrt(var + EPS) * w + b
        B, LQ, _ = hidden_states.shape
        LK = encoder_hidden_states.shape[1]
        residual = hidden_states
        x = layer_norm(hidden_states, ln1_w, ln1_b)
        q = (x @ q_w + q_b).reshape(B, LQ, H, HD).transpose(0, 2, 1, 3)
        k = (encoder_hidden_states @ k_w + k_b).reshape(B, LK, H, HD).transpose(0, 2, 1, 3)
        v = (encoder_hidden_states @ v_w + v_b).reshape(B, LK, H, HD).transpose(0, 2, 1, 3)
        scale = 1.0 / np.sqrt(HD).astype(np.float32)
        scores = jnp.einsum('bhqd,bhkd->bhqk', q, k) * scale
        mask = encoder_attention_mask[:, None, None, :]
        mask_value = jnp.finfo(scores.dtype).min
        scores = jnp.where(mask, scores, mask_value)
        attn = jax.nn.softmax(scores, axis=-1)
        out = jnp.einsum('bhqk,bhkd->bhqd', attn, v)
        out = out.transpose(0, 2, 1, 3).reshape(B, LQ, D)
        out = out @ cproj_w + cproj_b
        hidden = out + residual
        residual = hidden
        y = layer_norm(hidden, ln2_w, ln2_b)
        y = jax.nn.gelu(y @ fc_w + fc_b, approximate=True)
        y = y @ proj_w + proj_b
        return residual + y
    x = _L0_xattn_ref(x, mask_Bx1x2048_bf1, ctx_2048, mask_Bx1x2048_bf1, L0_xattn_Wq, L0_xattn_bq, L0_xattn_Wk, L0_xattn_bk, L0_xattn_Wv, L0_xattn_bv)
    x = _L1_xattn_ref(ctx_2048, x, mask_BxS2_ik0, L1_xattn_q_w, L1_xattn_q_b, L1_xattn_kv_w, L1_xattn_kv_b, L1_xattn_out_w, L1_xattn_out_b, L1_xattn_postnorm_w, L1_xattn_mlp_w1, L1_xattn_mlp_b1, L1_xattn_mlp_w2, L1_xattn_mlp_b2)
    x = _L2_xattn_ref(x, ctx_2048, ctx_2048, L2_xattn_ln1_scale, L2_xattn_ln1_offset, L2_xattn_wq1, L2_xattn_bq1, L2_xattn_wk1, L2_xattn_bk1, L2_xattn_wv1, L2_xattn_bv1, L2_xattn_wo1, L2_xattn_bo1, L2_xattn_bias_k1, L2_xattn_bias_v1, L2_xattn_ln2_scale, L2_xattn_ln2_offset, L2_xattn_wq2, L2_xattn_bq2, L2_xattn_wk2, L2_xattn_bk2, L2_xattn_wv2, L2_xattn_bv2, L2_xattn_wo2, L2_xattn_bo2, L2_xattn_bias_k2, L2_xattn_bias_v2, L2_xattn_ln_mlp_scale, L2_xattn_ln_mlp_offset, L2_xattn_w_fc1, L2_xattn_b_fc1, L2_xattn_w_fc2, L2_xattn_b_fc2)
    x = _L3_xattn_ref(x, ctx_2048, mask_BxS2_bf1, L3_xattn_ln1_w, L3_xattn_ln1_b, L3_xattn_q_w, L3_xattn_q_b, L3_xattn_k_w, L3_xattn_k_b, L3_xattn_v_w, L3_xattn_v_b, L3_xattn_cproj_w, L3_xattn_cproj_b, L3_xattn_ln2_w, L3_xattn_ln2_b, L3_xattn_fc_w, L3_xattn_fc_b, L3_xattn_proj_w, L3_xattn_proj_b)
    return x

_drawn_inputs = setup_inputs


def setup_inputs(seed=0):
    import zlib

    import numpy as np

    out = dict(_drawn_inputs(seed))
    spreads = {'L0_xattn_bq': (0.0, 0.283),
     'L0_xattn_bk': (0.0, 2.0),
     'L0_xattn_bv': (0.0, 0.1),
     'L1_xattn_q_b': (0.0, 0.8),
     'L1_xattn_kv_b': (0.0, 0.8),
     'L1_xattn_out_b': (0.0, 0.8),
     'L1_xattn_postnorm_w': (1.0, 0.6),
     'L1_xattn_mlp_b1': (0.0, 0.1),
     'L1_xattn_mlp_b2': (0.0, 0.1),
     'L2_xattn_ln1_scale': (1.0, 0.6),
     'L2_xattn_ln1_offset': (0.0, 0.8),
     'L2_xattn_bq1': (0.0, 0.8),
     'L2_xattn_bk1': (0.0, 2.0),
     'L2_xattn_bv1': (0.0, 0.1),
     'L2_xattn_bo1': (0.0, 0.1),
     'L2_xattn_ln2_scale': (1.0, 0.6),
     'L2_xattn_ln2_offset': (0.0, 0.8),
     'L2_xattn_bq2': (0.0, 0.8),
     'L2_xattn_bk2': (0.0, 2.0),
     'L2_xattn_bv2': (0.0, 0.1),
     'L2_xattn_bo2': (0.0, 0.1),
     'L2_xattn_ln_mlp_scale': (1.0, 0.6),
     'L2_xattn_ln_mlp_offset': (0.0, 0.8),
     'L2_xattn_b_fc1': (0.0, 0.1),
     'L2_xattn_b_fc2': (0.0, 0.1),
     'L3_xattn_ln1_w': (1.0, 0.6),
     'L3_xattn_ln1_b': (0.0, 0.8),
     'L3_xattn_q_b': (0.0, 0.8),
     'L3_xattn_k_b': (0.0, 2.0),
     'L3_xattn_v_b': (0.0, 0.283),
     'L3_xattn_cproj_b': (0.0, 0.1),
     'L3_xattn_ln2_w': (1.0, 0.6),
     'L3_xattn_ln2_b': (0.0, 0.738),
     'L3_xattn_fc_b': (0.0, 0.271),
     'L3_xattn_proj_b': (0.0, 0.1)}
    factors = {'L1_xattn_q_w': 8.0,
     'L1_xattn_kv_w': 8.0,
     'L1_xattn_out_w': 8.0,
     'L2_xattn_wq1': 8.0,
     'L2_xattn_wk1': 8.0,
     'L2_xattn_bias_k1': 64.0,
     'L2_xattn_bias_v1': 64.0,
     'L2_xattn_wq2': 8.0,
     'L2_xattn_wk2': 8.0,
     'L2_xattn_bias_k2': 64.0,
     'L2_xattn_bias_v2': 64.0,
     'L3_xattn_q_w': 8.0,
     'L3_xattn_k_w': 8.0}
    for name, (base, spread) in spreads.items():
        noise = np.random.default_rng([zlib.crc32(name.encode()), seed]).standard_normal(out[name].shape)
        drawn = base * np.exp(spread * noise) if base else spread * noise
        out[name] = jnp.asarray(drawn.astype(out[name].dtype))
    for name, factor in factors.items():
        out[name] = (out[name] * factor).astype(out[name].dtype)
    return out
```

```python
from contextlib import ExitStack

import numpy as np

import concourse.bass as bass
from concourse import mybir

F32 = mybir.dt.float32
F32R = mybir.dt.float32r
U8 = mybir.dt.uint8
I32 = mybir.dt.int32
ACT = mybir.ActivationFunctionType
ALU = mybir.AluOpType
AX = mybir.AxisListType

P = 128
B = 8
D = 256
KT = D // P
H = 16
DK2 = 128
PAIRS = H // 2
FF = 4 * D
FT = FF // P
PACK = 1024
MASKED = -float(2 ** 100)
Q0_SCALE = 8 ** -0.5
Q2_SCALE = DK2 ** -0.5

PACKS = ["L0w0"]
for _n in (["L0sel", "L1sel", "L1att", "L1w1_", "L1w2_"] + [f"L2a{i}_" for i in range(PAIRS)] + [f"L2b{i}_" for i in range(PAIRS)]
           + ["L2w1_", "L2w2_", "L3sel", "L3att", "L3w1_", "L3w2_"]):
    PACKS += [_n + "0", _n + "1"]
PACK_AT = {n: i for i, n in enumerate(PACKS)}
COPIED = ("L0w", "L0sel", "L1sel", "L3sel")
SPLIT_COUNT = {}
for _n in PACKS:
    if not _n.startswith(COPIED):
        SPLIT_COUNT[_n] = len(SPLIT_COUNT) + 1

COLS = {}
for _n, _w in ([("ones0", 1), ("ones1", 1), ("L0q", 1), ("L0k", 1), ("L1q", 2), ("L1k", 2), ("L1w", 2), ("L1b1", 8)]
               + [(f"L2{s}{l}", w) for l in (1, 2) for s, w in (("q", 16), ("k", 16), ("bk", 16), ("bv", 16), ("lw", 2), ("lb", 2))]
               + [("L2mw", 2), ("L2mb", 2), ("L2b1", 8), ("L3q", 2), ("L3k", 2), ("L3lw", 2), ("L3lb", 2),
                  ("L3mw", 2), ("L3mb", 2), ("L3b1", 8)]):
    COLS[_n] = (sum(w for _, w in COLS.values()), _w)
NCOLS = sum(w for _, w in COLS.values())

ROWS = ["L0v", "L1v", "L1o", "L1b2", "L2bo1", "L2bo2", "L2b2", "L3v", "L3o", "L3b2"]
ROW_SET = 5

ATT = {
    "L0": dict(iters=8, keys=256, units=2, key_tiles=2, stack_a=2, stack_d=1),
    "L1": dict(iters=4, keys=256, units=2, key_tiles=2, stack_a=3, stack_d=2),
    "L3": dict(iters=4, keys=128, units=1, key_tiles=1, stack_a=2, stack_d=1),
}
STEPS = 4
T_LAG = 3
NORMS = ["ctx", "lat", "L1r", "L2n1", "L2n2", "L2nm", "L3n1", "L3nm"]


def att_order(ph):
    c = ATT[ph]
    U = c["units"]
    per_it = STEPS * 2 * U
    total = c["iters"] * per_it
    yield ("dense", 0)
    yield ("prep", 0)
    for u in range(total + T_LAG + 1):
        s, r = divmod(u, 2 * U)
        if u < total and r == 0:
            if s % STEPS == STEPS - 1 and s // STEPS + 1 < c["iters"]:
                yield ("dense", s // STEPS + 1)
            if s + 1 < c["iters"] * STEPS:
                yield ("prep", s + 1)
        if u < total:
            yield ("S", u)
        if 0 <= u - T_LAG < total:
            yield ("T", u - T_LAG)
        w = u - T_LAG - 1
        if w >= 0 and w % U == U - 1:
            yield ("PV", w // U)
            if w % per_it == per_it - 1:
                yield ("OUT", w // per_it)


def wide_order():
    for k in range(8):
        yield ("qk", 0, k // 4, k % 4)
    for k in range(4):
        yield ("v", 0, k)
    yield ("split", 1)
    yield ("split_o", 1)
    for p in range(PAIRS + 1):
        for u in range(8):
            g = 8 * p + u
            if p < PAIRS:
                yield ("S", g)
            if 0 <= g - 1 < 8 * PAIRS:
                yield ("T", g - 1)
                if p == PAIRS or u % 4 == 0:
                    yield ("PV", g - 1)
            if p >= 1 and u < 4:
                yield ("wo", p - 1, u)
                if u == 3 and p + 1 < PAIRS:
                    yield ("split_o", p + 1)
            if p + 1 < PAIRS and u >= 4:
                yield ("v", p + 1, u - 4)
            if 0 <= g - 1 < 8 * PAIRS and not (p == PAIRS or u % 4 == 0):
                yield ("PV", g - 1)
            if p + 1 < PAIRS:
                yield ("qk", p + 1, u // 4, u % 4)
        if p + 2 < PAIRS:
            yield ("split", p + 2)


def mlp_order():
    for c in range(B // 2):
        for f2 in range(FT // 2):
            yield ("up", c, f2)
        yield ("down", c)


def build(nc, x, ctx_in, mask_t, mask_s2, mask_s3, packs, cols, rows, l2rows, inds, ident_in, out):
    stack = ExitStack()
    with stack:
        def sb(name, shape, dt=F32):
            return stack.enter_context(nc.sbuf_tensor(name, shape, dt))

        def sem(name):
            return stack.enter_context(nc.semaphore(name))

        ps = stack.enter_context(nc.psum_tensor("ps", [P, 8, 512], F32))
        S_BANK, T_BANK, O_BANK, J_BANK = 0, 2, 4, 6
        X = sb("X", [P, B, D])
        XH = sb("XH", [P, B, D])
        wraw = sb("wraw", [P, 2, PACK])
        ident = sb("ident", [P, P])
        col = sb("col", [P, NCOLS])
        row = sb("row", [P, ROW_SET, D])
        prob = sb("prob", [P, 3, 512])
        probT = sb("probT", [P, 3, 512])
        nmax = sb("nmax", [P, 4, 4])
        psums = sb("psums", [P, 4, 4])
        prec = sb("prec", [P, 4, 4])
        st6 = sb("st6", [P, B, 6])
        mv = sb("mv", [P, B, 2])
        sd = sb("sd", [P, 6, B])
        eps = sb("eps", [P, 2])
        q0b = sb("q0b", [P, 1])
        l2q = sb("l2q", [P, 2, H])
        bvr = sb("bvr", [P, 2, 2, D])
        ct = [sb(f"ct{i}", [P, KT, B, P], F32R) for i in range(2)]
        ht = [sb(f"ht{i}", [P, KT, B, P], F32R) for i in range(2)]
        sel = sb("sel", [P, 16, P], F32R)
        indr = sb("indr", [1, 2, P], F32R)
        mb13 = sb("mb13", [1, B * P], F32R)
        mt8 = sb("mt8", [P, B, D], U8)
        mraw3 = sb("mraw3", [1, B * P], U8)
        fs = sb("fs", [P, 10264])
        rs = sb("rs", [P, 13312], F32R)

        def carve(t, at, shape):
            n = int(np.prod(shape))
            names = "abcdef"[:len(shape)]
            kw = {c: k for c, k in zip(names[1:], shape[1:])}
            v = t[:, at:at + n]
            if len(shape) > 1:
                v = v.rearrange(f"p ({' '.join(names)}) -> p {' '.join(names)}", **kw)
            return v, at + n

        def carve2(t, at, shape):
            h, at = carve(t, at, shape)
            l, at = carve(t, at, shape)
            return [h, l], at

        ks, o = carve(rs, 0, [2, 2048])
        qs, o = carve(rs, o, [2, 512])
        dq, o = carve2(rs, o, [2, D])
        dk, o = carve2(rs, o, [2, 512])
        uu, o = carve2(rs, o, [2, 2, P])
        aw_at = o
        aw, o = carve2(rs, o, [4, KT, D])
        assert o <= 13312
        mb0 = rs[0:1, aw_at:aw_at + B * D]
        vt, o = carve(fs, 0, [2, 2, 2, H, 32])
        ms, o = carve(fs, o, [2, B, D])
        xq, o = carve(fs, o, [D])
        w0, o = carve(fs, o, [3, P])
        assert o <= 10264
        pw = [None, None]
        o = 0
        for i in range(2):
            pw[i], o = carve2(rs, o, [4, 512])
        cc, o = carve2(rs, o, [2, B, P])
        assert o <= 13312
        qT, o = carve(fs, 0, [3, B, P])
        kT, o = carve(fs, o, [3, B, P + 1])
        v2, o = carve(fs, o, [2, B, 2, P])
        assert o <= 10264
        mw1, o = carve2(rs, 0, [KT, FF])
        mw2, o = carve2(rs, o, [FT, D])
        gg, o = carve2(rs, o, [FT, D])
        assert o <= 13312
        gf, _ = carve(fs, 0, [2, 512])

        c_in, x_in = sem("constants_loaded"), sem("x_and_ctx_loaded")
        rowb_in = sem("second_rows_loaded")
        l_in = [sem(f"pack_loaded{i}") for i in range(2)]
        bv_in = [sem(f"l2_rows_loaded{i}") for i in range(2)]
        w_hi = sem("weight_hi_written")
        w_lo = sem("weight_pack_taken")
        wv_hi, w_v = sem("l2_v_hi_written"), sem("l2_v_weights_split")
        jm = sem("general_bank_filled")
        a_setup, g_setup = sem("scalar_setup"), sem("off_diagonal_zeroed")
        eps_ok = sem("eps_set")
        vzero = sem("values_zeroed")
        l0stat, l0sq, l0n = sem("l0_stats"), sem("l0_sqrt"), sem("l0_norm_factors")
        xn_done = sem("l0_x_normalised")
        l0var, l0dev, fin = sem("l0_variance"), sem("l0_deviation"), sem("l0_result")
        ybias = sem("residual_biased")
        dch = sem("vector_chain")
        out_done = sem("output_written")
        A = {ph: {n: sem(f"{ph}_{n}") for n in ("xq", "hi", "dense", "stA", "stD", "vals", "sm", "mx", "ex", "rc", "nm",
                                                 "tm", "teA", "teD", "pm", "oeA", "oeD", "done", "mask")} for ph in ATT}
        L = {n: sem(f"L2_{n}") for n in ("qk", "v", "bv", "sm", "mx", "ex", "rc", "nm", "tm", "teA", "teD", "pm", "ch", "cl", "acc")}
        M = {m: {n: sem(f"{m}_{n}") for n in ("gelu", "lo", "out")} for m in ("L1m", "L2m", "L3m")}
        N = {n: {k: sem(f"{n}_{k}") for k in ("stat", "sq", "xh", "a", "hi", "lo")} for n in NORMS}

        block = stack.enter_context(nc.Block())

        def C(name, i=0):
            return col[:, COLS[name][0] + i:COLS[name][0] + i + 1]

        def R(name):
            return row[:, ROWS.index(name) % ROW_SET, :]

        def loaded(eng, name):
            n = PACK_AT[name]
            eng.wait_ge(l_in[n % 2], 16 * (n // 2 + 1))

        def pack_dst(name):
            half = int(name[-1])
            base = name[:-1]
            cut = slice(half * PACK, (half + 1) * PACK)
            if base == "L0w":
                return [w0.rearrange("p a b -> p (a b)")]
            if base.endswith("sel"):
                return [sel[:, :, :].rearrange("p a b -> p (a b)")[:, cut]]
            if base.endswith("att"):
                return [t.rearrange("p a b c -> p (a b c)")[:, cut] for t in aw]
            if base[2] in "ab":
                return [t.rearrange("p a b -> p (a b)")[:, cut] for t in pw[int(base[3]) % 2]]
            return [t.rearrange("p a b -> p (a b)")[:, cut] for t in (mw1 if "w1" in base else mw2)]

        @block.sync
        def _(sp):
            sp.dma_start(X[:, :, :], x.rearrange("b p d -> p b d")).then_inc(x_in, 16)
            sp.dma_start(XH[:, :, :], ctx_in.rearrange("b p d -> p b d")).then_inc(x_in, 16)
            sp.dma_start(ident[:, :], ident_in).then_inc(c_in, 16)
            sp.dma_start(col[:, :], cols).then_inc(c_in, 16)
            sp.dma_start(row[:, :, :].rearrange("p r d -> p (r d)"), rows[0].partition_broadcast(P)).then_inc(c_in, 16)
            sp.dma_start(prob[0:1, 2, 0:2 * P], inds).then_inc(c_in, 16)
            sp.dma_start(probT[0:1, :, :].bitcast(I32).rearrange("p a b -> p (a b)")[:, 0:B * P], mask_s2).then_inc(c_in, 16)
            sp.dma_start(mraw3[:, :], mask_s3).then_inc(c_in, 16)
            sp.dma_start(mt8[:, :, :].rearrange("p b d -> p (b d)"), mask_t[0].partition_broadcast(P)).then_inc(c_in, 16)
            for n, name in enumerate(PACKS):
                if n >= 2:
                    sp.wait_ge(w_lo, n - 1)
                sp.dma_start(wraw[:, n % 2, :], packs[n]).then_inc(l_in[n % 2], 16)
                if name[:3] in ("L2a", "L2b") and name[-1] == "0":
                    i = PAIRS * (name[2] == "b") + int(name[3])
                    if i >= 2:
                        sp.wait_ge(L["v"], 4 * (i - 1))
                    sp.dma_start(bvr[:, i % 2, :, :].rearrange("p a d -> p (a d)"), l2rows[i].partition_broadcast(P))\
                      .then_inc(bv_in[i % 2], 16)
                if name == "L2a7_1":
                    sp.wait_ge(ybias, 3)
                    sp.dma_start(row[:, :, :].rearrange("p r d -> p (r d)"), rows[1].partition_broadcast(P)).then_inc(rowb_in, 16)
            sp.wait_ge(M["L3m"]["out"], B // 2)
            sp.dma_start(out.rearrange("b p d -> p b d"), X[:, :, :]).then_inc(out_done, 16)
            sp.wait_ge(out_done, 16)

        @block.tensor
        def _(pe):
            filled = [0]
            freed_by = [[], []]

            def j_bank():
                i = filled[0] % 2
                for s, v in freed_by[i]:
                    pe.wait_ge(s, v)
                return ps[:, J_BANK + i, :]

            def j_full(last, *frees):
                last.then_inc(jm, 1)
                freed_by[filled[0] % 2] = frees
                filled[0] += 1

            def three(dst, w, m, start, stop):
                nc.tensor.matmul(dst, w[0], m[1], start=start, stop=False)
                nc.tensor.matmul(dst, w[1], m[0], start=False, stop=False)
                return nc.tensor.matmul(dst, w[0], m[0], start=False, stop=stop)

            def both(f):
                return [f(0), f(1)]

            def norm(name, src, ready):
                n = N[name]
                for k in range(B // 2):
                    bank = j_bank()
                    if name == "ctx":
                        pe.wait_ge(x_in, 32)
                        pe.wait_ge(c_in, 16 * 7)
                    else:
                        pe.wait_ge(ready, 2 * k + 2)
                    for q in range(2):
                        for f in range(KT):
                            last = nc.tensor.transpose(bank[:, (2 * q + f) * P:(2 * q + f + 1) * P],
                                                       src[:, 2 * k + q, f * P:(f + 1) * P], ident[:, :])
                    j_full(last, (n["lo" if name in ("ctx", "lat") else "a"], k + 1))

            def dense0(it, a):
                if it == 0:
                    pe.wait_ge(w_lo, PACK_AT["L0w0"] + 1)
                bank = j_bank()
                nc.tensor.matmul(bank[:, 0:D], w0[:, 0, :], X[:, it, :], start=True, stop=True)
                j_full(nc.tensor.matmul(bank[:, D:2 * D], w0[:, 1, :], XH[:, it, :], start=True, stop=True), (a["dense"], it + 1))
                bank = j_bank()
                for t in range(2):
                    last = nc.tensor.matmul(bank[:, t * P:(t + 1) * P], XH[:, it, t * P:(t + 1) * P], w0[:, 2, :],
                                            start=True, stop=True)
                j_full(last, (a["vals"], it + 1))

            def dense(ph, it, a):
                if it == 0:
                    pe.wait_ge(w_lo, PACK_AT[ph + "att1"] + 1)
                pe.wait_ge(N["lat" if ph == "L1" else "L3n1"]["lo"], it + 1)
                bb = slice(2 * it, 2 * it + 2)
                W = lambda kind, f, t: both(lambda i: aw[i][:, kind, f, t * P:(t + 1) * P])
                bank = j_bank()
                for t in range(2):
                    for f in range(KT):
                        last = three(bank[:, t * D:(t + 1) * D], W(0, f, t), both(lambda i: ht[i][:, f, bb, :]), f == 0, f == KT - 1)
                n_hi = 3 if ph == "L1" else 2
                j_full(last, (a["hi"], n_hi * it + 1), (a["dense"], n_hi * it + 1))
                if ph == "L1":
                    for t in range(2):
                        bank = j_bank()
                        for s, src in enumerate((ct, ht)):
                            for f in range(KT):
                                last = three(bank[:, s * D:(s + 1) * D], W(1, f, t), both(lambda i: src[i][:, f, bb, :]),
                                             f == 0, f == KT - 1)
                        j_full(last, (a["hi"], 3 * it + 2 + t), (a["dense"], 3 * it + 2 + t))
                else:
                    bank = j_bank()
                    for t in range(2):
                        for f in range(KT):
                            last = three(bank[:, t * D:(t + 1) * D], W(1, f, t), both(lambda i: ct[i][:, f, bb, :]),
                                         f == 0, f == KT - 1)
                    j_full(last, (a["hi"], 2 * it + 2), (a["dense"], 2 * it + 2))
                for im in range(2 if ph == "L1" else 1):
                    bank = j_bank()
                    for s in range(2):
                        src, b = ((ct, ht)[s], 2 * it + im) if ph == "L1" else (ct, 2 * it + s)
                        for f in range(KT):
                            last = three(bank[:, s * D:(s + 1) * D], both(lambda i: src[i][:, f, b, :]),
                                         both(lambda i: aw[i][:, 2, f, :]), f == 0, f == KT - 1)
                    j_full(last, (a["vals"], (2 * it + im if ph == "L1" else it) + 1))

            def prep(ph, s, a):
                it, m = divmod(s, STEPS)
                per = {"L0": 1, "L1": 3, "L3": 2}[ph]
                pe.wait_ge(a["dense"], per * (it + 1))
                if s == 0:
                    pe.wait_ge(a["mask"], 1)
                    pe.wait_ge(w_lo, PACK_AT[ph + "sel1"] + 1)
                nA, nD = ATT[ph]["stack_a"], ATT[ph]["stack_d"]
                if ph == "L0":
                    bank = j_bank()
                    for i in range(2):
                        nc.tensor.matmul(bank[:, 0:D], sel[:, 4 * m + i, :], dq[i][:, 0, :], start=i == 0, stop=i == 1)
                    for i in range(2):
                        nc.tensor.matmul(bank[:, D:2 * D], sel[:, 4 * m + 2 + i, :], dk[i][:, 0, 0:D], start=i == 0, stop=False)
                    j_full(nc.tensor.matmul(bank[:, D:2 * D], indr[:, 0, :], mb0[:, it * D:(it + 1) * D], start=False, stop=True),
                           (a["stA"], nA * (s + 1)), (a["stD"], s + 1))
                    return
                bank = j_bank()
                for gi in range(2):
                    g = 2 * m + gi
                    for i in range(2):
                        last = nc.tensor.matmul(bank[:, gi * D:(gi + 1) * D], sel[:, 4 * (g % 4) + i, :], dq[i][:, g // 4, :],
                                                start=i == 0, stop=i == 1)
                j_full(last, (a["stA"], nA * s + 1))
                n = 512 if ph == "L1" else D
                for gi in range(2):
                    g = 2 * m + gi
                    if ph == "L1" or gi == 0:
                        bank = j_bank()
                    dst = bank if ph == "L1" else bank[:, gi * D:(gi + 1) * D]
                    for i in range(2):
                        nc.tensor.matmul(dst, sel[:, 4 * (g % 4) + 2 + i, :], dk[i][:, g // 4, 0:n], start=i == 0, stop=False,
                                         skip_group_check=True)
                    last = nc.tensor.matmul(dst[:, 0:D], indr[:, 1, :], mb13[:, 2 * it * P:(2 * it + 2) * P],
                                            start=False, stop=True, skip_group_check=True)
                    if ph == "L1":
                        j_full(last, (a["stA"], nA * s + 2 + gi), (a["stD"], nD * s + 1 + gi))
                if ph == "L3":
                    j_full(last, (a["stA"], nA * s + 2), (a["stD"], nD * s + 1))

            def attention(ph):
                c, a = ATT[ph], A[ph]
                U, KTL = c["units"], c["key_tiles"]
                nh = 4 // U
                for e, i in att_order(ph):
                    if e == "dense":
                        dense0(i, a) if ph == "L0" else dense(ph, i, a)
                    elif e == "prep":
                        prep(ph, i, a)
                    elif e == "S":
                        s, r = divmod(i, 2 * U)
                        im, k = divmod(r, U)
                        if r == 0:
                            pe.wait_ge(a["stA"], c["stack_a"] * (s + 1))
                            pe.wait_ge(a["stD"], c["stack_d"] * (s + 1))
                        if i >= 2:
                            pe.wait_ge(a["ex"], i - 1)
                        bank = ps[:, S_BANK + i % 2, :]
                        if ph == "L0":
                            last = nc.tensor.matmul(bank, qs[:, s % 2, im * P:(im + 1) * P], ks[:, s % 2, k * 512:(k + 1) * 512],
                                                    start=True, stop=True)
                        elif ph == "L1":
                            last = nc.tensor.matmul(bank, qs[:, s % 2, k * D + im * P:k * D + (im + 1) * P],
                                                    ks[:, s % 2, (2 * k + im) * 512:(2 * k + im + 1) * 512], start=True, stop=True)
                        else:
                            for g in range(2):
                                last = nc.tensor.matmul(bank[:, g * D:(g + 1) * D], qs[:, s % 2, g * D + im * P:g * D + (im + 1) * P],
                                                        ks[:, s % 2, (2 * g + im) * D:(2 * g + im + 1) * D], start=True, stop=True)
                        last.then_inc(a["sm"], 1)
                    elif e == "T":
                        pe.wait_ge(a["nm"], i + 1)
                        if i >= 2:
                            pe.wait_ge(a["teD" if i % 2 else "teA"], i // 2)
                        for k in range(4):
                            last = nc.tensor.transpose(ps[:, T_BANK + i % 2, k * P:(k + 1) * P], prob[:, i % 3, k * P:(k + 1) * P],
                                                       ident[:, :])
                        last.then_inc(a["tm"], 1)
                    elif e == "PV":
                        it, r = divmod(i, 2 * STEPS)
                        m, im = divmod(r, 2)
                        u1 = (i + 1) * U - 1
                        pe.wait_ge(a["teA"], u1 // 2 + 1)
                        if u1 >= 1:
                            pe.wait_ge(a["teD"], (u1 + 1) // 2)
                        if m == 0:
                            if im == 0:
                                pe.wait_ge(a["vals"], (2 if ph == "L1" else 1) * (it + 1))
                            if it > 0:
                                pe.wait_ge(a["oeA" if ph == "L0" else "oeD"], 2 * (it - 1) + im + 1)
                        bank = ps[:, O_BANK + im, :]
                        for st in range(2 if ph == "L0" else 1):
                            for t in range(KTL):
                                for q in range(4):
                                    slot = (i * U + q // nh) % 3
                                    c0 = ((q % nh) * KTL + t) * P
                                    if ph == "L0":
                                        v = vt[:, it % 2, st, t, 4 * q + m, :]
                                        dst = bank[32 * q:32 * q + 32, st * P:(st + 1) * P]
                                        first, stop = (m == 0 and t == 0 and st == 0), (m == 3 and t == 1)
                                    else:
                                        v = vt[:, it % 2, im, t, 4 * m + q, :]
                                        dst = bank[32 * q:32 * q + 32, (m // 2) * P:(m // 2 + 1) * P]
                                        first, stop = (m % 2 == 0 and t == 0), (m % 2 == 1 and t == KTL - 1)
                                    last = nc.tensor.matmul(dst, v, probT[:, slot, c0:c0 + P], start=first, stop=stop,
                                                            skip_group_check=True)
                        last.then_inc(a["pm"], 1)
                    elif ph != "L0":
                        pe.wait_ge(a["oeD"], 2 * (i + 1))
                        bank = j_bank()
                        for im in range(2):
                            for t in range(2):
                                last = three(bank[:, im * D:(im + 1) * D], both(lambda k: uu[k][:, im, t, :]),
                                             both(lambda k: aw[k][:, 3, t, :]), t == 0, t == 1)
                        j_full(last, (a["done"], i + 1))

            def wide(layer):
                u0 = 8 * PAIRS * layer
                nrm = N[f"L2n{layer + 1}"]
                for e in wide_order():
                    if e[0] == "qk":
                        _, p, hd, k = e
                        kind, ch = divmod(k, 2)
                        pe.wait_ge(w_lo, PACK_AT[f"L2{'ab'[layer]}{p}_0"] + 1)
                        if kind == 0 and p == 0:
                            pe.wait_ge(nrm["lo"], 2 * ch + 2)
                        src = ct if kind else ht
                        bank = j_bank()
                        for f in range(KT):
                            last = three(bank, both(lambda i: pw[p % 2][i][:, kind, f * D + hd * P:f * D + (hd + 1) * P]),
                                         both(lambda i: src[i][:, f, 4 * ch:4 * ch + 4, :]), f == 0, f == KT - 1)
                        j_full(last, (L["qk"], 4 * (2 * (PAIRS * layer + p) + hd) + k + 1))
                    elif e[0] == "v":
                        _, p, k = e
                        pe.wait_ge(w_v, PAIRS * layer + p + 1)
                        bank = j_bank()
                        for b in range(2):
                            for f in range(KT):
                                last = three(bank[:, b * D:(b + 1) * D], both(lambda i: ct[i][:, f, 2 * k + b, :]),
                                             both(lambda i: pw[p % 2][i][:, 2, f * D:(f + 1) * D]), f == 0, f == KT - 1)
                        j_full(last, (L["v"], 4 * (PAIRS * layer + p) + k + 1))
                    elif e[0] == "S":
                        g = u0 + e[1]
                        p, r = divmod(e[1], 8)
                        hd, b2 = divmod(r, 4)
                        hh = 2 * p + hd
                        pe.wait_ge(L["qk"], 4 * (H * layer + hh + 1))
                        if g >= 2:
                            pe.wait_ge(L["ex"], g - 1)
                        for b in range(2):
                            last = nc.tensor.matmul(ps[:, S_BANK + g % 2, b * D:b * D + P + 1], qT[:, hh % 3, 2 * b2 + b, :],
                                                    kT[:, hh % 3, 2 * b2 + b, :], start=True, stop=True)
                        last.then_inc(L["sm"], 1)
                    elif e[0] == "T":
                        g = u0 + e[1]
                        pe.wait_ge(L["nm"], g + 1)
                        if g >= 2:
                            pe.wait_ge(L["teD" if g % 2 else "teA"], g // 2)
                        for b in range(2):
                            last = nc.tensor.transpose(ps[:, T_BANK + g % 2, b * P:(b + 1) * P], prob[:, g % 3, b * D:b * D + P],
                                                       ident[:, :])
                        last.then_inc(L["tm"], 1)
                    elif e[0] == "PV":
                        g = u0 + e[1]
                        p, r = divmod(e[1], 8)
                        hd, b2 = divmod(r, 4)
                        pe.wait_ge(L["teD" if g % 2 else "teA"], g // 2 + 1)
                        if r == 0:
                            pe.wait_ge(L["v"], 4 * (PAIRS * layer + p + 1))
                        if g >= 2:
                            pe.wait_ge(L["cl"], g - 1)
                        for b in range(2):
                            last = nc.tensor.matmul(ps[:, O_BANK + g % 2, b * P:(b + 1) * P], v2[:, p % 2, 2 * b2 + b, hd, :],
                                                    probT[:, g % 3, b * P:(b + 1) * P], start=True, stop=True)
                        last.then_inc(L["pm"], 1)
                    elif e[0] == "wo":
                        _, p, b2 = e
                        pe.wait_ge(L["cl"], u0 + 8 * p + 4 + b2 + 1)
                        pe.wait_ge(w_lo, PACK_AT[f"L2{'ab'[layer]}{p}_1"] + 1)
                        bank = j_bank()
                        for b in range(2):
                            for hd in range(2):
                                last = three(bank[:, b * D:(b + 1) * D], both(lambda i: cc[i][:, hd, 2 * b2 + b, :]),
                                             both(lambda i: pw[p % 2][i][:, 3, hd * D:(hd + 1) * D]), hd == 0, hd == 1)
                        j_full(last, (L["acc"], 4 * (PAIRS * layer + p) + b2 + 1))

            def mlp(name, nrm):
                m = M[name + "m"]
                for e in mlp_order():
                    if e[0] == "up":
                        _, c, f2 = e
                        if c == 0:
                            pe.wait_ge(w_lo, PACK_AT[name + "w1_1"] + 1)
                        pe.wait_ge(nrm["lo"], c + 1)
                        bank = j_bank()
                        for fi in range(2):
                            f = 2 * f2 + fi
                            for k in range(KT):
                                last = three(bank[:, fi * D:(fi + 1) * D], both(lambda i: mw1[i][:, k, f * P:(f + 1) * P]),
                                             both(lambda i: ht[i][:, k, 2 * c:2 * c + 2, :]), k == 0, k == KT - 1)
                        j_full(last, (m["gelu"], (FT // 2) * c + f2 + 1))
                    else:
                        c = e[1]
                        pe.wait_ge(w_lo, PACK_AT[name + "w2_1"] + 1)
                        pe.wait_ge(m["lo"], (FT // 2) * (c + 1))
                        bank = j_bank()
                        for b in range(2):
                            for f in range(FT):
                                last = three(bank[:, b * D:(b + 1) * D], both(lambda i: gg[i][:, f, b * P:(b + 1) * P]),
                                             both(lambda i: mw2[i][:, f, :]), f == 0, f == FT - 1)
                        j_full(last, (m["out"], c + 1))

            norm("ctx", XH, None)
            attention("L0")
            norm("lat", X, fin)
            attention("L1")
            norm("L1r", XH, N["L1r"]["xh"])
            mlp("L1", N["L1r"])
            norm("L2n1", XH, N["L2n1"]["xh"])
            wide(0)
            norm("L2n2", XH, N["L2n2"]["xh"])
            wide(1)
            norm("L2nm", XH, N["L2nm"]["xh"])
            mlp("L2", N["L2nm"])
            norm("L3n1", XH, N["L3n1"]["xh"])
            attention("L3")
            norm("L3nm", XH, N["L3nm"]["xh"])
            mlp("L3", N["L3nm"])

        @block.scalar
        def _(act):
            taken = [0]

            def j_take():
                j = taken[0]
                taken[0] += 1
                act.wait_ge(jm, j + 1)
                return ps[:, J_BANK + j % 2, :]

            def j_skip():
                taken[0] += 1

            def take(name):
                loaded(act, name)
                nc.scalar.copy(pack_dst(name)[0], wraw[:, PACK_AT[name] % 2, :]).then_inc(w_hi, 1)

            def take_mlp(n):
                for w in ("w1_0", "w1_1", "w2_0", "w2_1"):
                    take(n + w)

            def norm(name, affine):
                n = N[name]
                if affine:
                    act.wait_ge(n["stat"], 1)
                    nc.scalar.activation(sd[:, 1, :], sd[:, 0, :], ACT.Sqrt,
                                         bias=eps[:, 1:2] if name == "L1r" else eps[:, 0:1]).then_inc(n["sq"], 1)
                for k in range(B // 2):
                    src = j_take().rearrange("p (q f n) -> p q f n", q=2, f=KT)
                    for f in range(KT):
                        if not affine:
                            dst = (ct if name == "ctx" else ht)[0]
                            last = nc.scalar.copy(dst[:, f, 2 * k:2 * k + 2, :], src[:, :, f, :])
                            continue
                        if k >= 3 and f == 0:
                            act.wait_ge(n["lo"], k - 2)
                        dst = probT[:, k % 3, f * D:(f + 1) * D].rearrange("p (q n) -> p q n", q=2)
                        if affine[1]:
                            last = nc.scalar.activation(dst, src[:, :, f, :], ACT.Identity, scale=C(affine[0], f), bias=C(affine[1], f))
                        else:
                            last = nc.scalar.mul(dst, src[:, :, f, :], C(affine[0], f))
                    last.then_inc(n["a" if affine else "hi"], 1)

            def attention(ph):
                c, a = ATT[ph], A[ph]
                U, keys = c["units"], c["keys"]
                nh = 4 // U
                for e, i in att_order(ph):
                    if e == "dense":
                        bank = j_take()
                        if ph == "L0":
                            if i > 0:
                                act.wait_ge(a["dense"], i)
                            nc.scalar.activation(xq, bank[:, 0:D], ACT.Identity, bias=q0b[:, :], scale=Q0_SCALE).then_inc(a["xq"], 1)
                            nc.scalar.activation(dk[0][:, 0, 0:D], bank[:, D:2 * D], ACT.Identity, bias=C("L0k")).then_inc(a["hi"], 1)
                            j_skip()
                            continue
                        for t in range(2):
                            last = nc.scalar.activation(dq[0][:, t, :], bank[:, t * D:(t + 1) * D], ACT.Identity, bias=C(ph + "q", t))
                        last.then_inc(a["hi"], 1)
                        if ph == "L1":
                            for t in range(2):
                                nc.scalar.activation(dk[0][:, t, :], j_take(), ACT.Identity, bias=C("L1k", t)).then_inc(a["hi"], 1)
                            j_skip()
                        else:
                            bank = j_take()
                            for t in range(2):
                                last = nc.scalar.activation(dk[0][:, t, 0:D], bank[:, t * D:(t + 1) * D], ACT.Identity, bias=C("L3k", t))
                            last.then_inc(a["hi"], 1)
                        j_skip()
                    elif e == "prep":
                        if i >= 2:
                            act.wait_ge(a["sm"], 2 * U * (i - 1))
                        else:
                            act.wait_ge(g_setup, {"L0": 1, "L1": 2, "L3": 3}[ph])
                        bank = j_take()
                        if ph == "L0":
                            nc.scalar.activation(qs[:, i % 2, 0:D], bank[:, 0:D], ACT.Identity, bias=C("ones0")).then_inc(a["stA"], 1)
                            for q in range(2):
                                last = nc.scalar.copy(ks[32 * q:32 * q + 32, i % 2, q * D:(q + 1) * D], bank[32 * q:32 * q + 32, D:2 * D])
                            last.then_inc(a["stA"], 1)
                            continue
                        nc.scalar.activation(qs[:, i % 2, :], bank, ACT.Identity, bias=C("ones1")).then_inc(a["stA"], 1)
                        if ph == "L1":
                            for g in range(2):
                                src = j_take()[0:64, :].rearrange("p (s m n) -> p m s n", s=2, m=2)
                                dst = ks[0:64, i % 2, g * 1024:(g + 1) * 1024].rearrange("p (m h s n) -> p m h s n", m=2, h=2, s=2)
                                nc.scalar.copy(dst[:, :, 0, :, :], src).then_inc(a["stA"], 1)
                        else:
                            bank = j_take()
                            for g in range(2):
                                src = bank[0:64, g * D:(g + 1) * D].rearrange("p (m n) -> p m n", m=2)
                                dst = ks[0:64, i % 2, g * 512:(g + 1) * 512].rearrange("p (m h n) -> p m h n", m=2, h=2)
                                last = nc.scalar.copy(dst[:, :, 0, :], src)
                            last.then_inc(a["stA"], 1)
                    elif e == "S":
                        act.wait_ge(a["mx"], i + 1)
                        if i >= 3:
                            act.wait_ge(a["tm"], i - 2)
                        for k in range(nh):
                            last = nc.scalar.activation(prob[:, i % 3, k * keys:(k + 1) * keys],
                                                        ps[:, S_BANK + i % 2, k * keys:(k + 1) * keys], ACT.Exp,
                                                        bias=nmax[:, i % 4, k:k + 1], accum_out=psums[:, i % 4, k:k + 1])
                        last.then_inc(a["ex"], 1)
                    elif e == "T":
                        if i % 2 == 0:
                            act.wait_ge(a["tm"], i + 1)
                            if i >= 3:
                                act.wait_ge(a["pm"], (i - 3) // U + 1)
                            nc.scalar.copy(probT[:, i % 3, :], ps[:, T_BANK, :]).then_inc(a["teA"], 1)
                    elif e == "OUT":
                        for im in range(2):
                            act.wait_ge(a["pm"], 2 * STEPS * (i + 1) - 1 + im)
                            bank = ps[:, O_BANK + im, :]
                            if ph == "L0":
                                if im == 0:
                                    act.wait_ge(xn_done, i + 1)
                                nc.scalar.copy(ms[:, :, i, im * P:(im + 1) * P], bank[:, 0:D].rearrange("p (t n) -> p t n", t=2))\
                                  .then_inc(a["oeA"], 1)
                            else:
                                if i > 0:
                                    act.wait_ge(a["done"], i)
                                nc.scalar.copy(uu[0][:, im, :, :], bank[:, 0:D].rearrange("p (t n) -> p t n", t=2)).then_inc(a["oeA"], 1)
                        if ph != "L0":
                            j_skip()

            def wide(layer):
                u0 = 8 * PAIRS * layer
                lt = "ab"[layer]
                for e in wide_order():
                    if e[0] == "qk":
                        _, p, hd, k = e
                        hh = 2 * p + hd
                        kind, ch = divmod(k, 2)
                        bank = j_take()
                        if hh >= 3:
                            act.wait_ge(L["sm"], u0 + 4 * (hh - 2))
                        src = bank.rearrange("p (b n) -> p b n", b=4)
                        if kind == 0:
                            last = nc.scalar.activation(qT[:, hh % 3, 4 * ch:4 * ch + 4, :], src, ACT.Identity,
                                                        bias=l2q[:, layer, hh:hh + 1], scale=Q2_SCALE)
                        else:
                            nc.scalar.activation(kT[:, hh % 3, 4 * ch:4 * ch + 4, P:P + 1], ident[:, 0:4].unsqueeze(2), ACT.Identity,
                                                 bias=C(f"L2bk{layer + 1}", hh), scale=0.0)
                            last = nc.scalar.activation(kT[:, hh % 3, 4 * ch:4 * ch + 4, 0:P], src, ACT.Identity,
                                                        bias=C(f"L2k{layer + 1}", hh))
                        last.then_inc(L["qk"], 1)
                    elif e[0] == "v":
                        j_skip()
                    elif e[0] == "wo":
                        j_skip()
                    elif e[0] == "split":
                        take(f"L2{lt}{e[1]}_0")
                        split_half(layer, e[1], 2)
                    elif e[0] == "split_o":
                        if e[1] >= 2:
                            act.wait_ge(L["acc"], 4 * (PAIRS * layer + e[1] - 1))
                        split_half(layer, e[1], 3)
                    elif e[0] == "S":
                        g = u0 + e[1]
                        act.wait_ge(L["mx"], g + 1)
                        if g >= 3:
                            act.wait_ge(L["tm"], g - 2)
                        for k in range(2):
                            last = nc.scalar.activation(prob[:, g % 3, k * D:k * D + P + 1], ps[:, S_BANK + g % 2, k * D:k * D + P + 1],
                                                        ACT.Exp, bias=nmax[:, g % 4, k:k + 1], accum_out=psums[:, g % 4, k:k + 1])
                        last.then_inc(L["ex"], 1)
                    elif e[0] == "T":
                        g = u0 + e[1]
                        if g % 2 == 0:
                            act.wait_ge(L["tm"], g + 1)
                            if g >= 3:
                                act.wait_ge(L["pm"], g - 2)
                            nc.scalar.copy(probT[:, g % 3, 0:D], ps[:, T_BANK, 0:D]).then_inc(L["teA"], 1)
                    elif e[0] == "PV":
                        g = u0 + e[1]
                        p, r = divmod(e[1], 8)
                        hd, b2 = divmod(r, 4)
                        act.wait_ge(L["pm"], g + 1)
                        if p >= 1:
                            act.wait_ge(L["acc"], 4 * (PAIRS * layer + p - 1) + b2 + 1)
                        nc.scalar.activation(cc[0][:, hd, 2 * b2:2 * b2 + 2, :],
                                             ps[:, O_BANK + g % 2, 0:D].rearrange("p (b n) -> p b n", b=2), ACT.Identity,
                                             bias=C(f"L2bv{layer + 1}", 2 * p + hd)).then_inc(L["ch"], 1)

            def split_half(layer, p, kind):
                name = f"L2{'ab'[layer]}{p}_1"
                loaded(act, name)
                at = (kind - 2) * 512
                nc.scalar.copy(pw[p % 2][0][:, kind, :], wraw[:, PACK_AT[name] % 2, at:at + 512])\
                  .then_inc(wv_hi if kind == 2 else w_hi, 1)

            def mlp(name, func):
                m = M[name + "m"]
                for e in mlp_order():
                    if e[0] == "down":
                        j_skip()
                        continue
                    k = (FT // 2) * e[1] + e[2]
                    bank = j_take()
                    if k >= 2:
                        act.wait_ge(m["lo"], k - 1)
                    for fi in range(2):
                        last = nc.scalar.activation(gf[:, k % 2, fi * D:(fi + 1) * D], bank[:, fi * D:(fi + 1) * D], func,
                                                    bias=C(name + "b1", 2 * e[2] + fi))
                    last.then_inc(m["gelu"], 1)

            act.wait_ge(c_in, 16 * 7)
            nc.scalar.mul(q0b[:, :], C("L0q"), Q0_SCALE).then_inc(a_setup, 1)
            for layer in range(2):
                at = COLS[f"L2q{layer + 1}"][0]
                nc.scalar.mul(l2q[:, layer, :], col[:, at:at + H], Q2_SCALE).then_inc(a_setup, 1)
            act.wait_ge(a_setup, 3)
            norm("ctx", None)
            act.wait_ge(l0stat, 1)
            act.wait_ge(eps_ok, 1)
            nc.scalar.activation(sd[:, 1, :], sd[:, 0, :], ACT.Sqrt, bias=eps[:, 0:1]).then_inc(l0sq, 1)
            attention("L0")
            for k in range(B // 2):
                act.wait_ge(l0var, k + 1)
                nc.scalar.activation(ms[:, 1, 2 * k:2 * k + 2, :], ms[:, 1, 2 * k:2 * k + 2, :], ACT.Sqrt).then_inc(l0dev, 1)
            act.wait_ge(fin, B)
            take("L1att0")
            take("L1att1")
            norm("lat", None)
            attention("L1")
            act.wait_ge(A["L1"]["done"], 4)
            take_mlp("L1")
            norm("L1r", ("L1w", None))
            mlp("L1", ACT.Gelu_apprx_tanh)
            act.wait_ge(M["L1m"]["out"], B // 2)
            for layer in range(2):
                take(f"L2{'ab'[layer]}0_0")
                split_half(layer, 0, 2)
                split_half(layer, 0, 3)
                norm(f"L2n{layer + 1}", (f"L2lw{layer + 1}", f"L2lb{layer + 1}"))
                wide(layer)
                act.wait_ge(L["acc"], 4 * PAIRS * (layer + 1))
            take_mlp("L2")
            norm("L2nm", ("L2mw", "L2mb"))
            mlp("L2", ACT.Gelu)
            act.wait_ge(M["L2m"]["out"], B // 2)
            take("L3att0")
            take("L3att1")
            norm("L3n1", ("L3lw", "L3lb"))
            attention("L3")
            act.wait_ge(A["L3"]["done"], 4)
            take_mlp("L3")
            norm("L3nm", ("L3mw", "L3mb"))
            mlp("L3", ACT.Gelu_apprx_tanh)

        @block.vector
        def _(dve):
            taken = [0]
            links = [0]

            def link(ins):
                links[0] += 1
                ins.then_inc(dch, 1)
                dve.wait_ge(dch, links[0])

            def j_take():
                j = taken[0]
                taken[0] += 1
                dve.wait_ge(jm, j + 1)
                return ps[:, J_BANK + j % 2, :]

            def j_skip():
                taken[0] += 1

            def f32(ap):
                return ap.bitcast(F32)

            def take(name):
                loaded(dve, name)
                src = wraw[:, PACK_AT[name] % 2, :]
                dst = pack_dst(name)
                if len(dst) == 1:
                    nc.vector.tensor_copy(dst[0], src[:, 0:dst[0].shape[-1]]).then_inc(w_lo, 1)
                    return
                dve.wait_ge(w_hi, SPLIT_COUNT[name])
                nc.vector.tensor_tensor(dst[1], src, f32(dst[0]), ALU.subtract).then_inc(w_lo, 1)

            def take_mlp(n):
                for w in ("w1_0", "w1_1", "w2_0", "w2_1"):
                    take(n + w)

            def norm(name, src):
                n = N[name]
                if src is not None:
                    for b in range(B):
                        last = nc.vector.bn_stats(st6[:, b, :], src[:, b, :])
                    link(last)
                    for b in range(B):
                        last = nc.vector.bn_aggr(mv[:, b, :], st6[:, b, :])
                    link(last)
                    if name == "L1r":
                        link(nc.vector.tensor_tensor(sd[:, 2, :], mv[:, :, 0], mv[:, :, 0], ALU.mult))
                        nc.vector.tensor_tensor(sd[:, 0, :], sd[:, 2, :], mv[:, :, 1], ALU.add).then_inc(n["stat"], 1)
                    else:
                        nc.vector.tensor_copy(sd[:, 0, :], mv[:, :, 1]).then_inc(n["stat"], 1)
                    dve.wait_ge(n["sq"], 1)
                    link(nc.vector.reciprocal(sd[:, 3, :], sd[:, 1, :]))
                    for b in range(B):
                        if name == "L1r":
                            i = nc.vector.tensor_scalar(XH[:, b, :], src[:, b, :], sd[:, 3, b:b + 1], None, ALU.mult)
                        else:
                            i = nc.vector.tensor_scalar(XH[:, b, :], src[:, b, :], mv[:, b, 0:1], sd[:, 3, b:b + 1],
                                                        ALU.subtract, ALU.mult)
                        i.then_inc(n["xh"], 1)
                for k in range(B // 2):
                    bank = j_take().rearrange("p (q f n) -> p q f n", q=2, f=KT)
                    hi, lo = ct if name == "ctx" else ht
                    two = slice(2 * k, 2 * k + 2)
                    if src is None:
                        dve.wait_ge(n["hi"], k + 1)
                        for f in range(KT):
                            last = nc.vector.tensor_tensor(lo[:, f, two, :], bank[:, :, f, :], f32(hi[:, f, two, :]), ALU.subtract)
                    else:
                        dve.wait_ge(n["a"], k + 1)
                        xa = probT[:, k % 3, :].rearrange("p (f q n) -> p f q n", f=KT, q=2)
                        link(nc.vector.tensor_copy(hi[:, :, two, :], xa))
                        last = nc.vector.tensor_tensor(lo[:, :, two, :], xa, f32(hi[:, :, two, :]), ALU.subtract)
                    last.then_inc(n["lo"], 1)

            def attention(ph):
                c, a = ATT[ph], A[ph]
                U, keys = c["units"], c["keys"]
                nh = 4 // U
                total = c["iters"] * STEPS * 2 * U

                def reciprocal(u):
                    dve.wait_ge(a["ex"], u + 1)
                    if u >= 4:
                        dve.wait_ge(a["nm"], u - 3)
                    nc.vector.reciprocal(prec[:, u % 4, 0:nh], psums[:, u % 4, 0:nh]).then_inc(a["rc"], 1)

                for e, i in att_order(ph):
                    if e == "dense" and ph == "L0":
                        bank = j_take()
                        dve.wait_ge(a["hi"], i + 1)
                        nc.vector.scalar_tensor_tensor(dk[1][:, 0, 0:D], bank[:, D:2 * D], C("L0k"), f32(dk[0][:, 0, 0:D]),
                                                       ALU.add, ALU.subtract)
                        dve.wait_ge(a["xq"], i + 1)
                        link(nc.vector.tensor_copy(dq[0][:, 0, :], xq))
                        nc.vector.tensor_tensor(dq[1][:, 0, :], xq, f32(dq[0][:, 0, :]), ALU.subtract).then_inc(a["dense"], 1)
                        bank = j_take()
                        if i == 0:
                            dve.wait_ge(vzero, 1)
                        for t in range(2):
                            v = diag(vt[:, i % 2, 0, t, :, :].rearrange("p (q g) c -> p q (g c)", q=4))
                            src = bank[:, t * P:(t + 1) * P].rearrange("p (q g d) -> p q g d", q=4, g=4)
                            bias = R("L0v")[:, 0:P].rearrange("p (q g d) -> p q g d", q=4, g=4)
                            last = nc.vector.tensor_tensor(v, src, bias, ALU.add)
                        link(last)
                        for t in range(2):
                            v = diag(vt[:, i % 2, 0, t, :, :].rearrange("p (q g) c -> p q (g c)", q=4))
                            vv = diag(vt[:, i % 2, 1, t, :, :].rearrange("p (q g) c -> p q (g c)", q=4))
                            last = nc.vector.tensor_tensor(vv, v, v, ALU.mult)
                        last.then_inc(a["vals"], 1)
                    elif e == "dense":
                        n_hi = 3 if ph == "L1" else 2
                        bank = j_take()
                        dve.wait_ge(a["hi"], n_hi * i + 1)
                        for t in range(2):
                            last = nc.vector.scalar_tensor_tensor(dq[1][:, t, :], bank[:, t * D:(t + 1) * D], C(ph + "q", t),
                                                                  f32(dq[0][:, t, :]), ALU.add, ALU.subtract)
                        last.then_inc(a["dense"], 1)
                        if ph == "L1":
                            for t in range(2):
                                bank = j_take()
                                dve.wait_ge(a["hi"], 3 * i + 2 + t)
                                nc.vector.scalar_tensor_tensor(dk[1][:, t, :], bank, C("L1k", t), f32(dk[0][:, t, :]),
                                                               ALU.add, ALU.subtract).then_inc(a["dense"], 1)
                        else:
                            bank = j_take()
                            dve.wait_ge(a["hi"], 2 * i + 2)
                            for t in range(2):
                                last = nc.vector.scalar_tensor_tensor(dk[1][:, t, 0:D], bank[:, t * D:(t + 1) * D], C("L3k", t),
                                                                      f32(dk[0][:, t, 0:D]), ALU.add, ALU.subtract)
                            last.then_inc(a["dense"], 1)
                        if i == 0:
                            dve.wait_ge(vzero, {"L1": 2, "L3": 3}[ph])
                        for k in range(2 if ph == "L1" else 1):
                            bank = j_take()
                            for s in range(2):
                                im, t = (k, s) if ph == "L1" else (s, 0)
                                src = bank[:, s * D:(s + 1) * D].rearrange("p (t e q d) -> p e t q d", t=2, e=2, q=4)
                                bias = R(ph + "v").rearrange("p (t e q d) -> p e t q d", t=2, e=2, q=4)
                                dst = vt[:, i % 2, im, t, :, :].rearrange("p (t e q) c -> p e t q c", t=2, e=2)
                                for half in range(2):
                                    last = nc.vector.tensor_tensor(dst[:, half, :, :, 16 * half:16 * half + 16], src[:, half], bias[:, half], ALU.add)
                            last.then_inc(a["vals"], 1)
                    elif e == "prep":
                        if i >= 2:
                            dve.wait_ge(a["sm"], 2 * U * (i - 1))
                        else:
                            dve.wait_ge(g_setup, {"L0": 1, "L1": 2, "L3": 3}[ph])
                        if ph == "L0":
                            bank = j_take()
                            dve.wait_ge(a["stA"], 2 * i + 1)
                            for q in range(2, 4):
                                last = nc.vector.tensor_copy(ks[32 * q:32 * q + 32, i % 2, q * D:(q + 1) * D],
                                                             bank[32 * q:32 * q + 32, D:2 * D])
                            last.then_inc(a["stD"], 1)
                            continue
                        j_skip()
                        if ph == "L1":
                            for g in range(2):
                                src = j_take()[64:128, :].rearrange("p (s m n) -> p m s n", s=2, m=2)
                                dst = ks[64:128, i % 2, g * 1024:(g + 1) * 1024].rearrange("p (m h s n) -> p m h s n", m=2, h=2, s=2)
                                nc.vector.tensor_copy(dst[:, :, 1, :, :], src).then_inc(a["stD"], 1)
                        else:
                            bank = j_take()
                            for g in range(2):
                                src = bank[64:128, g * D:(g + 1) * D].rearrange("p (m n) -> p m n", m=2)
                                dst = ks[64:128, i % 2, g * 512:(g + 1) * 512].rearrange("p (m h n) -> p m h n", m=2, h=2)
                                last = nc.vector.tensor_copy(dst[:, :, 1, :], src)
                            last.then_inc(a["stD"], 1)
                    elif e == "S":
                        dve.wait_ge(a["sm"], i + 1)
                        nc.vector.tensor_reduce(nmax[:, i % 4, 0:nh], ps[:, S_BANK + i % 2, :].rearrange("p (h n) -> p h n", h=nh),
                                                AX.X, ALU.max, negate=True).then_inc(a["mx"], 1)
                        if i >= 1:
                            reciprocal(i - 1)
                        if i == total - 1:
                            reciprocal(i)
                    elif e == "T":
                        if i % 2 == 1:
                            dve.wait_ge(a["tm"], i + 1)
                            if i >= 3:
                                dve.wait_ge(a["pm"], (i - 3) // U + 1)
                            nc.vector.tensor_copy(probT[:, i % 3, :], ps[:, T_BANK + 1, :]).then_inc(a["teD"], 1)
                    elif e == "OUT" and ph != "L0":
                        for im in range(2):
                            dve.wait_ge(a["oeA"], 2 * i + im + 1)
                            nc.vector.tensor_tensor(uu[1][:, im, :, :], ps[:, O_BANK + im, 0:D].rearrange("p (t n) -> p t n", t=2),
                                                    f32(uu[0][:, im, :, :]), ALU.subtract).then_inc(a["oeD"], 1)
                        bank = j_take()
                        dve.wait_ge(ybias, 1 if ph == "L1" else 6)
                        dst = (XH if ph == "L1" else X)[:, 2 * i:2 * i + 2, :]
                        nc.vector.tensor_tensor(dst, bank.rearrange("p (b n) -> p b n", b=2), dst, ALU.add).then_inc(a["done"], 1)

            def diag(v):
                return bass.AP(v.tensor, v.offset, [list(v.ap[0]), list(v.ap[1]), [40, 4], [1, 8]])

            def wide(layer):
                u0 = 8 * PAIRS * layer
                lt = "ab"[layer]

                def reciprocal(g):
                    dve.wait_ge(L["ex"], g + 1)
                    if g >= 4:
                        dve.wait_ge(L["nm"], g - 3)
                    nc.vector.reciprocal(prec[:, g % 4, 0:2], psums[:, g % 4, 0:2]).then_inc(L["rc"], 1)

                for e in wide_order():
                    if e[0] == "qk":
                        j_skip()
                    elif e[0] == "v":
                        _, p, k = e
                        i = PAIRS * layer + p
                        if k == 0:
                            dve.wait_ge(bv_in[i % 2], 16 * (i // 2 + 1))
                            link(nc.vector.tensor_tensor(bvr[:, i % 2, 0, :], bvr[:, i % 2, 0, :], bvr[:, i % 2, 1, :], ALU.subtract))
                        bank = j_take().rearrange("p (b n) -> p b n", b=2)
                        nc.vector.tensor_tensor(v2[:, p % 2, 2 * k:2 * k + 2, :, :].rearrange("p b h n -> p b (h n)"), bank,
                                                bvr[:, i % 2, 0:1, :].broadcast_to([P, 2, D]), ALU.add).then_inc(L["v"], 1)
                    elif e[0] == "wo":
                        _, p, b2 = e
                        bank = j_take().rearrange("p (b n) -> p b n", b=2)
                        if p == 0 and b2 == 0:
                            dve.wait_ge(ybias, 3 + layer)
                        if p > 0:
                            dve.wait_ge(L["acc"], 4 * (PAIRS * layer + p - 1) + b2 + 1)
                        dst = X[:, 2 * b2:2 * b2 + 2, :]
                        nc.vector.tensor_tensor(dst, bank, dst, ALU.add).then_inc(L["acc"], 1)
                    elif e[0] == "split":
                        take(f"L2{lt}{e[1]}_0")
                        split_half(layer, e[1], 2)
                    elif e[0] == "split_o":
                        split_half(layer, e[1], 3)
                    elif e[0] == "S":
                        g = u0 + e[1]
                        dve.wait_ge(L["sm"], g + 1)
                        nc.vector.tensor_reduce(nmax[:, g % 4, 0:2],
                                                ps[:, S_BANK + g % 2, :].rearrange("p (h n) -> p h n", h=2)[:, :, 0:P + 1],
                                                AX.X, ALU.max, negate=True).then_inc(L["mx"], 1)
                        reciprocal(g)
                    elif e[0] == "T":
                        g = u0 + e[1]
                        if g % 2 == 1:
                            dve.wait_ge(L["tm"], g + 1)
                            if g >= 3:
                                dve.wait_ge(L["pm"], g - 2)
                            nc.vector.tensor_copy(probT[:, g % 3, 0:D], ps[:, T_BANK + 1, 0:D]).then_inc(L["teD"], 1)
                    elif e[0] == "PV":
                        g = u0 + e[1]
                        p, r = divmod(e[1], 8)
                        hd, b2 = divmod(r, 4)
                        dve.wait_ge(L["ch"], g + 1)
                        two = slice(2 * b2, 2 * b2 + 2)
                        nc.vector.scalar_tensor_tensor(cc[1][:, hd, two, :], ps[:, O_BANK + g % 2, 0:D].rearrange("p (b n) -> p b n", b=2),
                                                       C(f"L2bv{layer + 1}", 2 * p + hd), f32(cc[0][:, hd, two, :]),
                                                       ALU.add, ALU.subtract).then_inc(L["cl"], 1)

            def split_half(layer, p, kind):
                name = f"L2{'ab'[layer]}{p}_1"
                loaded(dve, name)
                at = (kind - 2) * 512
                if kind == 2:
                    dve.wait_ge(wv_hi, PAIRS * layer + p + 1)
                else:
                    dve.wait_ge(w_hi, SPLIT_COUNT[name])
                nc.vector.tensor_tensor(pw[p % 2][1][:, kind, :], wraw[:, PACK_AT[name] % 2, at:at + 512], f32(pw[p % 2][0][:, kind, :]),
                                        ALU.subtract).then_inc(w_v if kind == 2 else w_lo, 1)

            def mlp(name, y):
                m = M[name + "m"]
                for e in mlp_order():
                    if e[0] == "up":
                        k = (FT // 2) * e[1] + e[2]
                        j_skip()
                        dve.wait_ge(m["gelu"], k + 1)
                        src = gf[:, k % 2, :].rearrange("p (f n) -> p f n", f=2)
                        two = slice(2 * e[2], 2 * e[2] + 2)
                        if e[1] > 0 and e[2] == 0:
                            dve.wait_ge(m["out"], e[1])
                        link(nc.vector.tensor_copy(gg[0][:, two, :], src))
                        nc.vector.tensor_tensor(gg[1][:, two, :], src, f32(gg[0][:, two, :]), ALU.subtract).then_inc(m["lo"], 1)
                    else:
                        c = e[1]
                        bank = j_take().rearrange("p (b n) -> p b n", b=2)
                        if c == 0:
                            dve.wait_ge(ybias, y)
                        dst = X[:, 2 * c:2 * c + 2, :]
                        nc.vector.tensor_tensor(dst, bank, dst, ALU.add).then_inc(m["out"], 1)

            nc.vector.memset(eps[:, 0:1], 1e-5)
            nc.vector.memset(eps[:, 1:2], 1e-6).then_inc(eps_ok, 1)
            dve.wait_ge(c_in, 16 * 7)
            nc.vector.tensor_copy(indr[:, :, :].rearrange("p a b -> p (a b)"), prob[0:1, 2, 0:2 * P])
            nc.vector.tensor_scalar(mb0, mt8[0:1, :, :].rearrange("p a b -> p (a b)"), 0.0, MASKED, ALU.is_equal, ALU.mult)\
              .then_inc(A["L0"]["mask"], 1)
            nc.vector.tensor_scalar(mb13[:, :], probT[0:1, :, :].bitcast(I32).rearrange("p a b -> p (a b)")[:, 0:B * P],
                                    0.0, MASKED, ALU.is_equal, ALU.mult).then_inc(A["L1"]["mask"], 1)
            take("L0w0")
            take("L0sel0")
            take("L0sel1")
            norm("ctx", None)
            dve.wait_ge(x_in, 32)
            link(nc.vector.tensor_reduce(sd[:, 2, :], mt8[:, :, :], AX.X, ALU.add))
            for b in range(B):
                last = nc.vector.tensor_tensor_reduce(ms[:, 0, b, :], X[:, b, :], mt8[:, b, :], 1.0, 0.0, ALU.mult, ALU.add, sd[:, 3, b:b + 1])
            link(last)
            for b in range(B):
                last = nc.vector.tensor_tensor_reduce(ms[:, 1, b, :], ms[:, 0, b, :], ms[:, 0, b, :], 1.0, 0.0, ALU.mult, ALU.add, sd[:, 4, b:b + 1])
            link(nc.vector.reciprocal(sd[:, 2, :], sd[:, 2, :]))
            link(nc.vector.tensor_tensor(mv[:, :, 0], sd[:, 3, :], sd[:, 2, :], ALU.mult))
            link(nc.vector.tensor_tensor(sd[:, 4, :], sd[:, 4, :], sd[:, 2, :], ALU.mult))
            link(nc.vector.tensor_tensor(sd[:, 5, :], mv[:, :, 0], mv[:, :, 0], ALU.mult))
            link(nc.vector.tensor_tensor(sd[:, 4, :], sd[:, 4, :], sd[:, 5, :], ALU.subtract))
            nc.vector.tensor_scalar(sd[:, 0, :], sd[:, 4, :], 0.0, None, ALU.max).then_inc(l0stat, 1)
            dve.wait_ge(l0sq, 1)
            nc.vector.reciprocal(sd[:, 3, :], sd[:, 1, :]).then_inc(l0n, 1)
            attention("L0")
            tmp = fs[:, 0:2 * D].rearrange("p (b n) -> p b n", b=2)
            for k in range(B // 2):
                two = slice(2 * k, 2 * k + 2)
                if k == 0:
                    dve.wait_ge(A["L0"]["oeA"], 2 * B)
                else:
                    dve.wait_ge(l0var, k)
                link(nc.vector.tensor_tensor(tmp, ms[:, 0, two, :], ms[:, 0, two, :], ALU.mult))
                link(nc.vector.tensor_tensor(tmp, ms[:, 1, two, :], tmp, ALU.subtract))
                nc.vector.tensor_scalar(ms[:, 1, two, :], tmp, 0.0, None, ALU.max).then_inc(l0var, 1)
            dve.wait_ge(l0var, B // 2)
            for k in range(B // 2):
                two = slice(2 * k, 2 * k + 2)
                if k == 0:
                    dve.wait_ge(xn_done, B)
                dve.wait_ge(l0dev, k + 1)
                link(nc.vector.tensor_tensor(X[:, two, :], X[:, two, :], ms[:, 1, two, :], ALU.mult))
                link(nc.vector.tensor_tensor(X[:, two, :], X[:, two, :], ms[:, 0, two, :], ALU.add))
                nc.vector.tensor_tensor(X[:, two, :], X[:, two, :], mt8[:, two, :], ALU.mult).then_inc(fin, 2)
            for n in ("L1sel0", "L1sel1", "L1att0", "L1att1"):
                take(n)
            norm("lat", None)
            attention("L1")
            dve.wait_ge(A["L1"]["done"], 4)
            take_mlp("L1")
            nc.vector.tensor_scalar(mb13[:, :], mraw3[:, :], 0.0, MASKED, ALU.is_equal, ALU.mult).then_inc(A["L3"]["mask"], 1)
            norm("L1r", XH)
            mlp("L1", 2)
            dve.wait_ge(M["L1m"]["out"], B // 2)
            for layer in range(2):
                take(f"L2{'ab'[layer]}0_0")
                split_half(layer, 0, 2)
                split_half(layer, 0, 3)
                norm(f"L2n{layer + 1}", X)
                wide(layer)
                dve.wait_ge(L["acc"], 4 * PAIRS * (layer + 1))
            take_mlp("L2")
            norm("L2nm", X)
            mlp("L2", 5)
            dve.wait_ge(M["L2m"]["out"], B // 2)
            for n in ("L3sel0", "L3sel1", "L3att0", "L3att1"):
                take(n)
            norm("L3n1", X)
            dve.wait_ge(rowb_in, 16)
            attention("L3")
            dve.wait_ge(A["L3"]["done"], 4)
            take_mlp("L3")
            norm("L3nm", X)
            mlp("L3", 7)

        @block.gpsimd
        def _(pool):
            def normalise(a, u, nh, keys, stride):
                pool.wait_ge(a["rc"], u + 1)
                pr = prob[:, u % 3, :].rearrange("p (h n) -> p h n", n=stride)[:, 0:nh, 0:keys]
                nc.gpsimd.tensor_tensor(pr, pr, prec[:, u % 4, 0:nh].unsqueeze(2).broadcast_to([P, nh, keys]), ALU.mult)\
                  .then_inc(a["nm"], 1)

            def zero_stacks():
                nc.gpsimd.memset(ks.rearrange("p a b -> p (a b)").bitcast(F32), 0.0).then_inc(g_setup, 1)
                nc.gpsimd.memset(fs[:, 0:4096], 0.0).then_inc(vzero, 1)

            def attention(ph):
                c, a = ATT[ph], A[ph]
                U, keys = c["units"], c["keys"]
                for e, i in att_order(ph):
                    if e == "S":
                        normalise(a, i, 4 // U, keys, keys)
                    if ph == "L0" and e == "prep" and i % STEPS == 2:
                        b = i // STEPS
                        pool.wait_ge(a["dense"], b + 1)
                        if b == 0:
                            pool.wait_ge(l0n, 1)
                        nc.gpsimd.tensor_scalar(X[:, b, :], ms[:, 0, b, :], mv[:, b, 0:1], sd[:, 3, b:b + 1], ALU.subtract, ALU.mult)\
                          .then_inc(xn_done, 1)

            def add_row(dst, name):
                nc.gpsimd.tensor_tensor(dst[:, :, :], X[:, :, :], R(name).unsqueeze(1).broadcast_to([P, B, D]), ALU.add)\
                  .then_inc(ybias, 1)

            zero_stacks()
            attention("L0")
            pool.wait_ge(fin, B)
            zero_stacks()
            add_row(XH, "L1o")
            attention("L1")
            pool.wait_ge(N["lat"]["lo"], B // 2)
            add_row(X, "L1b2")
            for layer in range(2):
                pool.wait_ge(N[f"L2n{layer + 1}"]["xh"], B)
                if layer == 1:
                    pool.wait_ge(rowb_in, 16)
                add_row(X, f"L2bo{layer + 1}")
                for u in range(8 * PAIRS):
                    normalise(L, 8 * PAIRS * layer + u, 2, P, D)
            pool.wait_ge(N["L2nm"]["xh"], B)
            add_row(X, "L2b2")
            pool.wait_ge(M["L2m"]["out"], B // 2)
            zero_stacks()
            pool.wait_ge(N["L3n1"]["xh"], B)
            add_row(X, "L3o")
            attention("L3")
            pool.wait_ge(N["L3nm"]["xh"], B)
            add_row(X, "L3b2")


def selection(ph):
    S = np.zeros((4, 4, P, P), np.float32)
    dh, heads = (8, 4) if ph == "L0" else (16, 2)
    scale = {"L0": 1.0, "L1": 1.0 / 16, "L3": 1.0 / 4}[ph]
    for g in range(4):
        for j in range(heads):
            h = 4 * j + g if ph == "L0" else 2 * g + j
            for d in range(dh):
                c = dh * h + d
                r = (P // heads) * j + d
                for part in range(3):
                    S[g, 0 if part != 1 else 1, c, r + dh * part] = scale
                    S[g, 2 if part != 2 else 3, c, r + dh * part] = 1.0
    return S.transpose(2, 0, 1, 3).reshape(P, 4 * 4 * P)


def kernel(**inputs):
    import concourse.bacc as _bacc
    from concourse.bass_utils import run_bass_kernel_spmd as _run

    g = {k: np.asarray(v) for k, v in inputs.items()}

    def tiles(w):
        return w.reshape(-1, P, w.shape[1]).transpose(1, 0, 2)

    def flat(*ws):
        return np.concatenate([w.reshape(P, -1) for w in ws], 1)

    packs = [np.concatenate([flat(*(g[f"L0_xattn_W{k}"].T for k in "qkv")), np.zeros((P, PACK - 3 * P), np.float32)], 1)]

    def add(w):
        assert w.shape == (P, 2 * PACK), w.shape
        packs.extend([w[:, :PACK], w[:, PACK:]])

    def out_rows(w):
        return w.reshape(2, 2, 4, 16, D).transpose(0, 2, 1, 3, 4).reshape(D, D)

    kv = g["L1_xattn_kv_w"].reshape(D, D, 2)
    kvb = g["L1_xattn_kv_b"].reshape(D, 2)
    add(selection("L0"))
    add(selection("L1"))
    add(flat(tiles(g["L1_xattn_q_w"]), tiles(kv[:, :, 0]), tiles(kv[:, :, 1]), tiles(out_rows(g["L1_xattn_out_w"]))))
    add(flat(tiles(g["L1_xattn_mlp_w1"])))
    add(flat(tiles(g["L1_xattn_mlp_w2"])))
    for l in (1, 2):
        for p in range(PAIRS):
            c = slice(2 * P * p, 2 * P * (p + 1))
            add(flat(*(tiles(g[f"L2_xattn_w{k}{l}"][:, c]) for k in "qkv"), tiles(g[f"L2_xattn_wo{l}"][c, :])))
    add(flat(tiles(g["L2_xattn_w_fc1"])))
    add(flat(tiles(g["L2_xattn_w_fc2"])))
    add(selection("L3"))
    add(flat(*(tiles(g[f"L3_xattn_{k}_w"]) for k in "qkv"), tiles(out_rows(g["L3_xattn_cproj_w"]))))
    add(flat(tiles(g["L3_xattn_fc_w"])))
    add(flat(tiles(g["L3_xattn_proj_w"])))

    r = np.arange(P)
    ind = [((r % 32) == 24).astype(np.float32), ((r % 64) == 48).astype(np.float32)]
    vec = {
        "ones0": ind[0], "ones1": ind[1],
        "L0q": g["L0_xattn_bq"], "L0k": g["L0_xattn_bk"], "L1q": g["L1_xattn_q_b"], "L1k": kvb[:, 0],
        "L1w": g["L1_xattn_postnorm_w"], "L1b1": g["L1_xattn_mlp_b1"],
        "L2mw": g["L2_xattn_ln_mlp_scale"], "L2mb": g["L2_xattn_ln_mlp_offset"], "L2b1": g["L2_xattn_b_fc1"],
        "L3q": g["L3_xattn_q_b"], "L3k": g["L3_xattn_k_b"], "L3lw": g["L3_xattn_ln1_w"], "L3lb": g["L3_xattn_ln1_b"],
        "L3mw": g["L3_xattn_ln2_w"], "L3mb": g["L3_xattn_ln2_b"], "L3b1": g["L3_xattn_fc_b"],
    }
    for l in (1, 2):
        vec |= {f"L2q{l}": g[f"L2_xattn_bq{l}"], f"L2k{l}": g[f"L2_xattn_bk{l}"], f"L2bk{l}": g[f"L2_xattn_bias_k{l}"],
                f"L2bv{l}": g[f"L2_xattn_bias_v{l}"], f"L2lw{l}": g[f"L2_xattn_ln{l}_scale"], f"L2lb{l}": g[f"L2_xattn_ln{l}_offset"]}
    cols = np.concatenate([vec[n].reshape(-1, P).T for n in COLS], 1)
    rowv = {"L0v": np.concatenate([g["L0_xattn_bv"], np.zeros(P, np.float32)]), "L1v": kvb[:, 1], "L1o": g["L1_xattn_out_b"],
            "L1b2": g["L1_xattn_mlp_b2"], "L2bo1": g["L2_xattn_bo1"], "L2bo2": g["L2_xattn_bo2"], "L2b2": g["L2_xattn_b_fc2"],
            "L3v": g["L3_xattn_v_b"], "L3o": g["L3_xattn_cproj_b"], "L3b2": g["L3_xattn_proj_b"]}
    rows = np.stack([rowv[n] for n in ROWS]).reshape(2, ROW_SET * D)
    l2rows = np.stack([np.stack([g[f"L2_xattn_bv{l}"].reshape(PAIRS, D), g[f"L2_xattn_bias_v{l}"].reshape(PAIRS, D)], 1)
                       for l in (1, 2)]).reshape(2 * PAIRS, 2 * D)

    arrays = {
        "x": g["x"], "ctx": g["ctx_2048"],
        "mask_t": g["mask_Bx1x2048_bf1"].reshape(1, B * D).view(np.uint8),
        "mask_s2": g["mask_BxS2_ik0"].reshape(1, B * P),
        "mask_s3": g["mask_BxS2_bf1"].reshape(1, B * P).view(np.uint8),
        "packs": np.stack(packs), "cols": cols, "rows": rows, "l2rows": l2rows,
        "inds": np.concatenate(ind).reshape(1, 2 * P), "ident": np.eye(P, dtype=np.float32),
    }
    nc = _bacc.Bacc("TRN2", target_bir_lowering=False, num_devices=1)
    sent, args = {}, []
    for name, a in arrays.items():
        a = np.ascontiguousarray(a)
        sent[f"in_{name}"] = a
        args.append(nc.dram_tensor(f"in_{name}", a.shape, mybir.dt.from_np(a.dtype), kind="ExternalInput").ap())
    args.append(nc.dram_tensor("out_0", (B, P, D), F32, kind="ExternalOutput").ap())
    build(nc, *args)
    res = _run(nc, [sent], core_ids=[0])
    return res.results[0]["out_0"]
```

```python
from contextlib import ExitStack

import numpy as np

import concourse.bass as bass
from concourse import mybir

F32 = mybir.dt.float32
F32R = mybir.dt.float32r
U8 = mybir.dt.uint8
I32 = mybir.dt.int32
ACT = mybir.ActivationFunctionType
ALU = mybir.AluOpType
AX = mybir.AxisListType

P = 128
B = 8
D = 256
KT = D // P
H = 16
DK2 = 128
PAIRS = H // 2
FF = 4 * D
FT = FF // P
PACK = 1024
MASKED = -float(2 ** 100)
Q0_SCALE = 8 ** -0.5
Q2_SCALE = DK2 ** -0.5

PACKS = ["L0w0"]
for _n in (["L0sel", "L1att", "L1sel", "L1w1_", "L1w2_", "L3sel"] + [f"L2p{i}_" for i in range(2 * PAIRS)]
           + ["L2w1_", "L2w2_", "L3att", "L3w1_", "L3w2_"]):
    PACKS += [_n + "0", _n + "1"]
PACK_AT = {n: i for i, n in enumerate(PACKS)}
PARTS = 4
HI_AT = {}
for _n in PACKS:
    if not _n.startswith(("L0w", "L0sel", "L1sel", "L3sel")):
        HI_AT[_n] = PARTS * sum(PACK_AT[m] % 2 == PACK_AT[_n] % 2 for m in HI_AT)

COLS = {}
for _n, _w in ([("ones0", 1), ("ones1", 1), ("L0q", 1), ("L0k", 1), ("L1q", 2), ("L1k", 2), ("L1w", 2), ("L1b1", 8)]
               + [(f"L2{s}{l}", w) for l in (1, 2) for s, w in (("q", 16), ("k", 16), ("bk", 16), ("bv", 16), ("lw", 2), ("lb", 2))]
               + [("L2mw", 2), ("L2mb", 2), ("L2b1", 8), ("L3q", 2), ("L3k", 2), ("L3lw", 2), ("L3lb", 2),
                  ("L3mw", 2), ("L3mb", 2), ("L3b1", 8)]):
    COLS[_n] = (sum(w for _, w in COLS.values()), _w)
NCOLS = sum(w for _, w in COLS.values())

ROWS = ["L0v", "L1v", "L1o", "L1b2", "L2bo1", "L2bo2", "L2b2", "L3v", "L3o", "L3b2"]
ROW_SET = 5

ATT = {
    "L0": dict(iters=8, keys=256, units=2, key_tiles=2, stack_a=2, stack_d=1),
    "L1": dict(iters=4, keys=256, units=2, key_tiles=2, stack_a=3, stack_d=2),
    "L3": dict(iters=4, keys=128, units=1, key_tiles=1, stack_a=2, stack_d=1),
}
STEPS = 4
T_LAG = 3
NORMS = ["ctx", "lat", "L1r", "L2n1", "L2n2", "L2nm", "L3n1", "L3nm"]


def att_order(ph):
    c = ATT[ph]
    U = c["units"]
    per_step = 2 * U
    per_it = STEPS * per_step
    total = c["iters"] * per_it
    prep = {"L0": [(1, "pq", 0)], "L1": [(0, "pq", 0), (1, "pk", 0), (2, "pk", 1)], "L3": [(0, "pq", 0), (0, "pk", 0)]}[ph]
    dense = {"L0": [(2 * 4 + 2, "dq", 0), (3 * 4 + 0, "dv", 0)],
             "L1": [(2 * 4 + 1, "dq", 0), (2 * 4 + 2, "dk", 0), (2 * 4 + 3, "dk", 1), (3 * 4 + 3, "dv", 0), (4 * 4 + 3, "dv", 1)],
             "L3": [(2 * 2 + 1, "dq", 0), (2 * 2 + 1, "dk", 0), (3 * 2 + 1, "dv", 0)]}[ph]
    weights = {"L0": {40: ["L1att0"], 48: ["L1att1"]}, "L1": {total + 1: ["L1w1_0"], total + 2: ["L1w1_1"]},
               "L3": {total + 1: ["L3w1_0"], total + 2: ["L3w1_1"]}}[ph]
    for _, e, k in dense:
        yield (e, 0, k)
    for _, e, k in prep:
        yield (e, 0, k)
    for u in range(total + T_LAG + 2):
        s, r = divmod(u, per_step)
        if u < total:
            yield ("S", u)
        if 0 <= u - T_LAG < total:
            yield ("T", u - T_LAG)
        if u < total:
            for at, e, k in prep:
                if r == at and s + 1 < c["iters"] * STEPS:
                    yield (e, s + 1, k)
            for at, e, k in dense:
                it, o = divmod(u - at, per_it)
                if o == 0 and it >= 0 and it + 1 < c["iters"]:
                    yield (e, it + 1, k)
        for name in weights.get(u, ()):
            yield ("w", name)
        w = u - T_LAG - 1
        if w >= 0 and w < total and w % U == U - 1:
            yield ("PV", w // U)
            if w % per_it >= per_it - 2 * U + U - 1:
                yield ("OUT", w // U // (2 * STEPS), w // U % 2)
        if w >= 1 and w % per_it == 0:
            yield ("WO", w // per_it - 1)


def late(order, kinds):
    order = list(order)
    scores = [n for n, e in enumerate(order) if e[0] == "S"]
    kept = []
    for n, e in enumerate(order):
        if e[0] in kinds and scores[0] < n < scores[-1]:
            kept.append(e)
            continue
        yield e
        if e[0] == "S":
            yield from kept
            kept = []


def wide_order():
    pairs = 2 * PAIRS

    def start(p):
        for hd in range(2):
            for ch in range(2):
                yield ("k", p, hd, ch)
        for k in range(4):
            yield ("v", p, k)
        yield ("norm", p // PAIRS)
        for hd in range(2):
            for ch in range(2):
                yield ("q", p, hd, ch)

    yield from start(0)
    for p in range(pairs):
        last = p % PAIRS == PAIRS - 1
        first = p % PAIRS == 0
        for u in range(12 if last else 8):
            g = 8 * p + u
            if u < 8:
                yield ("S", g)
            if 0 <= u - 1 < 8 or u == 0 and not first:
                yield ("T", g - 1)
            if u < 8:
                yield ("R", g)
            if u < 4 and not first:
                yield ("WO", p - 1, u)
            if u >= 8:
                yield ("WO", p, u - 8)
            if not last and u >= 4:
                yield ("v", p + 1, u - 4)
            if u < 10 and (u >= 2 or not first):
                yield ("PV", g - 2)
            if not last and u < 8:
                yield ("qk"[u // 2 % 2], p + 1, u // 4, u % 2)
            if u < 2 and p > 0:
                yield ("w", f"L2p{p}_1", 2 + u, 1)
            if u in (2, 3) and p + 1 < pairs:
                yield ("w", f"L2p{p + 1}_1", u - 2, 1)
            if 4 <= u < 8 and p + 2 < pairs:
                yield ("w", f"L2p{p + 2}_0", u - 4, 1)
            if 4 <= u < 8 and p == pairs - 1:
                yield ("w", f"L2w1_{u // 6}", 2 * (u % 2), 2)
        if last and not p == pairs - 1:
            yield from start(p + 1)


QK_AT = {}
for _n, _e in enumerate(e for e in wide_order() if e[0] in ("q", "k")):
    QK_AT[_e] = _n + 1


def mlp_order(name):
    for c in range(B // 2):
        for f2 in range(FT // 2):
            yield ("up", c, f2)
            if c == 0 and f2 in (0, 1):
                yield ("w", f"{name}w2_{f2}", 0, PARTS)
            if name == "L1" and c == 1 and f2 in (0, 2):
                yield ("w", f"L3sel{f2 // 2}", 0, PARTS)
        if c == B // 2 - 1:
            if name == "L1":
                yield ("w", "L2p0_0", 0, PARTS)
                yield ("w", "L2p0_1", 0, 2)
                yield ("w", "L2p0_1", 2, 2)
            if name == "L2":
                yield ("w", "L3att0", 0, PARTS)
                yield ("w", "L3att1", 0, PARTS)
        yield ("down", c)


def build(nc, x, ctx_in, mask_t, mask_s2, mask_s3, packs, cols, rows, l2rows, inds, ident_in, out):
    stack = ExitStack()
    with stack:
        def sb(name, shape, dt=F32):
            return stack.enter_context(nc.sbuf_tensor(name, shape, dt))

        def sem(name):
            return stack.enter_context(nc.semaphore(name))

        ps = stack.enter_context(nc.psum_tensor("ps", [P, 8, 512], F32))
        S_BANK, T_BANK, O_BANK, J_BANK = 0, 2, 4, 6
        X = sb("X", [P, B, D])
        XH = sb("XH", [P, B, D])
        wraw = sb("wraw", [P, 2, PACK])
        ident = sb("ident", [P, P])
        col = sb("col", [P, NCOLS])
        row = sb("row", [P, ROW_SET, D])
        prob = sb("prob", [P, 3, 512])
        probT = sb("probT", [P, 3, 512])
        nmax = sb("nmax", [P, 4, 4])
        psums = sb("psums", [P, 4, 4])
        prec = sb("prec", [P, 4, 4])
        st6 = sb("st6", [P, B, 6])
        mv = sb("mv", [P, B, 2])
        sd = sb("sd", [P, 6, B])
        eps = sb("eps", [P, 2])
        q0b = sb("q0b", [P, 1])
        l2q = sb("l2q", [P, 2, H])
        bvr = sb("bvr", [P, 2, 2, D])
        ct = [sb(f"ct{i}", [P, KT, B, P], F32R) for i in range(2)]
        ht = [sb(f"ht{i}", [P, KT, B, P], F32R) for i in range(2)]
        sel = sb("sel", [P, 16, P], F32R)
        indr = sb("indr", [1, 2, P], F32R)
        mb13 = sb("mb13", [1, B * P], F32R)
        mt8 = sb("mt8", [P, B, D], U8)
        mraw3 = sb("mraw3", [1, B * P], U8)
        fs = sb("fs", [P, 10264])
        rs = sb("rs", [P, 13312], F32R)

        def carve(t, at, shape):
            n = int(np.prod(shape))
            names = "abcdef"[:len(shape)]
            kw = {c: k for c, k in zip(names[1:], shape[1:])}
            v = t[:, at:at + n]
            if len(shape) > 1:
                v = v.rearrange(f"p ({' '.join(names)}) -> p {' '.join(names)}", **kw)
            return v, at + n

        def carve2(t, at, shape):
            h, at = carve(t, at, shape)
            l, at = carve(t, at, shape)
            return [h, l], at

        A0, A1, A2 = 0, 4096, 8192
        ksA, _ = carve(rs, A0, [2, 2048])
        ksB, _ = carve(rs, A1, [2, 2048])
        awA, _ = carve2(rs, A1, [4, KT, D])
        awB, _ = carve2(rs, A0, [4, KT, D])
        ks = {"L0": ksA, "L1": ksA, "L3": ksB}
        aw = {"L1": awA, "L3": awB}
        qs, o = carve(rs, A2, [2, 512])
        dq, o = carve2(rs, o, [2, D])
        dk, o = carve2(rs, o, [2, 512])
        uu, o = carve2(rs, o, [2, 2, P])
        assert o <= 13312
        mb0 = ht[1][0:1].rearrange("p f b n -> p (f b n)")
        vt, o = carve(fs, 0, [2, 2, 2, H, 32])
        ms, o = carve(fs, o, [2, B, D])
        xq, o = carve(fs, o, [D])
        w0, o = carve(fs, o, [3, P])
        msq, o = carve(fs, o, [D])
        assert o <= 10264
        pw = [carve2(rs, A0, [4, 512])[0], carve2(rs, A1, [4, 512])[0]]
        cc, o = carve2(rs, A2, [2, B, P])
        assert o <= 13312
        qT, o = carve(fs, 0, [3, B, P])
        kT, o = carve(fs, o, [3, B, P + 1])
        v2, o = carve(fs, o, [2, B, 2, P])
        assert o <= 10264
        mw1 = {m: carve2(rs, A1 if m == "L3" else A0, [KT, FF])[0] for m in ("L1", "L2", "L3")}
        mw2 = {m: carve2(rs, A0 if m == "L3" else A1, [FT, D])[0] for m in ("L1", "L2", "L3")}
        gg, o = carve2(rs, A2, [FT, D])
        assert o <= 13312
        gf, _ = carve(fs, 0, [2, 512])

        c_in, x_in = sem("constants_loaded"), sem("x_and_ctx_loaded")
        rowb_in = sem("second_rows_loaded")
        l_in = [sem(f"pack_loaded{i}") for i in range(2)]
        bv_in = [sem(f"l2_rows_loaded{i}") for i in range(2)]
        w_hi = [sem(f"weight_hi_written{i}") for i in range(2)]
        w_lo = [sem(f"weight_pack_taken{i}") for i in range(2)]
        w_v = sem("l2_v_weights_split")
        jm = sem("general_bank_filled")
        a_setup, g_setup = sem("scalar_setup"), sem("off_diagonal_zeroed")
        eps_ok = sem("eps_set")
        vzero = sem("values_zeroed")
        l0stat, l0sq, l0n = sem("l0_stats"), sem("l0_sqrt"), sem("l0_norm_factors")
        l0mul, g_link = sem("l0_x_times_deviation"), sem("pool_chain")
        xn_done = sem("l0_x_normalised")
        l0var, l0dev, fin = sem("l0_variance"), sem("l0_deviation"), sem("l0_result")
        ybias = sem("residual_biased")
        dch = sem("vector_chain")
        out_done = sem("output_written")
        A = {ph: {n: sem(f"{ph}_{n}") for n in ["hi", "dense", "stA", "stD", "vals", "sm", "mx", "ex", "rc", "nm", "tm", "teA", "teD",
                                                "pm", "oeA", "mask"] + (["xq"] if ph == "L0" else ["oeD", "done"])} for ph in ATT}
        L = {n: sem(f"L2_{n}") for n in ("qk", "v", "bv", "sm", "mx", "ex", "rc", "nm", "tm", "teA", "teD", "pm", "ch", "cl", "acc")}
        M = {m: {n: sem(f"{m}_{n}") for n in ("gelu", "lo", "out")} for m in ("L1m", "L2m", "L3m")}
        N = {n: {k: sem(f"{n}_{k}") for k in (["hi", "lo"] if n in ("ctx", "lat") else ["stat", "sq", "r", "xh", "xp", "a", "lo"])}
             for n in NORMS}

        block = stack.enter_context(nc.Block())

        def C(name, i=0):
            return col[:, COLS[name][0] + i:COLS[name][0] + i + 1]

        def R(name):
            return row[:, ROWS.index(name) % ROW_SET, :]

        def taken(eng, name):
            n = PACK_AT[name]
            eng.wait_ge(w_lo[n % 2], n // 2 + 1)

        def loaded(eng, name):
            n = PACK_AT[name]
            eng.wait_ge(l_in[n % 2], 16 * (n // 2 + 1))

        def pack_dst(name, part, parts):
            half = int(name[-1])
            base = name[:-1]
            at = half * PACK + part * (PACK // PARTS)
            cut = slice(at, at + parts * (PACK // PARTS))
            if base == "L0w":
                return [w0.rearrange("p a b -> p (a b)")]
            if base.endswith("sel"):
                return [sel[:, :, :].rearrange("p a b -> p (a b)")[:, cut]]
            if base.endswith("att"):
                return [t.rearrange("p a b c -> p (a b c)")[:, cut] for t in aw[base[:2]]]
            if base[2] == "p":
                return [t.rearrange("p a b -> p (a b)")[:, cut] for t in pw[int(base[3:-1]) % 2]]
            return [t.rearrange("p a b -> p (a b)")[:, cut] for t in (mw1 if "w1" in base else mw2)[base[:2]]]

        @block.sync
        def _(sp):
            sp.dma_start(X[:, :, :], x.rearrange("b p d -> p b d")).then_inc(x_in, 16)
            sp.dma_start(XH[:, :, :], ctx_in.rearrange("b p d -> p b d")).then_inc(x_in, 16)
            sp.dma_start(ident[:, :], ident_in).then_inc(c_in, 16)
            sp.dma_start(col[:, :], cols).then_inc(c_in, 16)
            sp.dma_start(row[:, :, :].rearrange("p r d -> p (r d)"), rows[0].partition_broadcast(P)).then_inc(c_in, 16)
            sp.dma_start(prob[0:1, 2, 0:2 * P], inds).then_inc(c_in, 16)
            sp.dma_start(probT[0:1, :, :].bitcast(I32).rearrange("p a b -> p (a b)")[:, 0:B * P], mask_s2).then_inc(c_in, 16)
            sp.dma_start(mraw3[:, :], mask_s3).then_inc(c_in, 16)
            sp.dma_start(mt8[:, :, :].rearrange("p b d -> p (b d)"), mask_t[0].partition_broadcast(P)).then_inc(c_in, 16)
            for n, name in enumerate(PACKS):
                if n >= 2:
                    sp.wait_ge(w_lo[n % 2], n // 2)
                sp.dma_start(wraw[:, n % 2, :], packs[n]).then_inc(l_in[n % 2], 16)
                if name[:3] == "L2p" and name[-1] == "0":
                    i = int(name[3:-2])
                    if i >= 2:
                        sp.wait_ge(L["v"], 4 * (i - 1))
                    sp.dma_start(bvr[:, i % 2, :, :].rearrange("p a d -> p (a d)"), l2rows[i].partition_broadcast(P))\
                      .then_inc(bv_in[i % 2], 16)
                if name == "L2p7_1":
                    sp.wait_ge(ybias, 3)
                    sp.dma_start(row[:, :, :].rearrange("p r d -> p (r d)"), rows[1].partition_broadcast(P)).then_inc(rowb_in, 16)
            sp.wait_ge(M["L3m"]["out"], B // 2)
            sp.dma_start(out.rearrange("b p d -> p b d"), X[:, :, :]).then_inc(out_done, 16)
            sp.wait_ge(out_done, 16)

        @block.tensor
        def _(pe):
            filled = [0]
            freed_by = [[], []]

            def j_bank():
                i = filled[0] % 2
                for s, v in freed_by[i]:
                    pe.wait_ge(s, v)
                return ps[:, J_BANK + i, :]

            def j_full(last, *frees):
                last.then_inc(jm, 1)
                freed_by[filled[0] % 2] = frees
                filled[0] += 1

            def three(dst, w, m, start, stop):
                nc.tensor.matmul(dst, w[0], m[1], start=start, stop=False)
                nc.tensor.matmul(dst, w[1], m[0], start=False, stop=False)
                return nc.tensor.matmul(dst, w[0], m[0], start=False, stop=stop)

            def both(f):
                return [f(0), f(1)]

            def norm(name, src, ready):
                n = N[name]
                for k in range(B // 2):
                    bank = j_bank()
                    if name == "ctx":
                        pe.wait_ge(x_in, 32)
                        pe.wait_ge(c_in, 16 * 7)
                    else:
                        for s, v in ready(k):
                            pe.wait_ge(s, v)
                    for q in range(2):
                        for f in range(KT):
                            last = nc.tensor.transpose(bank[:, (2 * q + f) * P:(2 * q + f + 1) * P],
                                                       src[:, 2 * k + q, f * P:(f + 1) * P], ident[:, :])
                    j_full(last, (n["lo" if name in ("ctx", "lat") else "a"], k + 1))

            def dense(ph, e, it, k, a):
                if ph == "L0":
                    if it == 0 and e == "dq":
                        taken(pe, "L0w0")
                    bank = j_bank()
                    if e == "dq":
                        nc.tensor.matmul(bank[:, 0:D], w0[:, 0, :], X[:, it, :], start=True, stop=True)
                        j_full(nc.tensor.matmul(bank[:, D:2 * D], w0[:, 1, :], XH[:, it, :], start=True, stop=True), (a["dense"], it + 1))
                        return
                    for t in range(2):
                        last = nc.tensor.matmul(bank[:, t * P:(t + 1) * P], XH[:, it, t * P:(t + 1) * P], w0[:, 2, :],
                                                start=True, stop=True)
                    j_full(last, (a["vals"], it + 1))
                    return
                if e == "dq":
                    if it == 0:
                        taken(pe, ph + "att0")
                        taken(pe, ph + "att1")
                    pe.wait_ge(N["lat" if ph == "L1" else "L3n1"]["lo"], it + 1)
                bb = slice(2 * it, 2 * it + 2)
                W = lambda kind, f, t: both(lambda i: aw[ph][i][:, kind, f, t * P:(t + 1) * P])
                n_hi = 3 if ph == "L1" else 2
                bank = j_bank()
                for s in range(2):
                    dst = bank[:, s * D:(s + 1) * D]
                    for f in range(KT):
                        if e == "dq":
                            last = three(dst, W(0, f, s), both(lambda i: ht[i][:, f, bb, :]), f == 0, f == KT - 1)
                        elif e == "dk" and ph == "L1":
                            src = (ct, ht)[s]
                            last = three(dst, W(1, f, k), both(lambda i: src[i][:, f, bb, :]), f == 0, f == KT - 1)
                        elif e == "dk":
                            last = three(dst, W(1, f, s), both(lambda i: ct[i][:, f, bb, :]), f == 0, f == KT - 1)
                        else:
                            src, b = ((ct, ht)[s], 2 * it + k) if ph == "L1" else (ct, 2 * it + s)
                            last = three(dst, both(lambda i: src[i][:, f, b, :]), both(lambda i: aw[ph][i][:, 2, f, :]), f == 0, f == KT - 1)
                if e == "dv":
                    j_full(last, (a["vals"], (2 * it + k if ph == "L1" else it) + 1))
                else:
                    n = n_hi * it + (1 if e == "dq" else 2 + k)
                    j_full(last, (a["hi"], n), (a["dense"], n))

            def prep(ph, e, s, gi, a):
                it, m = divmod(s, STEPS)
                if s == 0 and e == "pq":
                    pe.wait_ge(a["mask"], 1)
                    taken(pe, ph + "sel0")
                    taken(pe, ph + "sel1")
                pe.wait_ge(a["dense"], {"L0": it + 1, "L1": 3 * it + (1 if e == "pq" else 2 + m // 2),
                                        "L3": 2 * it + (1 if e == "pq" else 2)}[ph])
                nA, nD = ATT[ph]["stack_a"], ATT[ph]["stack_d"]
                bank = j_bank()
                if ph == "L0":
                    for i in range(2):
                        nc.tensor.matmul(bank[:, 0:D], sel[:, 4 * m + i, :], dq[i][:, 0, :], start=i == 0, stop=i == 1)
                    for i in range(2):
                        nc.tensor.matmul(bank[:, D:2 * D], sel[:, 4 * m + 2 + i, :], dk[i][:, 0, 0:D], start=i == 0, stop=False)
                    j_full(nc.tensor.matmul(bank[:, D:2 * D], indr[:, 0, :], mb0[:, it * D:(it + 1) * D], start=False, stop=True),
                           (a["stA"], nA * (s + 1)), (a["stD"], s + 1))
                    return
                if e == "pq":
                    for gi in range(2):
                        g = 2 * m + gi
                        for i in range(2):
                            last = nc.tensor.matmul(bank[:, gi * D:(gi + 1) * D], sel[:, 4 * (g % 4) + i, :], dq[i][:, g // 4, :],
                                                    start=i == 0, stop=i == 1)
                    j_full(last, (a["stA"], nA * s + 1))
                    return
                for g in [2 * m + gi] if ph == "L1" else [2 * m, 2 * m + 1]:
                    n, dst = (512, bank) if ph == "L1" else (D, bank[:, (g % 2) * D:(g % 2 + 1) * D])
                    for i in range(2):
                        nc.tensor.matmul(dst, sel[:, 4 * (g % 4) + 2 + i, :], dk[i][:, g // 4, 0:n], start=i == 0, stop=False,
                                         skip_group_check=True)
                    last = nc.tensor.matmul(dst[:, 0:D], indr[:, 1, :], mb13[:, 2 * it * P:(2 * it + 2) * P],
                                            start=False, stop=True, skip_group_check=True)
                j_full(last, (a["stA"], nA * s + 2 + gi), (a["stD"], nD * s + 1 + gi))

            def attention(ph):
                c, a = ATT[ph], A[ph]
                U, KTL = c["units"], c["key_tiles"]
                nh = 4 // U
                for e, i, *k in att_order(ph):
                    if e in ("dq", "dk", "dv"):
                        dense(ph, e, i, k[0], a)
                    elif e in ("pq", "pk"):
                        prep(ph, e, i, k[0], a)
                    elif e == "S":
                        s, r = divmod(i, 2 * U)
                        im, k = divmod(r, U)
                        if r == 0:
                            pe.wait_ge(a["stA"], c["stack_a"] * (s + 1))
                            pe.wait_ge(a["stD"], c["stack_d"] * (s + 1))
                        if i >= 2:
                            pe.wait_ge(a["ex"], i - 1)
                        bank = ps[:, S_BANK + i % 2, :]
                        if ph == "L0":
                            last = nc.tensor.matmul(bank, qs[:, s % 2, im * P:(im + 1) * P], ks[ph][:, s % 2, k * 512:(k + 1) * 512],
                                                    start=True, stop=True)
                        elif ph == "L1":
                            last = nc.tensor.matmul(bank, qs[:, s % 2, k * D + im * P:k * D + (im + 1) * P],
                                                    ks[ph][:, s % 2, (2 * k + im) * 512:(2 * k + im + 1) * 512], start=True, stop=True)
                        else:
                            for g in range(2):
                                last = nc.tensor.matmul(bank[:, g * D:(g + 1) * D], qs[:, s % 2, g * D + im * P:g * D + (im + 1) * P],
                                                        ks[ph][:, s % 2, (2 * g + im) * D:(2 * g + im + 1) * D], start=True, stop=True)
                        last.then_inc(a["sm"], 1)
                    elif e == "T":
                        pe.wait_ge(a["nm"], i + 1)
                        if i >= 2:
                            pe.wait_ge(a["teD" if i % 2 else "teA"], i // 2)
                        for k in range(4):
                            last = nc.tensor.transpose(ps[:, T_BANK + i % 2, k * P:(k + 1) * P], prob[:, i % 3, k * P:(k + 1) * P],
                                                       ident[:, :])
                        last.then_inc(a["tm"], 1)
                    elif e == "PV":
                        it, r = divmod(i, 2 * STEPS)
                        m, im = divmod(r, 2)
                        u1 = (i + 1) * U - 1
                        pe.wait_ge(a["teA"], u1 // 2 + 1)
                        if u1 >= 1:
                            pe.wait_ge(a["teD"], (u1 + 1) // 2)
                        if m == 0:
                            pe.wait_ge(a["vals"], 2 * it + im + 1 if ph == "L1" else it + 1)
                            if it > 0:
                                pe.wait_ge(a["oeA" if ph == "L0" else "oeD"], 2 * (it - 1) + im + 1)
                        bank = ps[:, O_BANK + im, :]
                        for st in range(2 if ph == "L0" else 1):
                            for t in range(KTL):
                                for q in range(4):
                                    slot = (i * U + q // nh) % 3
                                    c0 = ((q % nh) * KTL + t) * P
                                    if ph == "L0":
                                        v = vt[:, it % 2, st, t, 4 * q + m, :]
                                        dst = bank[32 * q:32 * q + 32, st * P:(st + 1) * P]
                                        first, stop = (m == 0 and t == 0 and st == 0), (m == 3 and t == 1)
                                    else:
                                        v = vt[:, it % 2, im, t, 4 * m + q, :]
                                        dst = bank[32 * q:32 * q + 32, (m // 2) * P:(m // 2 + 1) * P]
                                        first, stop = (m % 2 == 0 and t == 0), (m % 2 == 1 and t == KTL - 1)
                                    last = nc.tensor.matmul(dst, v, probT[:, slot, c0:c0 + P], start=first, stop=stop,
                                                            skip_group_check=True)
                        last.then_inc(a["pm"], 1)
                    elif e == "WO" and ph != "L0":
                        pe.wait_ge(a["oeD"], 2 * (i + 1))
                        bank = j_bank()
                        for im in range(2):
                            for t in range(2):
                                last = three(bank[:, im * D:(im + 1) * D], both(lambda k: uu[k][:, im, t, :]),
                                             both(lambda k: aw[ph][k][:, 3, t, :]), t == 0, t == 1)
                        j_full(last, (a["done"], i + 1))

            def wide():
                for e in wide_order():
                    if e[0] == "norm":
                        norm(f"L2n{e[1] + 1}", XH, normed(f"L2n{e[1] + 1}"))
                    elif e[0] in ("q", "k"):
                        kind, p, hd, ch = e
                        if hd == 0 and ch == 0:
                            taken(pe, f"L2p{p}_0")
                        if kind == "q" and p % PAIRS == 0:
                            pe.wait_ge(N[f"L2n{p // PAIRS + 1}"]["lo"], 2 * ch + 2)
                        src, kd = (ct, 1) if kind == "k" else (ht, 0)
                        bank = j_bank()
                        for f in range(KT):
                            last = three(bank, both(lambda i: pw[p % 2][i][:, kd, f * D + hd * P:f * D + (hd + 1) * P]),
                                         both(lambda i: src[i][:, f, 4 * ch:4 * ch + 4, :]), f == 0, f == KT - 1)
                        j_full(last, (L["qk"], QK_AT[e]))
                    elif e[0] == "v":
                        _, p, k = e
                        pe.wait_ge(w_v, p + 1)
                        bank = j_bank()
                        for b in range(2):
                            for f in range(KT):
                                last = three(bank[:, b * D:(b + 1) * D], both(lambda i: ct[i][:, f, 2 * k + b, :]),
                                             both(lambda i: pw[p % 2][i][:, 2, f * D:(f + 1) * D]), f == 0, f == KT - 1)
                        j_full(last, (L["v"], 4 * p + k + 1))
                    elif e[0] == "S":
                        g = e[1]
                        p, r = divmod(g, 8)
                        hd, b2 = divmod(r, 4)
                        hh = 2 * p + hd
                        pe.wait_ge(L["qk"], max(QK_AT["q", p, hd, 1], QK_AT["k", p, hd, 1]))
                        if g >= 2:
                            pe.wait_ge(L["ex"], g - 1)
                        for b in range(2):
                            last = nc.tensor.matmul(ps[:, S_BANK + g % 2, b * D:b * D + P + 1], qT[:, hh % 3, 2 * b2 + b, :],
                                                    kT[:, hh % 3, 2 * b2 + b, :], start=True, stop=True)
                        last.then_inc(L["sm"], 1)
                    elif e[0] == "T":
                        g = e[1]
                        pe.wait_ge(L["nm"], g + 1)
                        if g >= 2:
                            pe.wait_ge(L["teD" if g % 2 else "teA"], g // 2)
                        for b in range(2):
                            last = nc.tensor.transpose(ps[:, T_BANK + g % 2, b * P:(b + 1) * P], prob[:, g % 3, b * D:b * D + P],
                                                       ident[:, :])
                        last.then_inc(L["tm"], 1)
                    elif e[0] == "PV":
                        g = e[1]
                        p, r = divmod(g, 8)
                        hd, b2 = divmod(r, 4)
                        pe.wait_ge(L["teD" if g % 2 else "teA"], g // 2 + 1)
                        if r == 0:
                            pe.wait_ge(L["v"], 4 * (p + 1))
                        if g >= 2:
                            pe.wait_ge(L["cl"], g - 1)
                        for b in range(2):
                            last = nc.tensor.matmul(ps[:, O_BANK + g % 2, b * P:(b + 1) * P], v2[:, p % 2, 2 * b2 + b, hd, :],
                                                    probT[:, g % 3, b * P:(b + 1) * P], start=True, stop=True)
                        last.then_inc(L["pm"], 1)
                    elif e[0] == "WO":
                        _, p, b2 = e
                        pe.wait_ge(L["cl"], 8 * p + 4 + b2 + 1)
                        if b2 == 0:
                            taken(pe, f"L2p{p}_1")
                        bank = j_bank()
                        for b in range(2):
                            for hd in range(2):
                                last = three(bank[:, b * D:(b + 1) * D], both(lambda i: cc[i][:, hd, 2 * b2 + b, :]),
                                             both(lambda i: pw[p % 2][i][:, 3, hd * D:(hd + 1) * D]), hd == 0, hd == 1)
                        j_full(last, (L["acc"], 4 * p + b2 + 1))

            def mlp(name, nrm):
                m = M[name + "m"]
                for e in mlp_order(name):
                    if e[0] == "w":
                        continue
                    if e[0] == "up":
                        _, c, f2 = e
                        if c == 0 and f2 == 0:
                            taken(pe, name + "w1_0")
                            taken(pe, name + "w1_1")
                        pe.wait_ge(nrm["lo"], c + 1)
                        bank = j_bank()
                        for fi in range(2):
                            f = 2 * f2 + fi
                            for k in range(KT):
                                last = three(bank[:, fi * D:(fi + 1) * D], both(lambda i: mw1[name][i][:, k, f * P:(f + 1) * P]),
                                             both(lambda i: ht[i][:, k, 2 * c:2 * c + 2, :]), k == 0, k == KT - 1)
                        j_full(last, (m["gelu"], (FT // 2) * c + f2 + 1))
                    else:
                        c = e[1]
                        if c == 0:
                            taken(pe, name + "w2_0")
                            taken(pe, name + "w2_1")
                        pe.wait_ge(m["lo"], (FT // 2) * (c + 1))
                        bank = j_bank()
                        for b in range(2):
                            for f in range(FT):
                                last = three(bank[:, b * D:(b + 1) * D], both(lambda i: gg[i][:, f, b * P:(b + 1) * P]),
                                             both(lambda i: mw2[name][i][:, f, :]), f == 0, f == FT - 1)
                        j_full(last, (m["out"], c + 1))

            def normed(name):
                return lambda k: ((N[name]["xh"], k + 1), (N[name]["xp"], k + 1))

            norm("ctx", XH, None)
            attention("L0")
            norm("lat", X, lambda k: ((fin, 2 * k + 2),))
            attention("L1")
            norm("L1r", XH, normed("L1r"))
            mlp("L1", N["L1r"])
            wide()
            norm("L2nm", XH, normed("L2nm"))
            mlp("L2", N["L2nm"])
            norm("L3n1", XH, normed("L3n1"))
            attention("L3")
            norm("L3nm", XH, normed("L3nm"))
            mlp("L3", N["L3nm"])

        @block.scalar
        def _(act):
            taken = [0]

            def j_take():
                j = taken[0]
                taken[0] += 1
                act.wait_ge(jm, j + 1)
                return ps[:, J_BANK + j % 2, :]

            def j_skip():
                taken[0] += 1

            def take(name, part=0, parts=PARTS):
                if name not in HI_AT:
                    return
                loaded(act, name)
                n = PACK_AT[name]
                at = part * (PACK // PARTS)
                nc.scalar.copy(pack_dst(name, part, parts)[0], wraw[:, n % 2, at:at + parts * (PACK // PARTS)])\
                  .then_inc(w_hi[n % 2], parts)

            def norm(name, affine):
                n = N[name]
                if affine:
                    act.wait_ge(n["stat"], 1)
                    nc.scalar.activation(sd[:, 1, :], sd[:, 0, :], ACT.Sqrt,
                                         bias=eps[:, 1:2] if name == "L1r" else eps[:, 0:1]).then_inc(n["sq"], 1)
                for k in range(B // 2):
                    src = j_take().rearrange("p (q f n) -> p q f n", q=2, f=KT)
                    for f in range(KT):
                        if not affine:
                            dst = (ct if name == "ctx" else ht)[0]
                            last = nc.scalar.copy(dst[:, f, 2 * k:2 * k + 2, :], src[:, :, f, :])
                            continue
                        if k >= 3 and f == 0:
                            act.wait_ge(n["lo"], k - 2)
                        dst = probT[:, k % 3, f * D:(f + 1) * D].rearrange("p (q n) -> p q n", q=2)
                        if affine[1]:
                            last = nc.scalar.activation(dst, src[:, :, f, :], ACT.Identity, scale=C(affine[0], f), bias=C(affine[1], f))
                        else:
                            last = nc.scalar.mul(dst, src[:, :, f, :], C(affine[0], f))
                    last.then_inc(n["a" if affine else "hi"], 1)

            def attention(ph):
                c, a = ATT[ph], A[ph]
                U, keys = c["units"], c["keys"]
                nh = 4 // U
                for e, i, *k in att_order(ph):
                    if e == "dq" and ph == "L0":
                        bank = j_take()
                        if i > 0:
                            act.wait_ge(a["dense"], i)
                        nc.scalar.activation(xq, bank[:, 0:D], ACT.Identity, bias=q0b[:, :], scale=Q0_SCALE).then_inc(a["xq"], 1)
                        nc.scalar.activation(dk[0][:, 0, 0:D], bank[:, D:2 * D], ACT.Identity, bias=C("L0k")).then_inc(a["hi"], 1)
                    elif e == "w":
                        take(i)
                    elif e == "dv" or e == "WO" and ph != "L0":
                        j_skip()
                    elif e == "dk" and ph == "L1":
                        nc.scalar.activation(dk[0][:, k[0], :], j_take(), ACT.Identity, bias=C("L1k", k[0])).then_inc(a["hi"], 1)
                    elif e in ("dq", "dk"):
                        bank = j_take()
                        dst = (dq if e == "dq" else dk)[0]
                        for t in range(2):
                            last = nc.scalar.activation(dst[:, t, 0:D], bank[:, t * D:(t + 1) * D], ACT.Identity, bias=C(ph + e[1], t))
                        last.then_inc(a["hi"], 1)
                    elif e == "pq":
                        if i >= 2:
                            act.wait_ge(a["sm"], 2 * U * (i - 1))
                        bank = j_take()
                        if ph == "L0":
                            if i < 2:
                                act.wait_ge(g_setup, 1)
                            nc.scalar.activation(qs[:, i % 2, 0:D], bank[:, 0:D], ACT.Identity, bias=C("ones0")).then_inc(a["stA"], 1)
                            for q in range(2):
                                last = nc.scalar.copy(ks[ph][32 * q:32 * q + 32, i % 2, q * D:(q + 1) * D], bank[32 * q:32 * q + 32, D:2 * D])
                            last.then_inc(a["stA"], 1)
                        else:
                            nc.scalar.activation(qs[:, i % 2, :], bank, ACT.Identity, bias=C("ones1")).then_inc(a["stA"], 1)
                    elif e == "pk":
                        if i >= 2:
                            act.wait_ge(a["sm"], 2 * U * (i - 1))
                        else:
                            act.wait_ge(g_setup, {"L1": 2, "L3": 3}[ph])
                        bank = j_take()
                        if ph == "L1":
                            src = bank[0:64, :].rearrange("p (s m n) -> p m s n", s=2, m=2)
                            dst = ks[ph][0:64, i % 2, k[0] * 1024:(k[0] + 1) * 1024].rearrange("p (m h s n) -> p m h s n", m=2, h=2, s=2)
                            nc.scalar.copy(dst[:, :, 0, :, :], src).then_inc(a["stA"], 1)
                        else:
                            for g in range(2):
                                src = bank[0:64, g * D:(g + 1) * D].rearrange("p (m n) -> p m n", m=2)
                                dst = ks[ph][0:64, i % 2, g * 512:(g + 1) * 512].rearrange("p (m h n) -> p m h n", m=2, h=2)
                                last = nc.scalar.copy(dst[:, :, 0, :], src)
                            last.then_inc(a["stA"], 1)
                    elif e == "S":
                        act.wait_ge(a["mx"], i + 1)
                        if i >= 3:
                            act.wait_ge(a["tm"], i - 2)
                        for h in range(nh):
                            last = nc.scalar.activation(prob[:, i % 3, h * keys:(h + 1) * keys],
                                                        ps[:, S_BANK + i % 2, h * keys:(h + 1) * keys], ACT.Exp,
                                                        bias=nmax[:, i % 4, h:h + 1], accum_out=psums[:, i % 4, h:h + 1])
                        last.then_inc(a["ex"], 1)
                    elif e == "T":
                        if i % 2 == 0:
                            act.wait_ge(a["tm"], i + 1)
                            if i >= 3:
                                act.wait_ge(a["pm"], (i - 3) // U + 1)
                            nc.scalar.copy(probT[:, i % 3, :], ps[:, T_BANK, :]).then_inc(a["teA"], 1)
                    elif e == "OUT":
                        im = k[0]
                        act.wait_ge(a["pm"], 2 * STEPS * (i + 1) - 1 + im)
                        src = ps[:, O_BANK + im, 0:D].rearrange("p (t n) -> p t n", t=2)
                        if ph == "L0":
                            if im == 0:
                                act.wait_ge(xn_done, i + 1)
                            nc.scalar.copy(ms[:, :, i, im * P:(im + 1) * P], src).then_inc(a["oeA"], 1)
                        else:
                            if i > 0:
                                act.wait_ge(a["done"], i)
                            nc.scalar.copy(uu[0][:, im, :, :], src).then_inc(a["oeA"], 1)

            def wide():
                for e in wide_order():
                    if e[0] == "norm":
                        l = e[1] + 1
                        norm(f"L2n{l}", (f"L2lw{l}", f"L2lb{l}"))
                    elif e[0] in ("q", "k"):
                        kind, p, hd, ch = e
                        layer, hh = p // PAIRS, 2 * p + hd
                        h = hh % H
                        bank = j_take()
                        if hh >= 3:
                            act.wait_ge(L["sm"], 4 * (hh - 2))
                        src = bank.rearrange("p (b n) -> p b n", b=4)
                        if kind == "q":
                            last = nc.scalar.activation(qT[:, hh % 3, 4 * ch:4 * ch + 4, :], src, ACT.Identity,
                                                        bias=l2q[:, layer, h:h + 1], scale=Q2_SCALE)
                        else:
                            nc.scalar.activation(kT[:, hh % 3, 4 * ch:4 * ch + 4, P:P + 1], ident[:, 0:4].unsqueeze(2), ACT.Identity,
                                                 bias=C(f"L2bk{layer + 1}", h), scale=0.0)
                            last = nc.scalar.activation(kT[:, hh % 3, 4 * ch:4 * ch + 4, 0:P], src, ACT.Identity,
                                                        bias=C(f"L2k{layer + 1}", h))
                        last.then_inc(L["qk"], 1)
                    elif e[0] in ("v", "WO"):
                        j_skip()
                    elif e[0] == "w":
                        take(*e[1:])
                    elif e[0] == "S":
                        g = e[1]
                        act.wait_ge(L["mx"], g + 1)
                        if g >= 3:
                            act.wait_ge(L["tm"], g - 2)
                        for k in range(2):
                            last = nc.scalar.activation(prob[:, g % 3, k * D:k * D + P + 1], ps[:, S_BANK + g % 2, k * D:k * D + P + 1],
                                                        ACT.Exp, bias=nmax[:, g % 4, k:k + 1], accum_out=psums[:, g % 4, k:k + 1])
                        last.then_inc(L["ex"], 1)
                    elif e[0] == "T":
                        g = e[1]
                        if g % 2 == 0:
                            act.wait_ge(L["tm"], g + 1)
                            if g >= 3:
                                act.wait_ge(L["pm"], g - 2)
                            nc.scalar.copy(probT[:, g % 3, 0:D], ps[:, T_BANK, 0:D]).then_inc(L["teA"], 1)
                    elif e[0] == "PV":
                        g = e[1]
                        p, r = divmod(g, 8)
                        hd, b2 = divmod(r, 4)
                        act.wait_ge(L["pm"], g + 1)
                        if p >= 1:
                            act.wait_ge(L["acc"], 4 * (p - 1) + b2 + 1)
                        nc.scalar.activation(cc[0][:, hd, 2 * b2:2 * b2 + 2, :],
                                             ps[:, O_BANK + g % 2, 0:D].rearrange("p (b n) -> p b n", b=2), ACT.Identity,
                                             bias=C(f"L2bv{p // PAIRS + 1}", (2 * p + hd) % H)).then_inc(L["ch"], 1)

            def mlp(name, func):
                m = M[name + "m"]
                for e in mlp_order(name):
                    if e[0] == "down":
                        j_skip()
                        continue
                    if e[0] == "w":
                        take(*e[1:])
                        continue
                    k = (FT // 2) * e[1] + e[2]
                    bank = j_take()
                    if k >= 2:
                        act.wait_ge(m["lo"], k - 1)
                    for fi in range(2):
                        last = nc.scalar.activation(gf[:, k % 2, fi * D:(fi + 1) * D], bank[:, fi * D:(fi + 1) * D], func,
                                                    bias=C(name + "b1", 2 * e[2] + fi))
                    last.then_inc(m["gelu"], 1)

            act.wait_ge(c_in, 16 * 7)
            nc.scalar.mul(q0b[:, :], C("L0q"), Q0_SCALE).then_inc(a_setup, 1)
            for layer in range(2):
                at = COLS[f"L2q{layer + 1}"][0]
                nc.scalar.mul(l2q[:, layer, :], col[:, at:at + H], Q2_SCALE).then_inc(a_setup, 1)
            act.wait_ge(a_setup, 3)
            norm("ctx", None)
            act.wait_ge(l0stat, 1)
            act.wait_ge(eps_ok, 1)
            nc.scalar.activation(sd[:, 1, :], sd[:, 0, :], ACT.Sqrt, bias=eps[:, 0:1]).then_inc(l0sq, 1)
            attention("L0")
            for k in range(B // 2):
                act.wait_ge(l0var, 2 * k + 2)
                nc.scalar.activation(ms[:, 1, 2 * k:2 * k + 2, :], ms[:, 1, 2 * k:2 * k + 2, :], ACT.Sqrt).then_inc(l0dev, 1)
            norm("lat", None)
            attention("L1")
            norm("L1r", ("L1w", None))
            mlp("L1", ACT.Gelu_apprx_tanh)
            act.wait_ge(M["L1m"]["out"], B // 2)
            take("L2p1_0")
            wide()
            norm("L2nm", ("L2mw", "L2mb"))
            mlp("L2", ACT.Gelu)
            norm("L3n1", ("L3lw", "L3lb"))
            attention("L3")
            norm("L3nm", ("L3mw", "L3mb"))
            mlp("L3", ACT.Gelu_apprx_tanh)

        @block.vector
        def _(dve):
            taken = [0]
            links = [0]

            def link(ins):
                links[0] += 1
                ins.then_inc(dch, 1)
                dve.wait_ge(dch, links[0])

            def j_take():
                j = taken[0]
                taken[0] += 1
                dve.wait_ge(jm, j + 1)
                return ps[:, J_BANK + j % 2, :]

            def j_skip():
                taken[0] += 1

            def f32(ap):
                return ap.bitcast(F32)

            def take(name, part=0, parts=PARTS):
                loaded(dve, name)
                n = PACK_AT[name]
                dst = pack_dst(name, part, parts)
                at = part * (PACK // PARTS)
                src = wraw[:, n % 2, at:at + dst[0].shape[-1]]
                if len(dst) == 1:
                    nc.vector.tensor_copy(dst[0], src).then_inc(w_lo[n % 2], 1)
                    return
                dve.wait_ge(w_hi[n % 2], HI_AT[name] + part + parts)
                last = nc.vector.tensor_tensor(dst[1], src, f32(dst[0]), ALU.subtract)
                if part + parts == PARTS:
                    last.then_inc(w_lo[n % 2], 1)
                elif name[:3] == "L2p" and name[-1] == "1" and part + parts == 2:
                    last.then_inc(w_v, 1)

            def stats(src, k, s, v):
                dve.wait_ge(s, v)
                for b in (2 * k, 2 * k + 1):
                    last = nc.vector.bn_stats(st6[:, b, :], src[:, b, :])
                if k == B // 2 - 1:
                    link(last)

            def norm(name, src):
                n = N[name]
                if src is not None:
                    for b in range(B):
                        last = nc.vector.bn_aggr(mv[:, b, :], st6[:, b, :])
                    link(last)
                    if name == "L1r":
                        link(nc.vector.tensor_tensor(sd[:, 2, :], mv[:, :, 0], mv[:, :, 0], ALU.mult))
                        nc.vector.tensor_tensor(sd[:, 0, :], sd[:, 2, :], mv[:, :, 1], ALU.add).then_inc(n["stat"], 1)
                    else:
                        nc.vector.tensor_copy(sd[:, 0, :], mv[:, :, 1]).then_inc(n["stat"], 1)
                    dve.wait_ge(n["sq"], 1)
                    nc.vector.reciprocal(sd[:, 3, :], sd[:, 1, :]).then_inc(n["r"], 1)
                    dve.wait_ge(n["r"], 1)
                    for b in range(0, B, 2):
                        if name == "L1r":
                            i = nc.vector.tensor_scalar(XH[:, b, :], src[:, b, :], sd[:, 3, b:b + 1], None, ALU.mult)
                        else:
                            i = nc.vector.tensor_scalar(XH[:, b, :], src[:, b, :], mv[:, b, 0:1], sd[:, 3, b:b + 1],
                                                        ALU.subtract, ALU.mult)
                        i.then_inc(n["xh"], 1)
                for k in range(B // 2):
                    bank = j_take().rearrange("p (q f n) -> p q f n", q=2, f=KT)
                    hi, lo = ct if name == "ctx" else ht
                    two = slice(2 * k, 2 * k + 2)
                    if src is None:
                        dve.wait_ge(n["hi"], k + 1)
                        for f in range(KT):
                            last = nc.vector.tensor_tensor(lo[:, f, two, :], bank[:, :, f, :], f32(hi[:, f, two, :]), ALU.subtract)
                    else:
                        dve.wait_ge(n["a"], k + 1)
                        xa = probT[:, k % 3, :].rearrange("p (f q n) -> p f q n", f=KT, q=2)
                        link(nc.vector.tensor_copy(hi[:, :, two, :], xa))
                        last = nc.vector.tensor_tensor(lo[:, :, two, :], xa, f32(hi[:, :, two, :]), ALU.subtract)
                    last.then_inc(n["lo"], 1)

            def attention(ph):
                c, a = ATT[ph], A[ph]
                U, keys = c["units"], c["keys"]
                nh = 4 // U
                total = c["iters"] * STEPS * 2 * U

                def reciprocal(u):
                    dve.wait_ge(a["ex"], u + 1)
                    if u >= 4:
                        dve.wait_ge(a["nm"], u - 3)
                    nc.vector.reciprocal(prec[:, u % 4, 0:nh], psums[:, u % 4, 0:nh]).then_inc(a["rc"], 1)

                for e, i, *k in late(att_order(ph), ("dq", "dk", "dv", "pq", "pk", "OUT", "WO", "w")):
                    if e == "w":
                        take(i)
                    elif e == "dq" and ph == "L0":
                        bank = j_take()
                        dve.wait_ge(a["hi"], i + 1)
                        nc.vector.scalar_tensor_tensor(dk[1][:, 0, 0:D], bank[:, D:2 * D], C("L0k"), f32(dk[0][:, 0, 0:D]),
                                                       ALU.add, ALU.subtract)
                        dve.wait_ge(a["xq"], i + 1)
                        link(nc.vector.tensor_copy(dq[0][:, 0, :], xq))
                        nc.vector.tensor_tensor(dq[1][:, 0, :], xq, f32(dq[0][:, 0, :]), ALU.subtract).then_inc(a["dense"], 1)
                    elif e == "dv" and ph == "L0":
                        bank = j_take()
                        if i == 0:
                            dve.wait_ge(vzero, 1)
                        for t in range(2):
                            v = diag(vt[:, i % 2, 0, t, :, :].rearrange("p (q g) c -> p q (g c)", q=4))
                            src = bank[:, t * P:(t + 1) * P].rearrange("p (q g d) -> p q g d", q=4, g=4)
                            bias = R("L0v")[:, 0:P].rearrange("p (q g d) -> p q g d", q=4, g=4)
                            last = nc.vector.tensor_tensor(v, src, bias, ALU.add)
                        link(last)
                        for t in range(2):
                            v = diag(vt[:, i % 2, 0, t, :, :].rearrange("p (q g) c -> p q (g c)", q=4))
                            vv = diag(vt[:, i % 2, 1, t, :, :].rearrange("p (q g) c -> p q (g c)", q=4))
                            last = nc.vector.tensor_tensor(vv, v, v, ALU.mult)
                        last.then_inc(a["vals"], 1)
                    elif e == "dk" and ph == "L1":
                        bank = j_take()
                        dve.wait_ge(a["hi"], 3 * i + 2 + k[0])
                        nc.vector.scalar_tensor_tensor(dk[1][:, k[0], :], bank, C("L1k", k[0]), f32(dk[0][:, k[0], :]),
                                                       ALU.add, ALU.subtract).then_inc(a["dense"], 1)
                    elif e in ("dq", "dk"):
                        bank = j_take()
                        dve.wait_ge(a["hi"], (3 if ph == "L1" else 2) * i + (1 if e == "dq" else 2))
                        hi, lo = dq if e == "dq" else dk
                        for t in range(2):
                            last = nc.vector.scalar_tensor_tensor(lo[:, t, 0:D], bank[:, t * D:(t + 1) * D], C(ph + e[1], t),
                                                                  f32(hi[:, t, 0:D]), ALU.add, ALU.subtract)
                        last.then_inc(a["dense"], 1)
                    elif e == "dv":
                        if i == 0:
                            dve.wait_ge(vzero, {"L1": 2, "L3": 3}[ph])
                        bank = j_take()
                        for s in range(2):
                            im, t = (k[0], s) if ph == "L1" else (s, 0)
                            src = bank[:, s * D:(s + 1) * D].rearrange("p (t e q d) -> p e t q d", t=2, e=2, q=4)
                            bias = R(ph + "v").rearrange("p (t e q d) -> p e t q d", t=2, e=2, q=4)
                            dst = vt[:, i % 2, im, t, :, :].rearrange("p (t e q) c -> p e t q c", t=2, e=2)
                            for half in range(2):
                                last = nc.vector.tensor_tensor(dst[:, half, :, :, 16 * half:16 * half + 16], src[:, half], bias[:, half],
                                                               ALU.add)
                        last.then_inc(a["vals"], 1)
                    elif e == "pq" and ph != "L0":
                        j_skip()
                    elif e in ("pq", "pk"):
                        if i >= 2:
                            dve.wait_ge(a["sm"], 2 * U * (i - 1))
                        else:
                            dve.wait_ge(g_setup, {"L0": 1, "L1": 2, "L3": 3}[ph])
                        bank = j_take()
                        if ph == "L0":
                            dve.wait_ge(a["stA"], 2 * i + 1)
                            for q in range(2, 4):
                                last = nc.vector.tensor_copy(ks[ph][32 * q:32 * q + 32, i % 2, q * D:(q + 1) * D],
                                                             bank[32 * q:32 * q + 32, D:2 * D])
                        elif ph == "L1":
                            src = bank[64:128, :].rearrange("p (s m n) -> p m s n", s=2, m=2)
                            dst = ks[ph][64:128, i % 2, k[0] * 1024:(k[0] + 1) * 1024].rearrange("p (m h s n) -> p m h s n", m=2, h=2, s=2)
                            last = nc.vector.tensor_copy(dst[:, :, 1, :, :], src)
                        else:
                            for g in range(2):
                                src = bank[64:128, g * D:(g + 1) * D].rearrange("p (m n) -> p m n", m=2)
                                dst = ks[ph][64:128, i % 2, g * 512:(g + 1) * 512].rearrange("p (m h n) -> p m h n", m=2, h=2)
                                last = nc.vector.tensor_copy(dst[:, :, 1, :], src)
                        last.then_inc(a["stD"], 1)
                    elif e == "S":
                        dve.wait_ge(a["sm"], i + 1)
                        nc.vector.tensor_reduce(nmax[:, i % 4, 0:nh], ps[:, S_BANK + i % 2, :].rearrange("p (h n) -> p h n", h=nh),
                                                AX.X, ALU.max, negate=True).then_inc(a["mx"], 1)
                        if i >= 1:
                            reciprocal(i - 1)
                        if i == total - 1:
                            reciprocal(i)
                    elif e == "T":
                        if i % 2 == 1:
                            dve.wait_ge(a["tm"], i + 1)
                            if i >= 3:
                                dve.wait_ge(a["pm"], (i - 3) // U + 1)
                            nc.vector.tensor_copy(probT[:, i % 3, :], ps[:, T_BANK + 1, :]).then_inc(a["teD"], 1)
                    elif e == "OUT" and ph != "L0":
                        im = k[0]
                        dve.wait_ge(a["oeA"], 2 * i + im + 1)
                        nc.vector.tensor_tensor(uu[1][:, im, :, :], ps[:, O_BANK + im, 0:D].rearrange("p (t n) -> p t n", t=2),
                                                f32(uu[0][:, im, :, :]), ALU.subtract).then_inc(a["oeD"], 1)
                    elif e == "WO" and ph != "L0":
                        bank = j_take()
                        dve.wait_ge(ybias, 1 if ph == "L1" else 6)
                        dst = (XH if ph == "L1" else X)[:, 2 * i:2 * i + 2, :]
                        nc.vector.tensor_tensor(dst, bank.rearrange("p (b n) -> p b n", b=2), dst, ALU.add).then_inc(a["done"], 1)
                        stats(XH if ph == "L1" else X, i, a["done"], i + 1)

            def diag(v):
                return bass.AP(v.tensor, v.offset, [list(v.ap[0]), list(v.ap[1]), [40, 4], [1, 8]])

            def wide():
                for e in wide_order():
                    if e[0] == "norm":
                        norm(f"L2n{e[1] + 1}", X)
                    elif e[0] in ("q", "k"):
                        j_skip()
                    elif e[0] == "w":
                        take(*e[1:])
                    elif e[0] == "v":
                        _, p, k = e
                        if k == 0:
                            dve.wait_ge(bv_in[p % 2], 16 * (p // 2 + 1))
                            link(nc.vector.tensor_tensor(bvr[:, p % 2, 0, :], bvr[:, p % 2, 0, :], bvr[:, p % 2, 1, :], ALU.subtract))
                        bank = j_take().rearrange("p (b n) -> p b n", b=2)
                        nc.vector.tensor_tensor(v2[:, p % 2, 2 * k:2 * k + 2, :, :].rearrange("p b h n -> p b (h n)"), bank,
                                                bvr[:, p % 2, 0:1, :].broadcast_to([P, 2, D]), ALU.add).then_inc(L["v"], 1)
                    elif e[0] == "WO":
                        _, p, b2 = e
                        bank = j_take().rearrange("p (b n) -> p b n", b=2)
                        if p % PAIRS == 0 and b2 == 0:
                            dve.wait_ge(ybias, 3 + p // PAIRS)
                        if p > 0:
                            dve.wait_ge(L["acc"], 4 * (p - 1) + b2 + 1)
                        dst = X[:, 2 * b2:2 * b2 + 2, :]
                        nc.vector.tensor_tensor(dst, bank, dst, ALU.add).then_inc(L["acc"], 1)
                        if p % PAIRS == PAIRS - 1:
                            stats(X, b2, L["acc"], 4 * p + b2 + 1)
                    elif e[0] == "S":
                        g = e[1]
                        dve.wait_ge(L["sm"], g + 1)
                        nc.vector.tensor_reduce(nmax[:, g % 4, 0:2],
                                                ps[:, S_BANK + g % 2, :].rearrange("p (h n) -> p h n", h=2)[:, :, 0:P + 1],
                                                AX.X, ALU.max, negate=True).then_inc(L["mx"], 1)
                    elif e[0] == "R":
                        g = e[1]
                        dve.wait_ge(L["ex"], g + 1)
                        if g >= 4:
                            dve.wait_ge(L["nm"], g - 3)
                        nc.vector.reciprocal(prec[:, g % 4, 0:2], psums[:, g % 4, 0:2]).then_inc(L["rc"], 1)
                    elif e[0] == "T":
                        g = e[1]
                        if g % 2 == 1:
                            dve.wait_ge(L["tm"], g + 1)
                            if g >= 3:
                                dve.wait_ge(L["pm"], g - 2)
                            nc.vector.tensor_copy(probT[:, g % 3, 0:D], ps[:, T_BANK + 1, 0:D]).then_inc(L["teD"], 1)
                    elif e[0] == "PV":
                        g = e[1]
                        p, r = divmod(g, 8)
                        hd, b2 = divmod(r, 4)
                        dve.wait_ge(L["ch"], g + 1)
                        two = slice(2 * b2, 2 * b2 + 2)
                        nc.vector.scalar_tensor_tensor(cc[1][:, hd, two, :], ps[:, O_BANK + g % 2, 0:D].rearrange("p (b n) -> p b n", b=2),
                                                       C(f"L2bv{p // PAIRS + 1}", (2 * p + hd) % H), f32(cc[0][:, hd, two, :]),
                                                       ALU.add, ALU.subtract).then_inc(L["cl"], 1)

            def mlp(name, y):
                m = M[name + "m"]
                for e in mlp_order(name):
                    if e[0] == "w":
                        take(*e[1:])
                    elif e[0] == "up":
                        k = (FT // 2) * e[1] + e[2]
                        j_skip()
                        dve.wait_ge(m["gelu"], k + 1)
                        src = gf[:, k % 2, :].rearrange("p (f n) -> p f n", f=2)
                        two = slice(2 * e[2], 2 * e[2] + 2)
                        if e[1] > 0 and e[2] == 0:
                            dve.wait_ge(m["out"], e[1])
                        link(nc.vector.tensor_copy(gg[0][:, two, :], src))
                        nc.vector.tensor_tensor(gg[1][:, two, :], src, f32(gg[0][:, two, :]), ALU.subtract).then_inc(m["lo"], 1)
                    else:
                        c = e[1]
                        bank = j_take().rearrange("p (b n) -> p b n", b=2)
                        if c == 0:
                            dve.wait_ge(ybias, y)
                        dst = X[:, 2 * c:2 * c + 2, :]
                        nc.vector.tensor_tensor(dst, bank, dst, ALU.add).then_inc(m["out"], 1)
                        if name != "L3":
                            stats(X, c, m["out"], c + 1)

            nc.vector.memset(eps[:, 0:1], 1e-5)
            nc.vector.memset(eps[:, 1:2], 1e-6).then_inc(eps_ok, 1)
            dve.wait_ge(c_in, 16 * 7)
            nc.vector.tensor_copy(indr[:, :, :].rearrange("p a b -> p (a b)"), prob[0:1, 2, 0:2 * P])
            nc.vector.tensor_scalar(mb0, mt8[0:1, :, :].rearrange("p a b -> p (a b)"), 0.0, MASKED, ALU.is_equal, ALU.mult)\
              .then_inc(A["L0"]["mask"], 1)
            nc.vector.tensor_scalar(mb13[:, :], probT[0:1, :, :].bitcast(I32).rearrange("p a b -> p (a b)")[:, 0:B * P],
                                    0.0, MASKED, ALU.is_equal, ALU.mult).then_inc(A["L1"]["mask"], 1)
            take("L0w0")
            take("L0sel0")
            take("L0sel1")
            norm("ctx", None)
            dve.wait_ge(x_in, 32)
            link(nc.vector.tensor_reduce(sd[:, 2, :], mt8[:, :, :], AX.X, ALU.add))
            for b in range(B):
                last = nc.vector.tensor_tensor_reduce(ms[:, 0, b, :], X[:, b, :], mt8[:, b, :], 1.0, 0.0, ALU.mult, ALU.add, sd[:, 3, b:b + 1])
            link(last)
            for b in range(B):
                last = nc.vector.tensor_tensor_reduce(ms[:, 1, b, :], ms[:, 0, b, :], ms[:, 0, b, :], 1.0, 0.0, ALU.mult, ALU.add, sd[:, 4, b:b + 1])
            link(nc.vector.reciprocal(sd[:, 2, :], sd[:, 2, :]))
            link(nc.vector.tensor_tensor(mv[:, :, 0], sd[:, 3, :], sd[:, 2, :], ALU.mult))
            link(nc.vector.tensor_tensor(sd[:, 4, :], sd[:, 4, :], sd[:, 2, :], ALU.mult))
            link(nc.vector.tensor_tensor(sd[:, 5, :], mv[:, :, 0], mv[:, :, 0], ALU.mult))
            link(nc.vector.tensor_tensor(sd[:, 4, :], sd[:, 4, :], sd[:, 5, :], ALU.subtract))
            nc.vector.tensor_scalar(sd[:, 0, :], sd[:, 4, :], 0.0, None, ALU.max).then_inc(l0stat, 1)
            dve.wait_ge(l0sq, 1)
            nc.vector.reciprocal(sd[:, 3, :], sd[:, 1, :]).then_inc(l0n, 1)
            attention("L0")
            take("L1sel0")
            take("L1sel1")
            for k in range(B // 2):
                two = slice(2 * k, 2 * k + 2)
                dve.wait_ge(l0mul, k + 1)
                link(nc.vector.tensor_tensor(X[:, two, :], X[:, two, :], ms[:, 0, two, :], ALU.add))
                nc.vector.tensor_tensor(X[:, two, :], X[:, two, :], mt8[:, two, :], ALU.mult).then_inc(fin, 2)
            norm("lat", None)
            attention("L1")
            norm("L1r", XH)
            nc.vector.tensor_scalar(mb13[:, :], mraw3[:, :], 0.0, MASKED, ALU.is_equal, ALU.mult).then_inc(A["L3"]["mask"], 1)
            mlp("L1", 2)
            dve.wait_ge(M["L1m"]["out"], B // 2)
            take("L2p1_0")
            wide()
            norm("L2nm", X)
            mlp("L2", 5)
            norm("L3n1", X)
            dve.wait_ge(rowb_in, 16)
            attention("L3")
            norm("L3nm", X)
            mlp("L3", 7)

        @block.gpsimd
        def _(pool):
            glinks = [0]

            def link(ins):
                glinks[0] += 1
                ins.then_inc(g_link, 1)
                pool.wait_ge(g_link, glinks[0])

            def normalise(a, u, nh, keys, stride):
                pool.wait_ge(a["rc"], u + 1)
                pr = prob[:, u % 3, :].rearrange("p (h n) -> p h n", n=stride)[:, 0:nh, 0:keys]
                nc.gpsimd.tensor_tensor(pr, pr, prec[:, u % 4, 0:nh].unsqueeze(2).broadcast_to([P, nh, keys]), ALU.mult)\
                  .then_inc(a["nm"], 1)

            def zero_stacks(ph):
                nc.gpsimd.memset(ks[ph].rearrange("p a b -> p (a b)").bitcast(F32), 0.0).then_inc(g_setup, 1)
                nc.gpsimd.memset(fs[:, 0:4096], 0.0).then_inc(vzero, 1)

            def norm(name, src):
                n = N[name]
                pool.wait_ge(n["r"], 1)
                for b in range(1, B, 2):
                    if name == "L1r":
                        i = nc.gpsimd.tensor_scalar(XH[:, b, :], src[:, b, :], sd[:, 3, b:b + 1], None, ALU.mult)
                    else:
                        i = nc.gpsimd.tensor_scalar(XH[:, b, :], src[:, b, :], mv[:, b, 0:1], sd[:, 3, b:b + 1], ALU.subtract, ALU.mult)
                    i.then_inc(n["xp"], 1)
                pool.wait_ge(n["xh"], B // 2)
                pool.wait_ge(n["xp"], B // 2)

            def attention(ph):
                c, a = ATT[ph], A[ph]
                U, keys = c["units"], c["keys"]
                for e, i, *k in att_order(ph):
                    if e == "S":
                        normalise(a, i, 4 // U, keys, keys)
                    if ph == "L0" and e == "S" and i % (2 * U * STEPS) == 8:
                        b = i // (2 * U * STEPS)
                        pool.wait_ge(a["dense"], b + 1)
                        if b == 0:
                            pool.wait_ge(l0n, 1)
                        nc.gpsimd.tensor_scalar(X[:, b, :], ms[:, 0, b, :], mv[:, b, 0:1], sd[:, 3, b:b + 1], ALU.subtract, ALU.mult)\
                          .then_inc(xn_done, 1)
                    if ph == "L0" and e == "OUT" and k[0] == 1:
                        pool.wait_ge(a["oeA"], 2 * i + 2)
                        if i > 0:
                            pool.wait_ge(l0var, i)
                        link(nc.gpsimd.tensor_tensor(msq, ms[:, 0, i, :], ms[:, 0, i, :], ALU.mult))
                        link(nc.gpsimd.tensor_tensor(ms[:, 1, i, :], ms[:, 1, i, :], msq, ALU.subtract))
                        nc.gpsimd.tensor_scalar(ms[:, 1, i, :], ms[:, 1, i, :], 0.0, None, ALU.max).then_inc(l0var, 1)

            def add_row(dst, name):
                nc.gpsimd.tensor_tensor(dst[:, :, :], X[:, :, :], R(name).unsqueeze(1).broadcast_to([P, B, D]), ALU.add)\
                  .then_inc(ybias, 1)

            zero_stacks("L0")
            attention("L0")
            pool.wait_ge(xn_done, B)
            for k in range(B // 2):
                two = slice(2 * k, 2 * k + 2)
                pool.wait_ge(l0dev, k + 1)
                nc.gpsimd.tensor_tensor(X[:, two, :], X[:, two, :], ms[:, 1, two, :], ALU.mult).then_inc(l0mul, 1)
            zero_stacks("L1")
            pool.wait_ge(fin, B)
            add_row(XH, "L1o")
            attention("L1")
            pool.wait_ge(ybias, 1)
            pool.wait_ge(N["lat"]["lo"], B // 2)
            add_row(X, "L1b2")
            norm("L1r", XH)
            for layer in range(2):
                norm(f"L2n{layer + 1}", X)
                if layer == 1:
                    pool.wait_ge(rowb_in, 16)
                add_row(X, f"L2bo{layer + 1}")
                for u in range(8 * PAIRS):
                    normalise(L, 8 * PAIRS * layer + u, 2, P, D)
            norm("L2nm", X)
            add_row(X, "L2b2")
            pool.wait_ge(M["L2m"]["out"], B // 2)
            zero_stacks("L3")
            norm("L3n1", X)
            add_row(X, "L3o")
            attention("L3")
            norm("L3nm", X)
            add_row(X, "L3b2")


def selection(ph):
    S = np.zeros((4, 4, P, P), np.float32)
    dh, heads = (8, 4) if ph == "L0" else (16, 2)
    scale = {"L0": 1.0, "L1": 1.0 / 16, "L3": 1.0 / 4}[ph]
    for g in range(4):
        for j in range(heads):
            h = 4 * j + g if ph == "L0" else 2 * g + j
            for d in range(dh):
                c = dh * h + d
                r = (P // heads) * j + d
                for part in range(3):
                    S[g, 0 if part != 1 else 1, c, r + dh * part] = scale
                    S[g, 2 if part != 2 else 3, c, r + dh * part] = 1.0
    return S.transpose(2, 0, 1, 3).reshape(P, 4 * 4 * P)


def kernel(**inputs):
    import concourse.bacc as _bacc
    from concourse.bass_utils import run_bass_kernel_spmd as _run

    g = {k: np.asarray(v) for k, v in inputs.items()}

    def tiles(w):
        return w.reshape(-1, P, w.shape[1]).transpose(1, 0, 2)

    def flat(*ws):
        return np.concatenate([w.reshape(P, -1) for w in ws], 1)

    packs = [np.concatenate([flat(*(g[f"L0_xattn_W{k}"].T for k in "qkv")), np.zeros((P, PACK - 3 * P), np.float32)], 1)]

    def add(w):
        assert w.shape == (P, 2 * PACK), w.shape
        packs.extend([w[:, :PACK], w[:, PACK:]])

    def out_rows(w):
        return w.reshape(2, 2, 4, 16, D).transpose(0, 2, 1, 3, 4).reshape(D, D)

    kv = g["L1_xattn_kv_w"].reshape(D, D, 2)
    kvb = g["L1_xattn_kv_b"].reshape(D, 2)
    add(selection("L0"))
    add(flat(tiles(g["L1_xattn_q_w"]), tiles(kv[:, :, 0]), tiles(kv[:, :, 1]), tiles(out_rows(g["L1_xattn_out_w"]))))
    add(selection("L1"))
    add(flat(tiles(g["L1_xattn_mlp_w1"])))
    add(flat(tiles(g["L1_xattn_mlp_w2"])))
    add(selection("L3"))
    for l in (1, 2):
        for p in range(PAIRS):
            c = slice(2 * P * p, 2 * P * (p + 1))
            add(flat(*(tiles(g[f"L2_xattn_w{k}{l}"][:, c]) for k in "qkv"), tiles(g[f"L2_xattn_wo{l}"][c, :])))
    add(flat(tiles(g["L2_xattn_w_fc1"])))
    add(flat(tiles(g["L2_xattn_w_fc2"])))
    add(flat(*(tiles(g[f"L3_xattn_{k}_w"]) for k in "qkv"), tiles(out_rows(g["L3_xattn_cproj_w"]))))
    add(flat(tiles(g["L3_xattn_fc_w"])))
    add(flat(tiles(g["L3_xattn_proj_w"])))

    r = np.arange(P)
    ind = [((r % 32) == 24).astype(np.float32), ((r % 64) == 48).astype(np.float32)]
    vec = {
        "ones0": ind[0], "ones1": ind[1],
        "L0q": g["L0_xattn_bq"], "L0k": g["L0_xattn_bk"], "L1q": g["L1_xattn_q_b"], "L1k": kvb[:, 0],
        "L1w": g["L1_xattn_postnorm_w"], "L1b1": g["L1_xattn_mlp_b1"],
        "L2mw": g["L2_xattn_ln_mlp_scale"], "L2mb": g["L2_xattn_ln_mlp_offset"], "L2b1": g["L2_xattn_b_fc1"],
        "L3q": g["L3_xattn_q_b"], "L3k": g["L3_xattn_k_b"], "L3lw": g["L3_xattn_ln1_w"], "L3lb": g["L3_xattn_ln1_b"],
        "L3mw": g["L3_xattn_ln2_w"], "L3mb": g["L3_xattn_ln2_b"], "L3b1": g["L3_xattn_fc_b"],
    }
    for l in (1, 2):
        vec |= {f"L2q{l}": g[f"L2_xattn_bq{l}"], f"L2k{l}": g[f"L2_xattn_bk{l}"], f"L2bk{l}": g[f"L2_xattn_bias_k{l}"],
                f"L2bv{l}": g[f"L2_xattn_bias_v{l}"], f"L2lw{l}": g[f"L2_xattn_ln{l}_scale"], f"L2lb{l}": g[f"L2_xattn_ln{l}_offset"]}
    cols = np.concatenate([vec[n].reshape(-1, P).T for n in COLS], 1)
    rowv = {"L0v": np.concatenate([g["L0_xattn_bv"], np.zeros(P, np.float32)]), "L1v": kvb[:, 1], "L1o": g["L1_xattn_out_b"],
            "L1b2": g["L1_xattn_mlp_b2"], "L2bo1": g["L2_xattn_bo1"], "L2bo2": g["L2_xattn_bo2"], "L2b2": g["L2_xattn_b_fc2"],
            "L3v": g["L3_xattn_v_b"], "L3o": g["L3_xattn_cproj_b"], "L3b2": g["L3_xattn_proj_b"]}
    rows = np.stack([rowv[n] for n in ROWS]).reshape(2, ROW_SET * D)
    l2rows = np.stack([np.stack([g[f"L2_xattn_bv{l}"].reshape(PAIRS, D), g[f"L2_xattn_bias_v{l}"].reshape(PAIRS, D)], 1)
                       for l in (1, 2)]).reshape(2 * PAIRS, 2 * D)

    arrays = {
        "x": g["x"], "ctx": g["ctx_2048"],
        "mask_t": g["mask_Bx1x2048_bf1"].reshape(1, B * D).view(np.uint8),
        "mask_s2": g["mask_BxS2_ik0"].reshape(1, B * P),
        "mask_s3": g["mask_BxS2_bf1"].reshape(1, B * P).view(np.uint8),
        "packs": np.stack(packs), "cols": cols, "rows": rows, "l2rows": l2rows,
        "inds": np.concatenate(ind).reshape(1, 2 * P), "ident": np.eye(P, dtype=np.float32),
    }
    nc = _bacc.Bacc("TRN2", target_bir_lowering=False, num_devices=1)
    sent, args = {}, []
    for name, a in arrays.items():
        a = np.ascontiguousarray(a)
        sent[f"in_{name}"] = a
        args.append(nc.dram_tensor(f"in_{name}", a.shape, mybir.dt.from_np(a.dtype), kind="ExternalInput").ap())
    args.append(nc.dram_tensor("out_0", (B, P, D), F32, kind="ExternalOutput").ap())
    build(nc, *args)
    res = _run(nc, [sent], core_ids=[0])
    return res.results[0]["out_0"]
```

```python
from contextlib import ExitStack

import numpy as np

import concourse.bass as bass
from concourse import mybir

F32 = mybir.dt.float32
F32R = mybir.dt.float32r
U8 = mybir.dt.uint8
I32 = mybir.dt.int32
ACT = mybir.ActivationFunctionType
ALU = mybir.AluOpType
AX = mybir.AxisListType

P = 128
B = 8
D = 256
KT = D // P
H = 16
DK2 = 128
PAIRS = H // 2
FF = 4 * D
FT = FF // P
GT = FT + 2
PACK = 1024
MASKED = -float(2 ** 100)
Q0_SCALE = 8 ** -0.5
Q2_SCALE = DK2 ** -0.5

PACKS = ["L0w0"]
for _n in (["L0sel", "L1att", "L1sel", "L1w1_", "L1w2_", "L3sel"] + [f"L2p{i}_" for i in range(2 * PAIRS)]
           + ["L2w1_", "L2w2_", "L3att", "L3w1_", "L3w2_"]):
    PACKS += [_n + "0", _n + "1"]
PACK_AT = {n: i for i, n in enumerate(PACKS)}
PARTS = 4
HI_AT = {}
for _n in PACKS:
    if not _n.startswith(("L0w", "L0sel", "L1sel", "L3sel")):
        HI_AT[_n] = PARTS * sum(PACK_AT[m] % 2 == PACK_AT[_n] % 2 for m in HI_AT)

COLS = {}
for _n, _w in ([("ones0", 1), ("ones1", 1), ("L0q", 1), ("L0k", 1), ("L1q", 2), ("L1k", 2), ("L1w", 2), ("L1b1", 8)]
               + [(f"L2{s}{l}", w) for l in (1, 2) for s, w in (("q", 16), ("k", 16), ("bk", 16), ("bv", 16), ("lw", 2), ("lb", 2))]
               + [("L2mw", 2), ("L2mb", 2), ("L2b1", 8), ("L3q", 2), ("L3k", 2), ("L3lw", 2), ("L3lb", 2),
                  ("L3mw", 2), ("L3mb", 2), ("L3b1", 8)]):
    COLS[_n] = (sum(w for _, w in COLS.values()), _w)
NCOLS = sum(w for _, w in COLS.values())

ROWS = ["L0v", "L1v", "L1o", "L1b2", "L2bo1", "L2bo2", "L2b2", "L3v", "L3o", "L3b2"]
ROW_SET = 5

ATT = {
    "L0": dict(iters=8, keys=256, units=2, key_tiles=2, stack_a=2, stack_d=1),
    "L1": dict(iters=4, keys=256, units=2, key_tiles=2, stack_a=3, stack_d=2),
    "L3": dict(iters=4, keys=128, units=1, key_tiles=1, stack_a=2, stack_d=1),
}
STEPS = 4
AFFINE = {"L1r": ("L1w", None), "L2n1": ("L2lw1", "L2lb1"), "L2n2": ("L2lw2", "L2lb2"), "L2nm": ("L2mw", "L2mb"),
          "L3n1": ("L3lw", "L3lb"), "L3nm": ("L3mw", "L3mb")}
T_LAG = 3
WO_LATE = 5 - T_LAG
TE_ACT = {"L0": 4, "L1": 2, "L3": 2}
LATE = {"L0": ("dq", "pq", "dv", "OUT", "w", "nT"), "L1": ("dq", "dk", "w", "nT"),
        "L3": ("dq", "dk", "pq", "pk", "OUT", "WO", "dv", "w", "nT")}
CHUNKS = (range(0, B // 2 - 1), range(B // 2 - 1, B // 2))
NORMS = ["ctx", "lat", "L1r", "L2n1", "L2n2", "L2nm", "L3n1", "L3nm"]


def att_order(ph):
    c = ATT[ph]
    U = c["units"]
    per_step = 2 * U
    per_it = STEPS * per_step
    total = c["iters"] * per_it
    prep = {"L0": [(1, "pq", 0)], "L1": [(0, "pq", 0), (1, "pk", 0), (2, "pk", 1)], "L3": [(0, "pq", 0), (0, "pk", 0)]}[ph]
    dense = {"L0": [(2 * 4 + 2, "dq", 0), (3 * 4 + 0, "dv", 0)],
             "L1": [(1 * 4 + 3, "dk", 0), (2 * 4 + 1, "dq", 0), (2 * 4 + 3, "dk", 1), (3 * 4 + 3, "dv", 0), (4 * 4 + 3, "dv", 1)],
             "L3": [(2 * 2 + 1, "dq", 0), (2 * 2 + 1, "dk", 0), (4 * 2 + 1, "dv", 0)]}[ph]
    after = {"L0": None, "L1": "L1r", "L3": "L3nm"}[ph]
    for _, e, k in dense:
        yield (e, 0, k)
    for _, e, k in prep:
        yield (e, 0, k)
    for u in range(total + T_LAG + 4):
        s, r = divmod(u, per_step)
        if u < total:
            yield ("S", u)
        w = u - T_LAG - 2
        if w >= 0 and w < total and w % U == U - 1:
            yield ("PV", w // U)
            if w % per_it == per_it - 1:
                yield ("OUT", w // per_it)
        if 0 <= u - T_LAG < total:
            yield ("T", u - T_LAG)
        for it in range(c["iters"]):
            if w == (it + 1) * per_it + (WO_LATE if ph == "L3" and it + 1 < c["iters"] else 0):
                if it + 1 == c["iters"] and ph != "L0":
                    yield ("w", ph + "w1_1")
                yield ("WO", it)
        if ph == "L0" and 2 <= u <= B + 2:
            yield ("xs", u - 2)
        if ph == "L0" and u == B + 4:
            yield ("sq", 0)
        if ph == "L0" and u % per_step == 3 and 1 <= u // 8 <= 4 and u // 4 % 2:
            yield ("nT", "ctx", u // 8 - 1)
        if u < total:
            for at, e, k in prep:
                if r == at and s + 1 < c["iters"] * STEPS:
                    yield (e, s + 1, k)
            for at, e, k in dense:
                it, o = divmod(u - at, per_it)
                if o == 0 and it >= 0 and it + 1 < c["iters"]:
                    yield (e, it + 1, k)
        if ph == "L0" and u in (40, 48):
            yield ("w", f"L1att{u // 48}")
        if u == total and ph != "L0":
            yield ("nS", after, 0)
            yield ("nX", after, 0)
            yield ("w", ph + "w1_0")
        if u == total and ph == "L0":
            for k in range(3):
                yield ("fin", k)
    if ph == "L0":
        yield ("nT", "lat", 0)
        yield ("fin", 3)
        for k in range(1, B // 2):
            yield ("nT", "lat", k)
    else:
        yield from norm_end(after)


def norm_end(name):
    yield ("nS", name, 1)
    yield ("nT", name, 0)
    yield ("nX", name, 1)
    for k in range(1, B // 2):
        yield ("nT", name, k)


def dense_at(ph, it, e, k):
    order = {"L0": [("dq", 0)], "L1": [("dk", 0), ("dq", 0), ("dk", 1)], "L3": [("dq", 0), ("dk", 0)]}[ph]
    return len(order) * it + order.index((e, k)) + 1


def late(order, kinds):
    order = list(order)
    scores = [n for n, e in enumerate(order) if e[0] == "S"]
    kept = []
    for n, e in enumerate(order):
        if e[0] in kinds and scores[0] < n < scores[-1]:
            kept.append(e)
            continue
        yield e
        if e[0] == "S":
            yield from kept
            kept = []


def first_keys(p):
    return [("k", p, hd, ch) for hd in range(2) for ch in range(2)]


def wide_order():
    pairs = 2 * PAIRS

    def start(p):
        if p:
            yield from norm_end("L2n2")
        else:
            for k in range(4):
                yield ("v", p, k)
        for hd in range(2):
            for ch in range(2):
                yield ("q", p, hd, ch)

    yield from start(0)
    for p in range(pairs):
        last = p % PAIRS == PAIRS - 1
        first = p % PAIRS == 0
        norm = "L2n2" if p < PAIRS else "L2nm"
        for u in range(12 if last else 8):
            g = 8 * p + u
            if u < 8:
                yield ("S", g)
            if 0 <= u - 1 < 8 or u == 0 and not first:
                yield ("R", g - 1)
            if 0 <= u - 2 < 8 or u < 2 and not first:
                yield ("T", g - 2)
            if u < 4 and not first:
                yield ("WO", p - 1, u)
            if 4 <= u < 8 and p + 1 < pairs:
                yield ("v", p + 1, u - 4)
            if u < 11 and (u >= 3 or not first):
                yield ("PV", g - 3)
            if u >= 8:
                yield ("WO", p, u - 8)
            if u == 10:
                yield ("nS", norm, 0)
            if u == 11:
                yield ("nX", norm, 0)
            if u >= 8 and p + 1 < pairs:
                yield first_keys(p + 1)[u - 8]
            if not last and u < 8:
                yield ("qk"[u // 2 % 2], p + 1, u // 4, u % 2)
            if u == 0 and p > 0:
                yield ("w", f"L2p{p}_1", 2, 2)
            if u == 2 and p + 1 < pairs:
                yield ("w", f"L2p{p + 1}_1", 0, 2)
            if 4 <= u < 8 and p + 2 < pairs:
                yield ("w", f"L2p{p + 2}_0", u - 4, 1)
            if 4 <= u < 8 and p == pairs - 1:
                yield ("w", f"L2w1_{u // 6}", 2 * (u % 2), 2)
        if last and not p == pairs - 1:
            yield from start(p + 1)
    yield from norm_end("L2nm")


QK_AT = {}
for _n, _e in enumerate(e for e in [*first_keys(0), *wide_order()] if e[0] in ("q", "k")):
    QK_AT[_e] = _n + 1


def mlp_order(name):
    after = {"L1": "L2n1", "L2": "L3n1", "L3": None}[name]
    for c in range(B // 2):
        for f2 in range(FT // 2):
            yield ("up", c, f2)
            if f2 == 0 and c > 0:
                yield ("down", c - 1)
            if c == 0 and f2 in (0, 1):
                yield ("w", f"{name}w2_{f2}", 0, PARTS)
            if name == "L1" and c == 1 and f2 in (0, 2):
                yield ("w", f"L3sel{f2 // 2}", 0, PARTS)
    if name == "L1":
        yield ("w", "L2p0_0", 0, PARTS)
        yield ("w", "L2p0_1", 0, 2)
        yield ("w", "L2p0_1", 2, 2)
    if name == "L2":
        yield ("w", "L3att0", 0, PARTS)
        yield ("w", "L3att1", 0, PARTS)
    if after:
        yield ("nS", after, 0)
        yield ("nX", after, 0)
    yield ("down", B // 2 - 1)
    if name == "L1":
        yield from first_keys(0)
    if after:
        yield from norm_end(after)


def build(nc, x, ctx_in, mask_t, mask_s2, mask_s3, packs, cols, rows, l2rows, inds, ident_in, out):
    stack = ExitStack()
    with stack:
        def sb(name, shape, dt=F32):
            return stack.enter_context(nc.sbuf_tensor(name, shape, dt))

        def sem(name):
            return stack.enter_context(nc.semaphore(name))

        ps = stack.enter_context(nc.psum_tensor("ps", [P, 8, 512], F32))
        S_BANK, T_BANK, O_BANK, J_BANK = 0, 2, 4, 6
        SCORE_BANKS = {"L0": (0, 1, 5), "L1": (0, 1), "L3": (0, 1)}
        OUT_BANKS = {"L0": (4,), "L1": (4, 5), "L3": (4, 5)}
        X = sb("X", [P, B, D])
        XH = sb("XH", [P, B, D])
        wraw = sb("wraw", [P, 2, PACK])
        ident = sb("ident", [P, P])
        col = sb("col", [P, NCOLS])
        row = sb("row", [P, ROW_SET, D])
        prob = sb("prob", [P, 3, 512])
        probT = sb("probT", [P, 3, 512])
        nmax = sb("nmax", [P, 4, 4])
        psums = sb("psums", [P, 4, 4])
        prec = sb("prec", [P, 4, 4])
        st6 = sb("st6", [P, B, 6])
        mv = sb("mv", [P, B, 2])
        sd = sb("sd", [P, 6, B])
        eps = sb("eps", [P, 2])
        q0b = sb("q0b", [P, 1])
        l2q = sb("l2q", [P, 2, H])
        bvr = sb("bvr", [P, 2, 2, D])
        ct = [sb(f"ct{i}", [P, KT, B, P], F32R) for i in range(2)]
        ht = [sb(f"ht{i}", [P, KT, B, P], F32R) for i in range(2)]
        sel = sb("sel", [P, 16, P], F32R)
        indr = sb("indr", [1, 2, P], F32R)
        mb13 = sb("mb13", [1, B * P], F32R)
        mt8 = sb("mt8", [P, B, D], U8)
        mraw3 = sb("mraw3", [1, B * P], U8)
        fs = sb("fs", [P, 10264])
        rs = sb("rs", [P, 13312], F32R)

        def carve(t, at, shape):
            n = int(np.prod(shape))
            names = "abcdef"[:len(shape)]
            kw = {c: k for c, k in zip(names[1:], shape[1:])}
            v = t[:, at:at + n]
            if len(shape) > 1:
                v = v.rearrange(f"p ({' '.join(names)}) -> p {' '.join(names)}", **kw)
            return v, at + n

        def carve2(t, at, shape):
            h, at = carve(t, at, shape)
            l, at = carve(t, at, shape)
            return [h, l], at

        A0, A1, A2 = 0, 4096, 8192
        ksA, _ = carve(rs, A0, [2, 2048])
        ksB, _ = carve(rs, A1, [2, 2048])
        awA, _ = carve2(rs, A1, [4, KT, D])
        awB, _ = carve2(rs, A0, [4, KT, D])
        ks = {"L0": ksA, "L1": ksA, "L3": ksB}
        aw = {"L1": awA, "L3": awB}
        qs, o = carve(rs, A2, [2, 512])
        dq, o = carve2(rs, o, [2, D])
        dk, o = carve2(rs, o, [2, 512])
        uu, o = carve2(rs, o, [2, 2, P])
        assert o <= 13312
        mb0 = ht[1][0:1].rearrange("p f b n -> p (f b n)")
        vt, o = carve(fs, 0, [2, 2, 2, H, 32])
        ms, o = carve(fs, o, [2, B, D])
        xq, o = carve(fs, o, [D])
        w0, o = carve(fs, o, [3, P])
        msq, o = carve(fs, o, [D])
        xs, _ = carve(fs, 8192, [3, 512])
        assert o <= 10264
        pw = [carve2(rs, A0, [4, 512])[0], carve2(rs, A1, [4, 512])[0]]
        cc, o = carve2(rs, A2, [2, B, P])
        assert o <= 13312
        qT, o = carve(fs, 0, [3, B, P])
        kT, o = carve(fs, o, [3, B, P + 1])
        v2, o = carve(fs, o, [2, B, 2, P])
        assert o <= 10264
        mw1 = {m: carve2(rs, A1 if m == "L3" else A0, [KT, FF])[0] for m in ("L1", "L2", "L3")}
        mw2 = {m: carve2(rs, A0 if m == "L3" else A1, [FT, D])[0] for m in ("L1", "L2", "L3")}
        gg, o = carve2(rs, A2, [GT, D])
        assert o <= 13312
        gf, _ = carve(fs, 0, [2, 512])

        c_in, d_in = sem("columns_and_masks_loaded"), sem("rows_and_identity_loaded")
        x0_in, x_in = sem("first_two_sequences_loaded"), sem("other_sequences_loaded")
        rowb_in = sem("second_rows_loaded")
        l_in = [sem(f"pack_loaded{i}") for i in range(2)]
        bv_in = [sem(f"l2_rows_loaded{i}") for i in range(2)]
        w_hi = [sem(f"weight_hi_written{i}") for i in range(2)]
        w_lo = [sem(f"weight_pack_taken{i}") for i in range(2)]
        w_v = sem("l2_v_weights_split")
        jm = sem("general_bank_filled")
        a_setup, g_setup = sem("scalar_setup"), sem("off_diagonal_zeroed")
        eps_ok = sem("eps_set")
        vzero = sem("values_zeroed")
        l0stat, l0sq, l0n = sem("l0_stats"), sem("l0_sqrt"), sem("l0_norm_factors")
        l0mul, g_link = sem("l0_x_times_deviation"), sem("pool_chain")
        xn_done = sem("l0_x_normalised")
        l0var, l0dev, fin = sem("l0_variance"), sem("l0_deviation"), sem("l0_result")
        ybias = sem("residual_biased")
        dch = sem("vector_chain")
        out_done = sem("output_written")
        A = {ph: {n: sem(f"{ph}_{n}") for n in ["hi", "dense", "stA", "stD", "vals", "sm", "mx", "ex", "rc", "nm", "tm", "teA", "teD",
                                                "pm", "oeA", "mask"] + (["xq"] if ph == "L0" else ["oeD", "done"])} for ph in ATT}
        L = {n: sem(f"L2_{n}") for n in ("qk", "v", "bv", "sm", "mx", "ex", "rc", "nm", "tm", "teA", "teD", "pm", "ch", "cl", "acc")}
        M = {m: {n: sem(f"{m}_{n}") for n in ("gelu", "lo", "out")} for m in ("L1m", "L2m", "L3m")}
        N = {n: {k: sem(f"{n}_{k}") for k in (["hi", "lo"] if n in ("ctx", "lat") else ["stat", "sq", "r", "xh", "a", "lo"])}
             for n in NORMS}

        block = stack.enter_context(nc.Block())

        def C(name, i=0):
            return col[:, COLS[name][0] + i:COLS[name][0] + i + 1]

        def R(name):
            return row[:, ROWS.index(name) % ROW_SET, :]

        def copied(eng, ph, i):
            n = TE_ACT[ph]
            if i % n == 0:
                eng.wait_ge(A[ph]["teA"], i // n + 1)
            else:
                eng.wait_ge(A[ph]["teD"], i - i // n)

        def taken(eng, name):
            n = PACK_AT[name]
            eng.wait_ge(w_lo[n % 2], n // 2 + 1)

        def loaded(eng, name):
            n = PACK_AT[name]
            eng.wait_ge(l_in[n % 2], 16 * (n // 2 + 1))

        def scaled(name):
            return xs if name in ("L1r", "L3nm") else probT

        def pack_dst(name, part, parts):
            half = int(name[-1])
            base = name[:-1]
            at = half * PACK + part * (PACK // PARTS)
            cut = slice(at, at + parts * (PACK // PARTS))
            if base == "L0w":
                return [w0.rearrange("p a b -> p (a b)")]
            if base.endswith("sel"):
                return [sel[:, :, :].rearrange("p a b -> p (a b)")[:, cut]]
            if base.endswith("att"):
                return [t.rearrange("p a b c -> p (a b c)")[:, cut] for t in aw[base[:2]]]
            if base[2] == "p":
                return [t.rearrange("p a b -> p (a b)")[:, cut] for t in pw[int(base[3:-1]) % 2]]
            return [t.rearrange("p a b -> p (a b)")[:, cut] for t in (mw1 if "w1" in base else mw2)[base[:2]]]

        @block.sync
        def _(sp):
            def both_inputs(b0, b1, s):
                sp.dma_start(X[:, b0:b1, :], x[b0:b1].rearrange("b p d -> p b d")).then_inc(s, 16)
                sp.dma_start(XH[:, b0:b1, :], ctx_in[b0:b1].rearrange("b p d -> p b d")).then_inc(s, 16)

            both_inputs(0, 2, x0_in)
            for n, name in enumerate(PACKS):
                if n >= 2:
                    sp.wait_ge(w_lo[n % 2], n // 2)
                sp.dma_start(wraw[:, n % 2, :], packs[n]).then_inc(l_in[n % 2], 16)
                if n == 0:
                    sp.dma_start(col[:, :], cols).then_inc(c_in, 16)
                    sp.dma_start(prob[0:1, 2, 0:2 * P], inds).then_inc(c_in, 16)
                    sp.dma_start(mt8[:, :, :].rearrange("p b d -> p (b d)"), mask_t[0].partition_broadcast(P)).then_inc(c_in, 16)
                    sp.dma_start(probT[0:1, :, :].bitcast(I32).rearrange("p a b -> p (a b)")[:, 0:B * P], mask_s2).then_inc(c_in, 16)
                if n == 2:
                    sp.dma_start(row[:, :, :].rearrange("p r d -> p (r d)"), rows[0].partition_broadcast(P)).then_inc(d_in, 16)
                    sp.dma_start(ident[:, :], ident_in).then_inc(d_in, 16)
                    sp.dma_start(mraw3[:, :], mask_s3).then_inc(d_in, 16)
                    both_inputs(2, B, x_in)
                if name[:3] == "L2p" and name[-1] == "0":
                    i = int(name[3:-2])
                    if i >= 2:
                        sp.wait_ge(L["v"], 4 * (i - 1))
                    sp.dma_start(bvr[:, i % 2, :, :].rearrange("p a d -> p (a d)"), l2rows[i].partition_broadcast(P))\
                      .then_inc(bv_in[i % 2], 16)
                if name == "L2p7_1":
                    sp.wait_ge(ybias, 3)
                    sp.dma_start(row[:, :, :].rearrange("p r d -> p (r d)"), rows[1].partition_broadcast(P)).then_inc(rowb_in, 16)
            sp.wait_ge(M["L3m"]["out"], B // 2)
            sp.dma_start(out.rearrange("b p d -> p b d"), X[:, :, :]).then_inc(out_done, 16)
            sp.wait_ge(out_done, 16)

        @block.tensor
        def _(pe):
            filled = [0]
            freed_by = [[], []]

            def j_bank():
                i = filled[0] % 2
                for s, v in freed_by[i]:
                    pe.wait_ge(s, v)
                return ps[:, J_BANK + i, :]

            def j_full(last, *frees):
                last.then_inc(jm, 1)
                freed_by[filled[0] % 2] = frees
                filled[0] += 1

            def three(dst, w, m, start, stop):
                nc.tensor.matmul(dst, w[0], m[1], start=start, stop=False)
                nc.tensor.matmul(dst, w[1], m[0], start=False, stop=False)
                return nc.tensor.matmul(dst, w[0], m[0], start=False, stop=stop)

            def both(f):
                return [f(0), f(1)]

            def norm_step(e, name, k):
                if e != "nT":
                    return
                n = N[name]
                bank = j_bank()
                if name == "ctx":
                    pe.wait_ge(x0_in, 32)
                    pe.wait_ge(x_in, 32)
                elif name == "lat":
                    pe.wait_ge(fin, 2 * k + 2)
                else:
                    pe.wait_ge(n["xh"], 2 * k + 2)
                src = X if name == "lat" else XH
                for q in range(2):
                    for f in range(KT):
                        last = nc.tensor.transpose(bank[:, (2 * q + f) * P:(2 * q + f + 1) * P],
                                                   src[:, 2 * k + q, f * P:(f + 1) * P], ident[:, :])
                j_full(last, (n["lo" if name in ("ctx", "lat") else "a"], k + 1))

            def dense(ph, e, it, k, a):
                if ph == "L0":
                    if it == 0:
                        pe.wait_ge(x0_in, 32)
                    if it == 2:
                        pe.wait_ge(x_in, 32)
                    if it == 0 and e == "dq":
                        taken(pe, "L0w0")
                    bank = j_bank()
                    if e == "dq":
                        nc.tensor.matmul(bank[:, 0:D], w0[:, 0, :], X[:, it, :], start=True, stop=True)
                        j_full(nc.tensor.matmul(bank[:, D:2 * D], w0[:, 1, :], XH[:, it, :], start=True, stop=True), (a["dense"], it + 1))
                        return
                    for t in range(2):
                        last = nc.tensor.matmul(bank[:, t * P:(t + 1) * P], XH[:, it, t * P:(t + 1) * P], w0[:, 2, :],
                                                start=True, stop=True)
                    j_full(last, (a["vals"], it + 1))
                    return
                if e == "dq" or (e, k, ph) == ("dk", 0, "L1"):
                    if it == 0:
                        taken(pe, ph + "att0")
                        taken(pe, ph + "att1")
                    pe.wait_ge(N["lat" if ph == "L1" else "L3n1"]["lo"], it + 1)
                bb = slice(2 * it, 2 * it + 2)
                W = lambda kind, f, t: both(lambda i: aw[ph][i][:, kind, f, t * P:(t + 1) * P])
                bank = j_bank()
                for s in range(2):
                    dst = bank[:, s * D:(s + 1) * D]
                    for f in range(KT):
                        if e == "dq":
                            last = three(dst, W(0, f, s), both(lambda i: ht[i][:, f, bb, :]), f == 0, f == KT - 1)
                        elif e == "dk" and ph == "L1":
                            src = (ct, ht)[s]
                            last = three(dst, W(1, f, k), both(lambda i: src[i][:, f, bb, :]), f == 0, f == KT - 1)
                        elif e == "dk":
                            last = three(dst, W(1, f, s), both(lambda i: ct[i][:, f, bb, :]), f == 0, f == KT - 1)
                        else:
                            src, b = ((ct, ht)[s], 2 * it + k) if ph == "L1" else (ct, 2 * it + s)
                            last = three(dst, both(lambda i: src[i][:, f, b, :]), both(lambda i: aw[ph][i][:, 2, f, :]), f == 0, f == KT - 1)
                if e == "dv":
                    j_full(last, (a["vals"], (2 * it + k if ph == "L1" else it) + 1))
                else:
                    n = dense_at(ph, it, e, k)
                    j_full(last, (a["hi"], n), (a["dense"], n))

            def prep(ph, e, s, gi, a):
                it, m = divmod(s, STEPS)
                if s == 0 and e == "pq":
                    pe.wait_ge(a["mask"], 1)
                    taken(pe, ph + "sel0")
                    taken(pe, ph + "sel1")
                pe.wait_ge(a["dense"], dense_at(ph, it, "dq", 0) if e == "pq" else dense_at(ph, it, "dk", m // 2 if ph == "L1" else 0))
                nA, nD = ATT[ph]["stack_a"], ATT[ph]["stack_d"]
                bank = j_bank()
                if ph == "L0":
                    for i in range(2):
                        nc.tensor.matmul(bank[:, 0:D], sel[:, 4 * m + i, :], dq[i][:, 0, :], start=i == 0, stop=i == 1)
                    for i in range(2):
                        nc.tensor.matmul(bank[:, D:2 * D], sel[:, 4 * m + 2 + i, :], dk[i][:, 0, 0:D], start=i == 0, stop=False)
                    j_full(nc.tensor.matmul(bank[:, D:2 * D], indr[:, 0, :], mb0[:, it * D:(it + 1) * D], start=False, stop=True),
                           (a["stA"], nA * (s + 1)), (a["stD"], s + 1))
                    return
                if e == "pq":
                    for gi in range(2):
                        g = 2 * m + gi
                        for i in range(2):
                            last = nc.tensor.matmul(bank[:, gi * D:(gi + 1) * D], sel[:, 4 * (g % 4) + i, :], dq[i][:, g // 4, :],
                                                    start=i == 0, stop=i == 1)
                    j_full(last, (a["stA"], nA * s + 1))
                    return
                for g in [2 * m + gi] if ph == "L1" else [2 * m, 2 * m + 1]:
                    n, dst = (512, bank) if ph == "L1" else (D, bank[:, (g % 2) * D:(g % 2 + 1) * D])
                    for i in range(2):
                        nc.tensor.matmul(dst, sel[:, 4 * (g % 4) + 2 + i, :], dk[i][:, g // 4, 0:n], start=i == 0, stop=False,
                                         skip_group_check=True)
                    last = nc.tensor.matmul(dst[:, 0:D], indr[:, 1, :], mb13[:, 2 * it * P:(2 * it + 2) * P],
                                            start=False, stop=True, skip_group_check=True)
                j_full(last, (a["stA"], nA * s + 2 + gi), (a["stD"], nD * s + 1 + gi))

            def attention(ph):
                c, a = ATT[ph], A[ph]
                U, KTL = c["units"], c["key_tiles"]
                nh = 4 // U
                for e, i, *k in att_order(ph):
                    if e in ("dq", "dk", "dv"):
                        dense(ph, e, i, k[0], a)
                    elif e in ("pq", "pk"):
                        prep(ph, e, i, k[0], a)
                    elif e in ("nS", "nX", "nT"):
                        norm_step(e, i, k[0])
                    elif e == "S":
                        s, r = divmod(i, 2 * U)
                        im, k = divmod(r, U)
                        if r == 0:
                            pe.wait_ge(a["stA"], c["stack_a"] * (s + 1))
                            pe.wait_ge(a["stD"], c["stack_d"] * (s + 1))
                        n = len(SCORE_BANKS[ph])
                        if i >= n:
                            pe.wait_ge(a["ex"], i - n + 1)
                        bank = ps[:, SCORE_BANKS[ph][i % n], :]
                        if ph == "L0":
                            last = nc.tensor.matmul(bank, qs[:, s % 2, im * P:(im + 1) * P], ks[ph][:, s % 2, k * 512:(k + 1) * 512],
                                                    start=True, stop=True)
                        elif ph == "L1":
                            last = nc.tensor.matmul(bank, qs[:, s % 2, k * D + im * P:k * D + (im + 1) * P],
                                                    ks[ph][:, s % 2, (2 * k + im) * 512:(2 * k + im + 1) * 512], start=True, stop=True)
                        else:
                            for g in range(2):
                                last = nc.tensor.matmul(bank[:, g * D:(g + 1) * D], qs[:, s % 2, g * D + im * P:g * D + (im + 1) * P],
                                                        ks[ph][:, s % 2, (2 * g + im) * D:(2 * g + im + 1) * D], start=True, stop=True)
                        last.then_inc(a["sm"], 1)
                    elif e == "T":
                        if ph == "L0" and i == 0:
                            pe.wait_ge(d_in, 16 * 3)
                        pe.wait_ge(a["nm"], i + 1)
                        if i >= 2:
                            copied(pe, ph, i - 2)
                        for k in range(4):
                            last = nc.tensor.transpose(ps[:, T_BANK + i % 2, k * P:(k + 1) * P], prob[:, i % 3, k * P:(k + 1) * P],
                                                       ident[:, :])
                        last.then_inc(a["tm"], 1)
                    elif e == "PV":
                        it, r = divmod(i, 2 * STEPS)
                        m, im = divmod(r, 2)
                        u1 = (i + 1) * U - 1
                        for u in range(u1 - U + 1, u1 + 1):
                            copied(pe, ph, u)
                        if m == 0:
                            pe.wait_ge(a["vals"], 2 * it + im + 1 if ph == "L1" else it + 1)
                            n = len(OUT_BANKS[ph])
                            if it >= n and im == 0:
                                pe.wait_ge(a["oeA" if ph == "L0" else "oeD"], it - n + 1)
                        bank = ps[:, OUT_BANKS[ph][it % len(OUT_BANKS[ph])], im * D:(im + 1) * D]
                        begin = m == 0 and im == 0
                        for st in range(2 if ph == "L0" else 1):
                            for t in range(KTL):
                                for q in range(4):
                                    slot = (i * U + q // nh) % 3
                                    c0 = ((q % nh) * KTL + t) * P
                                    if ph == "L0":
                                        v = vt[:, it % 2, st, t, 4 * q + m, :]
                                        dst = bank[32 * q:32 * q + 32, st * P:(st + 1) * P]
                                        first, stop = (begin and t == 0 and st == 0), (m == 3 and t == 1)
                                    else:
                                        v = vt[:, it % 2, im, t, 4 * m + q, :]
                                        dst = bank[32 * q:32 * q + 32, (m // 2) * P:(m // 2 + 1) * P]
                                        first, stop = (begin and t == 0), (m % 2 == 1 and t == KTL - 1)
                                    last = nc.tensor.matmul(dst, v, probT[:, slot, c0:c0 + P], start=first, stop=stop,
                                                            skip_group_check=True)
                        last.then_inc(a["pm"], 1)
                    elif e == "WO" and ph != "L0":
                        pe.wait_ge(a["oeD"], i + 1)
                        bank = j_bank()
                        for im in range(2):
                            for t in range(2):
                                last = three(bank[:, im * D:(im + 1) * D], both(lambda k: uu[k][:, im, t, :]),
                                             both(lambda k: aw[ph][k][:, 3, t, :]), t == 0, t == 1)
                        j_full(last, (a["done"], i + 1))

            def wide(order):
                for e in order:
                    if e[0] in ("nS", "nX", "nT"):
                        norm_step(*e)
                    elif e[0] in ("q", "k"):
                        kind, p, hd, ch = e
                        if hd == 0 and ch == 0:
                            taken(pe, f"L2p{p}_0")
                        if kind == "q" and p % PAIRS == 0:
                            pe.wait_ge(N[f"L2n{p // PAIRS + 1}"]["lo"], 2 * ch + 2)
                        src, kd = (ct, 1) if kind == "k" else (ht, 0)
                        bank = j_bank()
                        for f in range(KT):
                            last = three(bank, both(lambda i: pw[p % 2][i][:, kd, f * D + hd * P:f * D + (hd + 1) * P]),
                                         both(lambda i: src[i][:, f, 4 * ch:4 * ch + 4, :]), f == 0, f == KT - 1)
                        j_full(last, (L["qk"], QK_AT[e]))
                    elif e[0] == "v":
                        _, p, k = e
                        pe.wait_ge(w_v, p + 1)
                        bank = j_bank()
                        for b in range(2):
                            for f in range(KT):
                                last = three(bank[:, b * D:(b + 1) * D], both(lambda i: ct[i][:, f, 2 * k + b, :]),
                                             both(lambda i: pw[p % 2][i][:, 2, f * D:(f + 1) * D]), f == 0, f == KT - 1)
                        j_full(last, (L["v"], 4 * p + k + 1))
                    elif e[0] == "S":
                        g = e[1]
                        p, r = divmod(g, 8)
                        hd, b2 = divmod(r, 4)
                        hh = 2 * p + hd
                        pe.wait_ge(L["qk"], max(QK_AT["q", p, hd, 1], QK_AT["k", p, hd, 1]))
                        if g >= 2:
                            pe.wait_ge(L["ex"], g - 1)
                        for b in range(2):
                            last = nc.tensor.matmul(ps[:, S_BANK + g % 2, b * D:b * D + P + 1], qT[:, hh % 3, 2 * b2 + b, :],
                                                    kT[:, hh % 3, 2 * b2 + b, :], start=True, stop=True)
                        last.then_inc(L["sm"], 1)
                    elif e[0] == "T":
                        g = e[1]
                        pe.wait_ge(L["nm"], g + 1)
                        if g >= 2:
                            pe.wait_ge(L["teD" if g % 2 else "teA"], g // 2)
                        for b in range(2):
                            last = nc.tensor.transpose(ps[:, T_BANK + g % 2, b * P:(b + 1) * P], prob[:, g % 3, b * D:b * D + P],
                                                       ident[:, :])
                        last.then_inc(L["tm"], 1)
                    elif e[0] == "PV":
                        g = e[1]
                        p, r = divmod(g, 8)
                        hd, b2 = divmod(r, 4)
                        pe.wait_ge(L["teD" if g % 2 else "teA"], g // 2 + 1)
                        if r == 0:
                            pe.wait_ge(L["v"], 4 * (p + 1))
                        if g >= 2:
                            pe.wait_ge(L["cl"], g - 1)
                        for b in range(2):
                            last = nc.tensor.matmul(ps[:, O_BANK + g % 2, b * P:(b + 1) * P], v2[:, p % 2, 2 * b2 + b, hd, :],
                                                    probT[:, g % 3, b * P:(b + 1) * P], start=True, stop=True)
                        last.then_inc(L["pm"], 1)
                    elif e[0] == "WO":
                        _, p, b2 = e
                        pe.wait_ge(L["cl"], 8 * p + 4 + b2 + 1)
                        if b2 == 0:
                            taken(pe, f"L2p{p}_1")
                        bank = j_bank()
                        for b in range(2):
                            for hd in range(2):
                                last = three(bank[:, b * D:(b + 1) * D], both(lambda i: cc[i][:, hd, 2 * b2 + b, :]),
                                             both(lambda i: pw[p % 2][i][:, 3, hd * D:(hd + 1) * D]), hd == 0, hd == 1)
                        j_full(last, (L["acc"], 4 * p + b2 + 1))

            def mlp(name, nrm):
                m = M[name + "m"]
                for e in mlp_order(name):
                    if e[0] in ("nS", "nX", "nT"):
                        norm_step(*e)
                    elif e[0] == "k":
                        wide([e])
                    elif e[0] == "up":
                        _, c, f2 = e
                        if c == 0 and f2 == 0:
                            taken(pe, name + "w1_0")
                            taken(pe, name + "w1_1")
                        pe.wait_ge(nrm["lo"], c + 1)
                        bank = j_bank()
                        for fi in range(2):
                            f = 2 * f2 + fi
                            for k in range(KT):
                                last = three(bank[:, fi * D:(fi + 1) * D], both(lambda i: mw1[name][i][:, k, f * P:(f + 1) * P]),
                                             both(lambda i: ht[i][:, k, 2 * c:2 * c + 2, :]), k == 0, k == KT - 1)
                        j_full(last, (m["gelu"], (FT // 2) * c + f2 + 1))
                    elif e[0] == "down":
                        c = e[1]
                        if c == 0:
                            taken(pe, name + "w2_0")
                            taken(pe, name + "w2_1")
                        pe.wait_ge(m["lo"], (FT // 2) * (c + 1))
                        bank = j_bank()
                        for b in range(2):
                            for f in range(FT):
                                last = three(bank[:, b * D:(b + 1) * D], both(lambda i: gg[i][:, (FT * c + f) % GT, b * P:(b + 1) * P]),
                                             both(lambda i: mw2[name][i][:, f, :]), f == 0, f == FT - 1)
                        j_full(last, (m["out"], c + 1))

            attention("L0")
            attention("L1")
            mlp("L1", N["L1r"])
            wide(wide_order())
            mlp("L2", N["L2nm"])
            attention("L3")
            mlp("L3", N["L3nm"])

        @block.scalar
        def _(act):
            taken = [0]

            def j_take():
                j = taken[0]
                taken[0] += 1
                act.wait_ge(jm, j + 1)
                return ps[:, J_BANK + j % 2, :]

            def j_skip():
                taken[0] += 1

            def take(name, part=0, parts=PARTS):
                if name not in HI_AT:
                    return
                loaded(act, name)
                n = PACK_AT[name]
                at = part * (PACK // PARTS)
                nc.scalar.copy(pack_dst(name, part, parts)[0], wraw[:, n % 2, at:at + parts * (PACK // PARTS)])\
                  .then_inc(w_hi[n % 2], parts)

            def norm_step(e, name, k):
                n = N[name]
                affine = AFFINE.get(name)
                if e == "nS":
                    act.wait_ge(n["stat"], k + 1)
                    g = slice(2 * CHUNKS[k][0], 2 * CHUNKS[k][-1] + 2)
                    nc.scalar.activation(sd[:, 1, g], sd[:, 0, g], ACT.Sqrt,
                                         bias=eps[:, 1:2] if name == "L1r" else eps[:, 0:1]).then_inc(n["sq"], 1)
                if e != "nT":
                    return
                src = j_take().rearrange("p (q f n) -> p q f n", q=2, f=KT)
                if affine and k >= 3:
                    act.wait_ge(n["lo"], k - 2)
                for f in range(KT):
                    if not affine:
                        dst = (ct if name == "ctx" else ht)[0]
                        last = nc.scalar.copy(dst[:, f, 2 * k:2 * k + 2, :], src[:, :, f, :])
                        continue
                    dst = scaled(name)[:, k % 3, f * D:(f + 1) * D].rearrange("p (q n) -> p q n", q=2)
                    if affine[1]:
                        last = nc.scalar.activation(dst, src[:, :, f, :], ACT.Identity, scale=C(affine[0], f), bias=C(affine[1], f))
                    else:
                        last = nc.scalar.mul(dst, src[:, :, f, :], C(affine[0], f))
                last.then_inc(n["a" if affine else "hi"], 1)

            def attention(ph):
                c, a = ATT[ph], A[ph]
                U, keys = c["units"], c["keys"]
                nh = 4 // U
                for e, i, *k in att_order(ph):
                    if e == "dq" and ph == "L0":
                        bank = j_take()
                        if i > 0:
                            act.wait_ge(a["dense"], i)
                        nc.scalar.activation(xq, bank[:, 0:D], ACT.Identity, bias=q0b[:, :], scale=Q0_SCALE).then_inc(a["xq"], 1)
                        nc.scalar.activation(dk[0][:, 0, 0:D], bank[:, D:2 * D], ACT.Identity, bias=C("L0k")).then_inc(a["hi"], 1)
                    elif e == "w":
                        take(i)
                    elif e in ("nS", "nX", "nT"):
                        norm_step(e, i, k[0])
                    elif e == "fin":
                        act.wait_ge(l0var, 2 * i + 2)
                        nc.scalar.activation(ms[:, 1, 2 * i:2 * i + 2, :], ms[:, 1, 2 * i:2 * i + 2, :], ACT.Sqrt).then_inc(l0dev, 1)
                    elif e == "sq":
                        act.wait_ge(l0stat, 1)
                        act.wait_ge(eps_ok, 1)
                        nc.scalar.activation(sd[:, 1, :], sd[:, 0, :], ACT.Sqrt, bias=eps[:, 0:1]).then_inc(l0sq, 1)
                    elif e == "dv" or e == "WO" and ph != "L0":
                        j_skip()
                    elif e == "dk" and ph == "L1":
                        nc.scalar.activation(dk[0][:, k[0], :], j_take(), ACT.Identity, bias=C("L1k", k[0])).then_inc(a["hi"], 1)
                    elif e in ("dq", "dk"):
                        bank = j_take()
                        dst = (dq if e == "dq" else dk)[0]
                        for t in range(2):
                            last = nc.scalar.activation(dst[:, t, 0:D], bank[:, t * D:(t + 1) * D], ACT.Identity, bias=C(ph + e[1], t))
                        last.then_inc(a["hi"], 1)
                    elif e == "pq":
                        if i >= 2:
                            act.wait_ge(a["sm"], 2 * U * (i - 1))
                        bank = j_take()
                        if ph == "L0":
                            if i < 2:
                                act.wait_ge(g_setup, 1)
                            nc.scalar.activation(qs[:, i % 2, 0:D], bank[:, 0:D], ACT.Identity, bias=C("ones0")).then_inc(a["stA"], 1)
                            for q in range(2):
                                last = nc.scalar.copy(ks[ph][32 * q:32 * q + 32, i % 2, q * D:(q + 1) * D], bank[32 * q:32 * q + 32, D:2 * D])
                            last.then_inc(a["stA"], 1)
                        else:
                            nc.scalar.activation(qs[:, i % 2, :], bank, ACT.Identity, bias=C("ones1")).then_inc(a["stA"], 1)
                    elif e == "pk":
                        if i >= 2:
                            act.wait_ge(a["sm"], 2 * U * (i - 1))
                        else:
                            act.wait_ge(g_setup, {"L1": 2, "L3": 3}[ph])
                        bank = j_take()
                        if ph == "L1":
                            src = bank[0:64, :].rearrange("p (s m n) -> p m s n", s=2, m=2)
                            dst = ks[ph][0:64, i % 2, k[0] * 1024:(k[0] + 1) * 1024].rearrange("p (m h s n) -> p m h s n", m=2, h=2, s=2)
                            nc.scalar.copy(dst[:, :, 0, :, :], src).then_inc(a["stA"], 1)
                        else:
                            for g in range(2):
                                src = bank[0:64, g * D:(g + 1) * D].rearrange("p (m n) -> p m n", m=2)
                                dst = ks[ph][0:64, i % 2, g * 512:(g + 1) * 512].rearrange("p (m h n) -> p m h n", m=2, h=2)
                                last = nc.scalar.copy(dst[:, :, 0, :], src)
                            last.then_inc(a["stA"], 1)
                    elif e == "S":
                        act.wait_ge(a["mx"], i + 1)
                        if i >= 3:
                            act.wait_ge(a["tm"], i - 2)
                        for h in range(nh):
                            last = nc.scalar.activation(prob[:, i % 3, h * keys:(h + 1) * keys],
                                                        ps[:, SCORE_BANKS[ph][i % len(SCORE_BANKS[ph])], h * keys:(h + 1) * keys], ACT.Exp,
                                                        bias=nmax[:, i % 4, h:h + 1], accum_out=psums[:, i % 4, h:h + 1])
                        last.then_inc(a["ex"], 1)
                    elif e == "T":
                        if i % TE_ACT[ph] == 0:
                            act.wait_ge(a["tm"], i + 1)
                            if i >= 3:
                                act.wait_ge(a["pm"], (i - 3) // U + 1)
                            nc.scalar.copy(probT[:, i % 3, :], ps[:, T_BANK + i % 2, :]).then_inc(a["teA"], 1)
                    elif e == "OUT":
                        act.wait_ge(a["pm"], 2 * STEPS * (i + 1))
                        bank = ps[:, OUT_BANKS[ph][i % len(OUT_BANKS[ph])], :]
                        if ph == "L0":
                            act.wait_ge(xn_done, i + 1)
                            nc.scalar.copy(ms[:, :, i, :].rearrange("p t (m n) -> p t m n", m=2),
                                           bank.rearrange("p (m t n) -> p t m n", m=2, t=2)).then_inc(a["oeA"], 1)
                        else:
                            if i > 0:
                                act.wait_ge(a["done"], i)
                            nc.scalar.copy(uu[0].rearrange("p m t n -> p (m t n)"), bank).then_inc(a["oeA"], 1)

            def wide(order):
                for e in order:
                    if e[0] in ("nS", "nX", "nT"):
                        norm_step(*e)
                    elif e[0] in ("q", "k"):
                        kind, p, hd, ch = e
                        layer, hh = p // PAIRS, 2 * p + hd
                        h = hh % H
                        bank = j_take()
                        if hh >= 3:
                            act.wait_ge(L["sm"], 4 * (hh - 2))
                        src = bank.rearrange("p (b n) -> p b n", b=4)
                        if kind == "q":
                            last = nc.scalar.activation(qT[:, hh % 3, 4 * ch:4 * ch + 4, :], src, ACT.Identity,
                                                        bias=l2q[:, layer, h:h + 1], scale=Q2_SCALE)
                        else:
                            nc.scalar.activation(kT[:, hh % 3, 4 * ch:4 * ch + 4, P:P + 1], ident[:, 0:4].unsqueeze(2), ACT.Identity,
                                                 bias=C(f"L2bk{layer + 1}", h), scale=0.0)
                            last = nc.scalar.activation(kT[:, hh % 3, 4 * ch:4 * ch + 4, 0:P], src, ACT.Identity,
                                                        bias=C(f"L2k{layer + 1}", h))
                        last.then_inc(L["qk"], 1)
                    elif e[0] in ("v", "WO"):
                        j_skip()
                    elif e[0] == "w":
                        take(*e[1:])
                    elif e[0] == "S":
                        g = e[1]
                        act.wait_ge(L["mx"], g + 1)
                        if g >= 3:
                            act.wait_ge(L["tm"], g - 2)
                        for k in range(2):
                            last = nc.scalar.activation(prob[:, g % 3, k * D:k * D + P + 1], ps[:, S_BANK + g % 2, k * D:k * D + P + 1],
                                                        ACT.Exp, bias=nmax[:, g % 4, k:k + 1], accum_out=psums[:, g % 4, k:k + 1])
                        last.then_inc(L["ex"], 1)
                    elif e[0] == "T":
                        g = e[1]
                        if g % 2 == 0:
                            act.wait_ge(L["tm"], g + 1)
                            if g >= 3:
                                act.wait_ge(L["pm"], g - 2)
                            nc.scalar.copy(probT[:, g % 3, 0:D], ps[:, T_BANK, 0:D]).then_inc(L["teA"], 1)
                    elif e[0] == "PV":
                        g = e[1]
                        p, r = divmod(g, 8)
                        hd, b2 = divmod(r, 4)
                        act.wait_ge(L["pm"], g + 1)
                        if p >= 1:
                            act.wait_ge(L["acc"], 4 * (p - 1) + b2 + 1)
                        nc.scalar.activation(cc[0][:, hd, 2 * b2:2 * b2 + 2, :],
                                             ps[:, O_BANK + g % 2, 0:D].rearrange("p (b n) -> p b n", b=2), ACT.Identity,
                                             bias=C(f"L2bv{p // PAIRS + 1}", (2 * p + hd) % H)).then_inc(L["ch"], 1)

            def mlp(name, func):
                m = M[name + "m"]
                for e in mlp_order(name):
                    if e[0] == "down":
                        j_skip()
                        continue
                    if e[0] == "w":
                        take(*e[1:])
                        continue
                    if e[0] in ("nS", "nX", "nT", "k"):
                        wide([e])
                        continue
                    k = (FT // 2) * e[1] + e[2]
                    bank = j_take()
                    if k >= 2:
                        act.wait_ge(m["lo"], k - 1)
                    for fi in range(2):
                        last = nc.scalar.activation(gf[:, k % 2, fi * D:(fi + 1) * D], bank[:, fi * D:(fi + 1) * D], func,
                                                    bias=C(name + "b1", 2 * e[2] + fi))
                    last.then_inc(m["gelu"], 1)

            act.wait_ge(c_in, 16 * 4)
            nc.scalar.mul(q0b[:, :], C("L0q"), Q0_SCALE).then_inc(a_setup, 1)
            for layer in range(2):
                at = COLS[f"L2q{layer + 1}"][0]
                nc.scalar.mul(l2q[:, layer, :], col[:, at:at + H], Q2_SCALE).then_inc(a_setup, 1)
            act.wait_ge(a_setup, 3)
            attention("L0")
            attention("L1")
            mlp("L1", ACT.Gelu_apprx_tanh)
            act.wait_ge(M["L1m"]["out"], B // 2)
            take("L2p1_0")
            wide(wide_order())
            mlp("L2", ACT.Gelu)
            attention("L3")
            mlp("L3", ACT.Gelu_apprx_tanh)

        @block.vector
        def _(dve):
            taken = [0]
            links = [0]

            def link(ins):
                links[0] += 1
                ins.then_inc(dch, 1)
                dve.wait_ge(dch, links[0])

            def j_take():
                j = taken[0]
                taken[0] += 1
                dve.wait_ge(jm, j + 1)
                return ps[:, J_BANK + j % 2, :]

            def j_skip():
                taken[0] += 1

            def f32(ap):
                return ap.bitcast(F32)

            def take(name, part=0, parts=PARTS):
                loaded(dve, name)
                n = PACK_AT[name]
                dst = pack_dst(name, part, parts)
                at = part * (PACK // PARTS)
                src = wraw[:, n % 2, at:at + dst[0].shape[-1]]
                if len(dst) == 1:
                    nc.vector.tensor_copy(dst[0], src).then_inc(w_lo[n % 2], 1)
                    return
                dve.wait_ge(w_hi[n % 2], HI_AT[name] + part + parts)
                last = nc.vector.tensor_tensor(dst[1], src, f32(dst[0]), ALU.subtract)
                if part + parts == PARTS:
                    last.then_inc(w_lo[n % 2], 1)
                elif name[:3] == "L2p" and name[-1] == "1" and part + parts == 2:
                    last.then_inc(w_v, 1)

            def stats(src, k, s, v):
                dve.wait_ge(s, v)
                for b in (2 * k, 2 * k + 1):
                    last = nc.vector.bn_stats(st6[:, b, :], src[:, b, :])
                if k >= B // 2 - 2:
                    link(last)

            def norm_step(e, name, k):
                n = N[name]
                if e in ("nS", "nX"):
                    src = XH if name == "L1r" else X
                    g = slice(2 * CHUNKS[k][0], 2 * CHUNKS[k][-1] + 2)
                if e == "nS":
                    for b in range(g.start, g.stop):
                        last = nc.vector.bn_aggr(mv[:, b, :], st6[:, b, :])
                    link(last)
                    if name == "L1r":
                        link(nc.vector.tensor_tensor(sd[:, 2, g], mv[:, g, 0], mv[:, g, 0], ALU.mult))
                        nc.vector.tensor_tensor(sd[:, 0, g], sd[:, 2, g], mv[:, g, 1], ALU.add).then_inc(n["stat"], 1)
                    else:
                        nc.vector.tensor_copy(sd[:, 0, g], mv[:, g, 1]).then_inc(n["stat"], 1)
                elif e == "nX":
                    dve.wait_ge(n["sq"], k + 1)
                    nc.vector.reciprocal(sd[:, 3, g], sd[:, 1, g]).then_inc(n["r"], 1)
                    dve.wait_ge(n["r"], k + 1)
                    for b in range(g.start, g.stop):
                        if name == "L1r":
                            i = nc.vector.tensor_scalar(XH[:, b, :], src[:, b, :], sd[:, 3, b:b + 1], None, ALU.mult)
                        else:
                            i = nc.vector.tensor_scalar(XH[:, b, :], src[:, b, :], mv[:, b, 0:1], sd[:, 3, b:b + 1],
                                                        ALU.subtract, ALU.mult)
                        i.then_inc(n["xh"], 1)
                else:
                    bank = j_take().rearrange("p (q f n) -> p q f n", q=2, f=KT)
                    hi, lo = ct if name == "ctx" else ht
                    two = slice(2 * k, 2 * k + 2)
                    if name in ("ctx", "lat"):
                        dve.wait_ge(n["hi"], k + 1)
                        for f in range(KT):
                            last = nc.vector.tensor_tensor(lo[:, f, two, :], bank[:, :, f, :], f32(hi[:, f, two, :]), ALU.subtract)
                    else:
                        dve.wait_ge(n["a"], k + 1)
                        xa = scaled(name)[:, k % 3, :].rearrange("p (f q n) -> p f q n", f=KT, q=2)
                        link(nc.vector.tensor_copy(hi[:, :, two, :], xa))
                        last = nc.vector.tensor_tensor(lo[:, :, two, :], xa, f32(hi[:, :, two, :]), ALU.subtract)
                    last.then_inc(n["lo"], 1)

            def x_stats(b):
                if b < B:
                    if b == 0:
                        link(nc.vector.tensor_reduce(sd[:, 2, :], mt8[:, :, :], AX.X, ALU.add))
                    if b == 2:
                        dve.wait_ge(x_in, 32)
                    link(nc.vector.tensor_tensor_reduce(ms[:, 0, b, :], X[:, b, :], mt8[:, b, :], 1.0, 0.0, ALU.mult, ALU.add,
                                                        sd[:, 3, b:b + 1]))
                    last = nc.vector.tensor_tensor_reduce(ms[:, 1, b, :], ms[:, 0, b, :], ms[:, 0, b, :], 1.0, 0.0, ALU.mult, ALU.add,
                                                          sd[:, 4, b:b + 1])
                    if b == B - 1:
                        link(last)
                    return
                link(nc.vector.reciprocal(sd[:, 2, :], sd[:, 2, :]))
                link(nc.vector.tensor_tensor(mv[:, :, 0], sd[:, 3, :], sd[:, 2, :], ALU.mult))
                link(nc.vector.tensor_tensor(sd[:, 4, :], sd[:, 4, :], sd[:, 2, :], ALU.mult))
                link(nc.vector.tensor_tensor(sd[:, 5, :], mv[:, :, 0], mv[:, :, 0], ALU.mult))
                link(nc.vector.tensor_tensor(sd[:, 4, :], sd[:, 4, :], sd[:, 5, :], ALU.subtract))
                nc.vector.tensor_scalar(sd[:, 0, :], sd[:, 4, :], 0.0, None, ALU.max).then_inc(l0stat, 1)

            def attention(ph):
                c, a = ATT[ph], A[ph]
                U, keys = c["units"], c["keys"]
                nh = 4 // U
                total = c["iters"] * STEPS * 2 * U

                def reciprocal(u):
                    dve.wait_ge(a["ex"], u + 1)
                    if u >= 4:
                        dve.wait_ge(a["nm"], u - 3)
                    nc.vector.reciprocal(prec[:, u % 4, 0:nh], psums[:, u % 4, 0:nh]).then_inc(a["rc"], 1)

                for e, i, *k in late(att_order(ph), LATE[ph]):
                    if e == "w":
                        take(i)
                    elif e in ("nS", "nX", "nT"):
                        norm_step(e, i, k[0])
                    elif e == "xs":
                        x_stats(i)
                    elif e == "fin":
                        if i == 0:
                            take("L1sel0")
                            take("L1sel1")
                        two = slice(2 * i, 2 * i + 2)
                        dve.wait_ge(l0mul, i + 1)
                        link(nc.vector.tensor_tensor(X[:, two, :], X[:, two, :], ms[:, 0, two, :], ALU.add))
                        nc.vector.tensor_tensor(X[:, two, :], X[:, two, :], mt8[:, two, :], ALU.mult).then_inc(fin, 2)
                    elif e == "sq":
                        dve.wait_ge(l0sq, 1)
                        nc.vector.reciprocal(sd[:, 3, :], sd[:, 1, :]).then_inc(l0n, 1)
                    elif e == "dq" and ph == "L0":
                        bank = j_take()
                        dve.wait_ge(a["hi"], i + 1)
                        nc.vector.scalar_tensor_tensor(dk[1][:, 0, 0:D], bank[:, D:2 * D], C("L0k"), f32(dk[0][:, 0, 0:D]),
                                                       ALU.add, ALU.subtract)
                        dve.wait_ge(a["xq"], i + 1)
                        link(nc.vector.tensor_copy(dq[0][:, 0, :], xq))
                        nc.vector.tensor_tensor(dq[1][:, 0, :], xq, f32(dq[0][:, 0, :]), ALU.subtract).then_inc(a["dense"], 1)
                    elif e == "dv" and ph == "L0":
                        bank = j_take()
                        if i == 0:
                            dve.wait_ge(vzero, 1)
                            dve.wait_ge(d_in, 16 * 3)
                        for t in range(2):
                            v = diag(vt[:, i % 2, 0, t, :, :].rearrange("p (q g) c -> p q (g c)", q=4))
                            src = bank[:, t * P:(t + 1) * P].rearrange("p (q g d) -> p q g d", q=4, g=4)
                            bias = R("L0v")[:, 0:P].rearrange("p (q g d) -> p q g d", q=4, g=4)
                            last = nc.vector.tensor_tensor(v, src, bias, ALU.add)
                        link(last)
                        for t in range(2):
                            v = diag(vt[:, i % 2, 0, t, :, :].rearrange("p (q g) c -> p q (g c)", q=4))
                            vv = diag(vt[:, i % 2, 1, t, :, :].rearrange("p (q g) c -> p q (g c)", q=4))
                            last = nc.vector.tensor_tensor(vv, v, v, ALU.mult)
                        last.then_inc(a["vals"], 1)
                    elif e == "dk" and ph == "L1":
                        bank = j_take()
                        dve.wait_ge(a["hi"], dense_at(ph, i, e, k[0]))
                        nc.vector.scalar_tensor_tensor(dk[1][:, k[0], :], bank, C("L1k", k[0]), f32(dk[0][:, k[0], :]),
                                                       ALU.add, ALU.subtract).then_inc(a["dense"], 1)
                    elif e in ("dq", "dk"):
                        bank = j_take()
                        dve.wait_ge(a["hi"], dense_at(ph, i, e, k[0]))
                        hi, lo = dq if e == "dq" else dk
                        for t in range(2):
                            last = nc.vector.scalar_tensor_tensor(lo[:, t, 0:D], bank[:, t * D:(t + 1) * D], C(ph + e[1], t),
                                                                  f32(hi[:, t, 0:D]), ALU.add, ALU.subtract)
                        last.then_inc(a["dense"], 1)
                    elif e == "dv":
                        if i == 0:
                            dve.wait_ge(vzero, {"L1": 2, "L3": 3}[ph])
                        bank = j_take()
                        for s in range(2):
                            im, t = (k[0], s) if ph == "L1" else (s, 0)
                            src = bank[:, s * D:(s + 1) * D].rearrange("p (t e q d) -> p e t q d", t=2, e=2, q=4)
                            bias = R(ph + "v").rearrange("p (t e q d) -> p e t q d", t=2, e=2, q=4)
                            dst = vt[:, i % 2, im, t, :, :].rearrange("p (t e q) c -> p e t q c", t=2, e=2)
                            for half in range(2):
                                last = nc.vector.tensor_tensor(dst[:, half, :, :, 16 * half:16 * half + 16], src[:, half], bias[:, half],
                                                               ALU.add)
                        last.then_inc(a["vals"], 1)
                    elif e == "pq" and ph != "L0":
                        j_skip()
                    elif e in ("pq", "pk"):
                        if i >= 2:
                            dve.wait_ge(a["sm"], 2 * U * (i - 1))
                        else:
                            dve.wait_ge(g_setup, {"L0": 1, "L1": 2, "L3": 3}[ph])
                        bank = j_take()
                        if ph == "L0":
                            dve.wait_ge(a["stA"], 2 * i + 1)
                            for q in range(2, 4):
                                last = nc.vector.tensor_copy(ks[ph][32 * q:32 * q + 32, i % 2, q * D:(q + 1) * D],
                                                             bank[32 * q:32 * q + 32, D:2 * D])
                        elif ph == "L1":
                            src = bank[64:128, :].rearrange("p (s m n) -> p m s n", s=2, m=2)
                            dst = ks[ph][64:128, i % 2, k[0] * 1024:(k[0] + 1) * 1024].rearrange("p (m h s n) -> p m h s n", m=2, h=2, s=2)
                            last = nc.vector.tensor_copy(dst[:, :, 1, :, :], src)
                        else:
                            for g in range(2):
                                src = bank[64:128, g * D:(g + 1) * D].rearrange("p (m n) -> p m n", m=2)
                                dst = ks[ph][64:128, i % 2, g * 512:(g + 1) * 512].rearrange("p (m h n) -> p m h n", m=2, h=2)
                                last = nc.vector.tensor_copy(dst[:, :, 1, :], src)
                        last.then_inc(a["stD"], 1)
                    elif e == "S":
                        dve.wait_ge(a["sm"], i + 1)
                        nc.vector.tensor_reduce(nmax[:, i % 4, 0:nh], ps[:, SCORE_BANKS[ph][i % len(SCORE_BANKS[ph])], :].rearrange("p (h n) -> p h n", h=nh),
                                                AX.X, ALU.max, negate=True).then_inc(a["mx"], 1)
                        if i >= 1:
                            reciprocal(i - 1)
                        if i == total - 1:
                            reciprocal(i)
                    elif e == "T":
                        if i % TE_ACT[ph]:
                            dve.wait_ge(a["tm"], i + 1)
                            if i >= 3:
                                dve.wait_ge(a["pm"], (i - 3) // U + 1)
                            nc.vector.tensor_copy(probT[:, i % 3, :], ps[:, T_BANK + i % 2, :]).then_inc(a["teD"], 1)
                    elif e == "OUT" and ph != "L0":
                        dve.wait_ge(a["oeA"], i + 1)
                        nc.vector.tensor_tensor(uu[1].rearrange("p m t n -> p (m t n)"), ps[:, OUT_BANKS[ph][i % len(OUT_BANKS[ph])], :],
                                                f32(uu[0].rearrange("p m t n -> p (m t n)")), ALU.subtract).then_inc(a["oeD"], 1)
                    elif e == "WO" and ph != "L0":
                        bank = j_take()
                        dve.wait_ge(ybias, 1 if ph == "L1" else 6)
                        dst = (XH if ph == "L1" else X)[:, 2 * i:2 * i + 2, :]
                        nc.vector.tensor_tensor(dst, bank.rearrange("p (b n) -> p b n", b=2), dst, ALU.add).then_inc(a["done"], 1)
                        stats(XH if ph == "L1" else X, i, a["done"], i + 1)

            def diag(v):
                return bass.AP(v.tensor, v.offset, [list(v.ap[0]), list(v.ap[1]), [40, 4], [1, 8]])

            def wide(order):
                for e in order:
                    if e[0] in ("nS", "nX", "nT"):
                        norm_step(*e)
                    elif e[0] in ("q", "k"):
                        j_skip()
                    elif e[0] == "w":
                        take(*e[1:])
                    elif e[0] == "v":
                        _, p, k = e
                        if k == 0:
                            dve.wait_ge(bv_in[p % 2], 16 * (p // 2 + 1))
                            link(nc.vector.tensor_tensor(bvr[:, p % 2, 0, :], bvr[:, p % 2, 0, :], bvr[:, p % 2, 1, :], ALU.subtract))
                        bank = j_take().rearrange("p (b n) -> p b n", b=2)
                        nc.vector.tensor_tensor(v2[:, p % 2, 2 * k:2 * k + 2, :, :].rearrange("p b h n -> p b (h n)"), bank,
                                                bvr[:, p % 2, 0:1, :].broadcast_to([P, 2, D]), ALU.add).then_inc(L["v"], 1)
                    elif e[0] == "WO":
                        _, p, b2 = e
                        bank = j_take().rearrange("p (b n) -> p b n", b=2)
                        if p % PAIRS == 0 and b2 == 0:
                            dve.wait_ge(ybias, 3 + p // PAIRS)
                        if p > 0:
                            dve.wait_ge(L["acc"], 4 * (p - 1) + b2 + 1)
                        dst = X[:, 2 * b2:2 * b2 + 2, :]
                        nc.vector.tensor_tensor(dst, bank, dst, ALU.add).then_inc(L["acc"], 1)
                        if p % PAIRS == PAIRS - 1:
                            stats(X, b2, L["acc"], 4 * p + b2 + 1)
                    elif e[0] == "S":
                        g = e[1]
                        dve.wait_ge(L["sm"], g + 1)
                        nc.vector.tensor_reduce(nmax[:, g % 4, 0:2],
                                                ps[:, S_BANK + g % 2, :].rearrange("p (h n) -> p h n", h=2)[:, :, 0:P + 1],
                                                AX.X, ALU.max, negate=True).then_inc(L["mx"], 1)
                    elif e[0] == "R":
                        g = e[1]
                        dve.wait_ge(L["ex"], g + 1)
                        if g >= 4:
                            dve.wait_ge(L["nm"], g - 3)
                        nc.vector.reciprocal(prec[:, g % 4, 0:2], psums[:, g % 4, 0:2]).then_inc(L["rc"], 1)
                    elif e[0] == "T":
                        g = e[1]
                        if g % 2 == 1:
                            dve.wait_ge(L["tm"], g + 1)
                            if g >= 3:
                                dve.wait_ge(L["pm"], g - 2)
                            nc.vector.tensor_copy(probT[:, g % 3, 0:D], ps[:, T_BANK + 1, 0:D]).then_inc(L["teD"], 1)
                    elif e[0] == "PV":
                        g = e[1]
                        p, r = divmod(g, 8)
                        hd, b2 = divmod(r, 4)
                        dve.wait_ge(L["ch"], g + 1)
                        two = slice(2 * b2, 2 * b2 + 2)
                        nc.vector.scalar_tensor_tensor(cc[1][:, hd, two, :], ps[:, O_BANK + g % 2, 0:D].rearrange("p (b n) -> p b n", b=2),
                                                       C(f"L2bv{p // PAIRS + 1}", (2 * p + hd) % H), f32(cc[0][:, hd, two, :]),
                                                       ALU.add, ALU.subtract).then_inc(L["cl"], 1)

            def mlp(name, y):
                m = M[name + "m"]
                for e in mlp_order(name):
                    if e[0] == "w":
                        take(*e[1:])
                    elif e[0] in ("nS", "nX", "nT", "k"):
                        wide([e])
                    elif e[0] == "up":
                        k = (FT // 2) * e[1] + e[2]
                        j_skip()
                        dve.wait_ge(m["gelu"], k + 1)
                        src = gf[:, k % 2, :].rearrange("p (f n) -> p f n", f=2)
                        at = (2 * k) % GT
                        two = slice(at, at + 2)
                        if 2 * k >= GT:
                            dve.wait_ge(m["out"], (2 * k - GT) // FT + 1)
                        link(nc.vector.tensor_copy(gg[0][:, two, :], src))
                        nc.vector.tensor_tensor(gg[1][:, two, :], src, f32(gg[0][:, two, :]), ALU.subtract).then_inc(m["lo"], 1)
                    else:
                        c = e[1]
                        bank = j_take().rearrange("p (b n) -> p b n", b=2)
                        if c == 0:
                            dve.wait_ge(ybias, y)
                        dst = X[:, 2 * c:2 * c + 2, :]
                        nc.vector.tensor_tensor(dst, bank, dst, ALU.add).then_inc(m["out"], 1)
                        if name != "L3":
                            stats(X, c, m["out"], c + 1)

            nc.vector.memset(eps[:, 0:1], 1e-5)
            nc.vector.memset(eps[:, 1:2], 1e-6).then_inc(eps_ok, 1)
            take("L0w0")
            dve.wait_ge(c_in, 16 * 4)
            nc.vector.tensor_copy(indr[:, :, :].rearrange("p a b -> p (a b)"), prob[0:1, 2, 0:2 * P])
            nc.vector.tensor_scalar(mb0, mt8[0:1, :, :].rearrange("p a b -> p (a b)"), 0.0, MASKED, ALU.is_equal, ALU.mult)\
              .then_inc(A["L0"]["mask"], 1)
            nc.vector.tensor_scalar(mb13[:, :], probT[0:1, :, :].bitcast(I32).rearrange("p a b -> p (a b)")[:, 0:B * P],
                                    0.0, MASKED, ALU.is_equal, ALU.mult).then_inc(A["L1"]["mask"], 1)
            take("L0sel0")
            take("L0sel1")
            attention("L0")
            attention("L1")
            nc.vector.tensor_scalar(mb13[:, :], mraw3[:, :], 0.0, MASKED, ALU.is_equal, ALU.mult).then_inc(A["L3"]["mask"], 1)
            mlp("L1", 2)
            dve.wait_ge(M["L1m"]["out"], B // 2)
            take("L2p1_0")
            wide(wide_order())
            mlp("L2", 5)
            dve.wait_ge(rowb_in, 16)
            attention("L3")
            mlp("L3", 7)

        @block.gpsimd
        def _(pool):
            glinks = [0]

            def link(ins):
                glinks[0] += 1
                ins.then_inc(g_link, 1)
                pool.wait_ge(g_link, glinks[0])

            def normalise(a, u, nh, keys, stride):
                pool.wait_ge(a["rc"], u + 1)
                pr = prob[:, u % 3, :].rearrange("p (h n) -> p h n", n=stride)[:, 0:nh, 0:keys]
                nc.gpsimd.tensor_tensor(pr, pr, prec[:, u % 4, 0:nh].unsqueeze(2).broadcast_to([P, nh, keys]), ALU.mult)\
                  .then_inc(a["nm"], 1)

            def zero_keys(ph):
                nc.gpsimd.memset(ks[ph].rearrange("p a b -> p (a b)").bitcast(F32), 0.0).then_inc(g_setup, 1)

            def zero_values():
                nc.gpsimd.memset(fs[:, 0:4096], 0.0).then_inc(vzero, 1)

            def attention(ph):
                c, a = ATT[ph], A[ph]
                U, keys = c["units"], c["keys"]
                for e, i, *k in att_order(ph):
                    if e == "S":
                        normalise(a, i, 4 // U, keys, keys)
                        if ph == "L1" and 1 <= i <= B:
                            add_row(XH, "L1o", i - 1)
                        if ph == "L1" and 20 <= i < 20 + B:
                            add_row(X, "L1b2", i - 20)
                        if ph == "L3" and 1 <= i <= B:
                            add_row(X, "L3o", i - 1)
                    if ph == "L0" and e == "S" and i % (2 * U * STEPS) == 15:
                        b = i // (2 * U * STEPS)
                        pool.wait_ge(a["dense"], b + 1)
                        if b == 0:
                            pool.wait_ge(l0n, 1)
                        nc.gpsimd.tensor_scalar(X[:, b, :], ms[:, 0, b, :], mv[:, b, 0:1], sd[:, 3, b:b + 1], ALU.subtract, ALU.mult)\
                          .then_inc(xn_done, 1)
                    if e == "fin":
                        two = slice(2 * i, 2 * i + 2)
                        pool.wait_ge(l0dev, i + 1)
                        nc.gpsimd.tensor_tensor(X[:, two, :], X[:, two, :], ms[:, 1, two, :], ALU.mult).then_inc(l0mul, 1)
                        if i == 2:
                            pool.wait_ge(a["sm"], c["iters"] * STEPS * 2 * U)
                            zero_keys("L1")
                        if i == 3:
                            zero_values()
                    if ph == "L0" and e == "OUT":
                        pool.wait_ge(a["oeA"], i + 1)
                        if i > 0:
                            pool.wait_ge(l0var, i)
                        link(nc.gpsimd.tensor_tensor(msq, ms[:, 0, i, :], ms[:, 0, i, :], ALU.mult))
                        link(nc.gpsimd.tensor_tensor(ms[:, 1, i, :], ms[:, 1, i, :], msq, ALU.subtract))
                        nc.gpsimd.tensor_scalar(ms[:, 1, i, :], ms[:, 1, i, :], 0.0, None, ALU.max).then_inc(l0var, 1)

            def add_row(dst, name, b):
                ins = nc.gpsimd.tensor_tensor(dst[:, b, :], X[:, b, :], R(name), ALU.add)
                if b == B - 1:
                    ins.then_inc(ybias, 1)

            zero_keys("L0")
            zero_values()
            attention("L0")
            pool.wait_ge(fin, B)
            attention("L1")
            for layer in range(2):
                pool.wait_ge(N[f"L2n{layer + 1}"]["xh"], B)
                if layer == 1:
                    pool.wait_ge(rowb_in, 16)
                for u in range(8 * PAIRS):
                    normalise(L, 8 * PAIRS * layer + u, 2, P, D)
                    if u < B:
                        add_row(X, f"L2bo{layer + 1}", u)
            pool.wait_ge(N["L2nm"]["xh"], B)
            for b in range(B):
                add_row(X, "L2b2", b)
            pool.wait_ge(M["L2m"]["out"], B // 2)
            zero_keys("L3")
            zero_values()
            pool.wait_ge(N["L3n1"]["xh"], B)
            attention("L3")
            pool.wait_ge(N["L3nm"]["xh"], B)
            for b in range(B):
                add_row(X, "L3b2", b)


def selection(ph):
    S = np.zeros((4, 4, P, P), np.float32)
    dh, heads = (8, 4) if ph == "L0" else (16, 2)
    scale = {"L0": 1.0, "L1": 1.0 / 16, "L3": 1.0 / 4}[ph]
    for g in range(4):
        for j in range(heads):
            h = 4 * j + g if ph == "L0" else 2 * g + j
            for d in range(dh):
                c = dh * h + d
                r = (P // heads) * j + d
                for part in range(3):
                    S[g, 0 if part != 1 else 1, c, r + dh * part] = scale
                    S[g, 2 if part != 2 else 3, c, r + dh * part] = 1.0
    return S.transpose(2, 0, 1, 3).reshape(P, 4 * 4 * P)


def kernel(**inputs):
    import concourse.bacc as _bacc
    from concourse.bass_utils import run_bass_kernel_spmd as _run

    g = {k: np.asarray(v) for k, v in inputs.items()}

    def tiles(w):
        return w.reshape(-1, P, w.shape[1]).transpose(1, 0, 2)

    def flat(*ws):
        return np.concatenate([w.reshape(P, -1) for w in ws], 1)

    packs = [np.concatenate([flat(*(g[f"L0_xattn_W{k}"].T for k in "qkv")), np.zeros((P, PACK - 3 * P), np.float32)], 1)]

    def add(w):
        assert w.shape == (P, 2 * PACK), w.shape
        packs.extend([w[:, :PACK], w[:, PACK:]])

    def out_rows(w):
        return w.reshape(2, 2, 4, 16, D).transpose(0, 2, 1, 3, 4).reshape(D, D)

    kv = g["L1_xattn_kv_w"].reshape(D, D, 2)
    kvb = g["L1_xattn_kv_b"].reshape(D, 2)
    add(selection("L0"))
    add(flat(tiles(g["L1_xattn_q_w"]), tiles(kv[:, :, 0]), tiles(kv[:, :, 1]), tiles(out_rows(g["L1_xattn_out_w"]))))
    add(selection("L1"))
    add(flat(tiles(g["L1_xattn_mlp_w1"])))
    add(flat(tiles(g["L1_xattn_mlp_w2"])))
    add(selection("L3"))
    for l in (1, 2):
        for p in range(PAIRS):
            c = slice(2 * P * p, 2 * P * (p + 1))
            add(flat(*(tiles(g[f"L2_xattn_w{k}{l}"][:, c]) for k in "qkv"), tiles(g[f"L2_xattn_wo{l}"][c, :])))
    add(flat(tiles(g["L2_xattn_w_fc1"])))
    add(flat(tiles(g["L2_xattn_w_fc2"])))
    add(flat(*(tiles(g[f"L3_xattn_{k}_w"]) for k in "qkv"), tiles(out_rows(g["L3_xattn_cproj_w"]))))
    add(flat(tiles(g["L3_xattn_fc_w"])))
    add(flat(tiles(g["L3_xattn_proj_w"])))

    r = np.arange(P)
    ind = [((r % 32) == 24).astype(np.float32), ((r % 64) == 48).astype(np.float32)]
    vec = {
        "ones0": ind[0], "ones1": ind[1],
        "L0q": g["L0_xattn_bq"], "L0k": g["L0_xattn_bk"], "L1q": g["L1_xattn_q_b"], "L1k": kvb[:, 0],
        "L1w": g["L1_xattn_postnorm_w"], "L1b1": g["L1_xattn_mlp_b1"],
        "L2mw": g["L2_xattn_ln_mlp_scale"], "L2mb": g["L2_xattn_ln_mlp_offset"], "L2b1": g["L2_xattn_b_fc1"],
        "L3q": g["L3_xattn_q_b"], "L3k": g["L3_xattn_k_b"], "L3lw": g["L3_xattn_ln1_w"], "L3lb": g["L3_xattn_ln1_b"],
        "L3mw": g["L3_xattn_ln2_w"], "L3mb": g["L3_xattn_ln2_b"], "L3b1": g["L3_xattn_fc_b"],
    }
    for l in (1, 2):
        vec |= {f"L2q{l}": g[f"L2_xattn_bq{l}"], f"L2k{l}": g[f"L2_xattn_bk{l}"], f"L2bk{l}": g[f"L2_xattn_bias_k{l}"],
                f"L2bv{l}": g[f"L2_xattn_bias_v{l}"], f"L2lw{l}": g[f"L2_xattn_ln{l}_scale"], f"L2lb{l}": g[f"L2_xattn_ln{l}_offset"]}
    cols = np.concatenate([vec[n].reshape(-1, P).T for n in COLS], 1)
    rowv = {"L0v": np.concatenate([g["L0_xattn_bv"], np.zeros(P, np.float32)]), "L1v": kvb[:, 1], "L1o": g["L1_xattn_out_b"],
            "L1b2": g["L1_xattn_mlp_b2"], "L2bo1": g["L2_xattn_bo1"], "L2bo2": g["L2_xattn_bo2"], "L2b2": g["L2_xattn_b_fc2"],
            "L3v": g["L3_xattn_v_b"], "L3o": g["L3_xattn_cproj_b"], "L3b2": g["L3_xattn_proj_b"]}
    rows = np.stack([rowv[n] for n in ROWS]).reshape(2, ROW_SET * D)
    l2rows = np.stack([np.stack([g[f"L2_xattn_bv{l}"].reshape(PAIRS, D), g[f"L2_xattn_bias_v{l}"].reshape(PAIRS, D)], 1)
                       for l in (1, 2)]).reshape(2 * PAIRS, 2 * D)

    arrays = {
        "x": g["x"], "ctx": g["ctx_2048"],
        "mask_t": g["mask_Bx1x2048_bf1"].reshape(1, B * D).view(np.uint8),
        "mask_s2": g["mask_BxS2_ik0"].reshape(1, B * P),
        "mask_s3": g["mask_BxS2_bf1"].reshape(1, B * P).view(np.uint8),
        "packs": np.stack(packs), "cols": cols, "rows": rows, "l2rows": l2rows,
        "inds": np.concatenate(ind).reshape(1, 2 * P), "ident": np.eye(P, dtype=np.float32),
    }
    nc = _bacc.Bacc("TRN2", target_bir_lowering=False, num_devices=1)
    sent, args = {}, []
    for name, a in arrays.items():
        a = np.ascontiguousarray(a)
        sent[f"in_{name}"] = a
        args.append(nc.dram_tensor(f"in_{name}", a.shape, mybir.dt.from_np(a.dtype), kind="ExternalInput").ap())
    args.append(nc.dram_tensor("out_0", (B, P, D), F32, kind="ExternalOutput").ap())
    build(nc, *args)
    res = _run(nc, [sent], core_ids=[0])
    return res.results[0]["out_0"]
```
